# Optimizing a Trainium2 kernel written in Bass

```python
import numpy as np
import jax
import jax.numpy as jnp

def _softmax(x, axis=-1):
    return jax.nn.softmax(x, axis=axis)

def _gelu(x):
    return jax.nn.gelu(x, approximate=True)

def _silu(x):
    return jax.nn.silu(x)

def _sigmoid(x):
    return jax.nn.sigmoid(x)

def _layernorm(x, axis=-1, eps=1e-05):
    m = jnp.mean(x, axis=axis, keepdims=True)
    v = jnp.var(x, axis=axis, keepdims=True)
    return (x - m) / jnp.sqrt(v + eps)

def _scatter_add(tgt, idx, src, axis=0):
    return tgt.at[idx].add(src)

def _segment_sum(src, seg, n):
    return jax.ops.segment_sum(src, seg, n)
kernel_name = 'mk_adj_preln_d4_adj_r2_c0e44f'

def setup_inputs(seed: int=0):
    np.random.seed(seed)
    _w = jnp.asarray

    def _rec_inputs():
        import jax
        import jax.numpy as jnp
        _gk = jax.random.key(seed)
        x = -0.0002928 + 1 * jax.random.normal(jax.random.fold_in(_gk, 1), (8, 1024, 128), jnp.float32)
        _a = jax.random.bernoulli(jax.random.fold_in(_gk, 2), 0.00195312, (8, 1024, 1024))
        _a = jnp.logical_or(_a, jnp.swapaxes(_a, -1, -2))
        _a = jnp.logical_or(_a, jnp.eye(1024, dtype=bool))
        _af = _a.astype(jnp.float32)
        _af = _af * jax.random.uniform(jax.random.fold_in(_gk, 3), (8, 1024, 1024), jnp.float32, 0.05, 1)
        adj = _af
        return (x, adj)
    x, adj = _rec_inputs()

    def _L0_gnn_setup():
        import jax, jax.numpy as jnp
        import numpy as np
        B, N, D, H = (8, 1024, 128, 512)
        RMS_EPS = 1e-06

        def _rmsnorm(h, w, eps=RMS_EPS):
            var = jnp.mean(jnp.square(h), axis=-1, keepdims=True)
            return h * jax.lax.rsqrt(var + eps) * w
        key = jax.random.key(seed)
        ks = jax.random.split(key, 5)
        x = jax.random.normal(ks[0], (B, N, D), dtype=jnp.float32)
        adjacency = jax.random.uniform(ks[1], (B, N, N), dtype=jnp.float32)
        epsilon = jnp.zeros((), dtype=jnp.float32)
        W1 = jax.random.normal(ks[2], (D, H), dtype=jnp.float32) * (1.0 / np.sqrt(D))
        b1 = jnp.zeros((H,), dtype=jnp.float32)
        rms_weight = jnp.ones((H,), dtype=jnp.float32)
        W2 = jax.random.normal(ks[3], (H, D), dtype=jnp.float32) * (1.0 / np.sqrt(H))
        b2 = jnp.zeros((D,), dtype=jnp.float32)
        return {'x': x, 'adjacency': adjacency, 'epsilon': epsilon, 'W1': W1, 'b1': b1, 'rms_weight': rms_weight, 'W2': W2, 'b2': b2}
    _L0_gnn_all = _L0_gnn_setup()
    _L0_gnn_in = {k: v for k, v in _L0_gnn_all.items() if k in ('epsilon', 'W1', 'b1', 'rms_weight', 'W2', 'b2')}
    del _L0_gnn_all

    def _L1_gnn_setup():
        import jax, jax.numpy as jnp
        import numpy as np
        K = 4
        EPS = 1e-09
        LEAKY_SLOPE = 0.2
        key = jax.random.key(seed)
        k1, k2, k3, k4, k5 = jax.random.split(key, 5)
        B, N, IN, OUT = (8, 1024, 128, 128)
        h = jax.random.normal(k1, (B, N, IN), dtype=jnp.float32)
        adj = jax.random.uniform(k2, (B, N, N), dtype=jnp.float32)
        W = jax.random.normal(k3, (OUT, IN), dtype=jnp.float32) * 0.05
        conv_w = jax.random.normal(k4, (K,), dtype=jnp.float32)
        conv_b = jax.random.normal(k5, (1,), dtype=jnp.float32)
        return {'h': h, 'adj': adj, 'W': W, 'conv_w': conv_w, 'conv_b': conv_b}
    _L1_gnn_all = _L1_gnn_setup()
    _L1_gnn_in = {k: v for k, v in _L1_gnn_all.items() if k in ('W', 'conv_w', 'conv_b')}
    del _L1_gnn_all

    def _L2_gnn_setup():
        import jax, jax.numpy as jnp
        import numpy as np
        from jax import lax
        DIM = 128
        EPS = 1e-05

        def _bn(h, g, b, m, v):
            scale = g / jnp.sqrt(v + EPS)
            return h * scale[None, :, None] + (b - m * scale)[None, :, None]

        def _conv1d(h, w, pad):
            return lax.conv_general_dilated(h, w, window_strides=(1,), padding=[(pad, pad)], dimension_numbers=('NCH', 'OIH', 'NCH'))
        key = jax.random.key(seed)
        ks = jax.random.split(key, 16)
        bs, n, d = (16, 1024, DIM)
        s = 0.05
        return {'x': jax.random.normal(ks[0], (bs, n, d), jnp.float32), 'mask': jnp.ones((bs, n, n), jnp.float32), 'w_se': jax.random.normal(ks[1], (3, d), jnp.float32) * s, 'b_se': jnp.zeros((3,), jnp.float32), 'conv1_w': jax.random.normal(ks[2], (d, d, 1), jnp.float32) * s, 'bn1_g': jnp.ones((d,), jnp.float32), 'bn1_b': jnp.zeros((d,), jnp.float32), 'bn1_m': jnp.zeros((d,), jnp.float32), 'bn1_v': jnp.ones((d,), jnp.float32), 'conv2_w': jax.random.normal(ks[3], (d, d, 17), jnp.float32) * s, 'bn2_g': jnp.ones((d,), jnp.float32), 'bn2_b': jnp.zeros((d,), jnp.float32), 'bn2_m': jnp.zeros((d,), jnp.float32), 'bn2_v': jnp.ones((d,), jnp.float32), 'w_msg': jax.random.normal(ks[4], (d, d), jnp.float32) * s, 'b_msg': jnp.zeros((d,), jnp.float32), 'w_ih': jax.random.normal(ks[5], (3 * d, 2 * d), jnp.float32) * s, 'b_ih': jnp.zeros((3 * d,), jnp.float32), 'w_hh': jax.random.normal(ks[6], (3 * d, d), jnp.float32) * s, 'b_hh': jnp.zeros((3 * d,), jnp.float32)}
    _L2_gnn_all = _L2_gnn_setup()
    _L2_gnn_in = {k: v for k, v in _L2_gnn_all.items() if k in ('w_se', 'b_se', 'conv1_w', 'bn1_g', 'bn1_b', 'bn1_m', 'bn1_v', 'conv2_w', 'bn2_g', 'bn2_b', 'bn2_m', 'bn2_v', 'w_msg', 'b_msg', 'w_ih', 'b_ih', 'w_hh', 'b_hh')}
    del _L2_gnn_all

    def _L3_gnn_setup():
        import jax, jax.numpy as jnp
        import numpy as np
        ALPHA = 0.2
        NEG_INF = -9000000000000000.0
        key = jax.random.key(seed)
        kw, ka, k1, k2, k3 = jax.random.split(key, 5)
        B, N1, N2, F, O = (4, 1024, 1024, 128, 128)
        word = jax.random.normal(kw, (B, N2, F), dtype=jnp.float32)
        adj = jax.random.randint(ka, (B, N1, N2), 0, 2).astype(jnp.float32)
        stdv = 1.0 / np.sqrt(O)
        W1 = jax.random.uniform(k1, (F, O), jnp.float32, -stdv, stdv)
        W2 = jax.random.uniform(k2, (F, O), jnp.float32, -stdv, stdv)
        w3 = jax.random.uniform(k3, (2 * O, 1), jnp.float32, -stdv, stdv)
        return {'word': word, 'adj': adj, 'W1': W1, 'W2': W2, 'w3': w3}
    _L3_gnn_all = _L3_gnn_setup()
    _L3_gnn_in = {k: v for k, v in _L3_gnn_all.items() if k in ('W1', 'W2', 'w3')}
    del _L3_gnn_all
    return {'x': x, 'adj': adj, 'L0_gnn_epsilon': _L0_gnn_in['epsilon'], 'L0_gnn_W1': _L0_gnn_in['W1'], 'L0_gnn_b1': _L0_gnn_in['b1'], 'L0_gnn_rms_weight': _L0_gnn_in['rms_weight'], 'L0_gnn_W2': _L0_gnn_in['W2'], 'L0_gnn_b2': _L0_gnn_in['b2'], 'L1_gnn_W': _L1_gnn_in['W'], 'L1_gnn_conv_w': _L1_gnn_in['conv_w'], 'L1_gnn_conv_b': _L1_gnn_in['conv_b'], 'L2_gnn_w_se': _L2_gnn_in['w_se'], 'L2_gnn_b_se': _L2_gnn_in['b_se'], 'L2_gnn_conv1_w': _L2_gnn_in['conv1_w'], 'L2_gnn_bn1_g': _L2_gnn_in['bn1_g'], 'L2_gnn_bn1_b': _L2_gnn_in['bn1_b'], 'L2_gnn_bn1_m': _L2_gnn_in['bn1_m'], 'L2_gnn_bn1_v': _L2_gnn_in['bn1_v'], 'L2_gnn_conv2_w': _L2_gnn_in['conv2_w'], 'L2_gnn_bn2_g': _L2_gnn_in['bn2_g'], 'L2_gnn_bn2_b': _L2_gnn_in['bn2_b'], 'L2_gnn_bn2_m': _L2_gnn_in['bn2_m'], 'L2_gnn_bn2_v': _L2_gnn_in['bn2_v'], 'L2_gnn_w_msg': _L2_gnn_in['w_msg'], 'L2_gnn_b_msg': _L2_gnn_in['b_msg'], 'L2_gnn_w_ih': _L2_gnn_in['w_ih'], 'L2_gnn_b_ih': _L2_gnn_in['b_ih'], 'L2_gnn_w_hh': _L2_gnn_in['w_hh'], 'L2_gnn_b_hh': _L2_gnn_in['b_hh'], 'L3_gnn_W1': _L3_gnn_in['W1'], 'L3_gnn_W2': _L3_gnn_in['W2'], 'L3_gnn_w3': _L3_gnn_in['w3']}

def reference(x, adj, L0_gnn_epsilon, L0_gnn_W1, L0_gnn_b1, L0_gnn_rms_weight, L0_gnn_W2, L0_gnn_b2, L1_gnn_W, L1_gnn_conv_w, L1_gnn_conv_b, L2_gnn_w_se, L2_gnn_b_se, L2_gnn_conv1_w, L2_gnn_bn1_g, L2_gnn_bn1_b, L2_gnn_bn1_m, L2_gnn_bn1_v, L2_gnn_conv2_w, L2_gnn_bn2_g, L2_gnn_bn2_b, L2_gnn_bn2_m, L2_gnn_bn2_v, L2_gnn_w_msg, L2_gnn_b_msg, L2_gnn_w_ih, L2_gnn_b_ih, L2_gnn_w_hh, L2_gnn_b_hh, L3_gnn_W1, L3_gnn_W2, L3_gnn_w3):
    import jax
    import jax.numpy as jnp

    def _L0_gnn_ref(x, adjacency, epsilon, W1, b1, rms_weight, W2, b2):
        import jax, jax.numpy as jnp
        import numpy as np
        B, N, D, H = (8, 1024, 128, 512)
        RMS_EPS = 1e-06

        def _rmsnorm(h, w, eps=RMS_EPS):
            var = jnp.mean(jnp.square(h), axis=-1, keepdims=True)
            return h * jax.lax.rsqrt(var + eps) * w
        neighbor_sum = jnp.einsum('bnm,bmd->bnd', adjacency, x)
        agg = epsilon * x + neighbor_sum
        h = jnp.einsum('bnd,dh->bnh', agg, W1) + b1
        h = jax.nn.silu(_rmsnorm(h, rms_weight))
        out = jnp.einsum('bnh,hd->bnd', h, W2) + b2
        return out

    def _L1_gnn_ref(h, adj, W, conv_w, conv_b):
        import jax, jax.numpy as jnp
        import numpy as np
        K = 4
        EPS = 1e-09
        LEAKY_SLOPE = 0.2
        h_trans = jnp.einsum('bni,oi->bno', h, W)
        row_sum = adj.sum(axis=2, keepdims=True) + EPS
        adj_norm = adj / row_sum
        curr = h_trans
        out = conv_w[0] * curr
        for k in range(1, K):
            curr = jnp.einsum('bnm,bmo->bno', adj_norm, curr)
            out = out + conv_w[k] * curr
        out = out + conv_b[0]
        return jnp.where(out >= 0, out, LEAKY_SLOPE * out)

    def _L2_gnn_ref(x, mask, w_se, b_se, conv1_w, bn1_g, bn1_b, bn1_m, bn1_v, conv2_w, bn2_g, bn2_b, bn2_m, bn2_v, w_msg, b_msg, w_ih, b_ih, w_hh, b_hh):
        import jax, jax.numpy as jnp
        import numpy as np
        from jax import lax
        DIM = 128
        EPS = 1e-05

        def _bn(h, g, b, m, v):
            scale = g / jnp.sqrt(v + EPS)
            return h * scale[None, :, None] + (b - m * scale)[None, :, None]

        def _conv1d(h, w, pad):
            return lax.conv_general_dilated(h, w, window_strides=(1,), padding=[(pad, pad)], dimension_numbers=('NCH', 'OIH', 'NCH'))
        d = x.shape[-1]
        xc = jnp.transpose(x, (0, 2, 1))
        h = _bn(_conv1d(xc, conv1_w, 0), bn1_g, bn1_b, bn1_m, bn1_v)
        h = jax.nn.relu(h)
        h = _bn(_conv1d(h, conv2_w, 8), bn2_g, bn2_b, bn2_m, bn2_v)
        x_conv = jnp.transpose(jax.nn.relu(h + xc), (0, 2, 1))
        s = x @ w_se.T + b_se
        sq = jnp.sum(s * s, axis=-1)
        dist = sq[:, :, None] + sq[:, None, :] - 2.0 * jnp.einsum('bnd,bmd->bnm', s, s)
        A = jnp.exp(-dist) * mask
        msg = jax.nn.relu(x @ w_msg.T + b_msg)
        x_nmp = jnp.einsum('bnm,bmd->bnd', A, msg)
        x_in = jnp.concatenate([x_conv, x_nmp], axis=-1)
        gi = x_in @ w_ih.T + b_ih
        gh = x @ w_hh.T + b_hh
        gi_r, gi_z, gi_n = (gi[..., :d], gi[..., d:2 * d], gi[..., 2 * d:])
        gh_r, gh_z, gh_n = (gh[..., :d], gh[..., d:2 * d], gh[..., 2 * d:])
        r = jax.nn.sigmoid(gi_r + gh_r)
        z = jax.nn.sigmoid(gi_z + gh_z)
        nn_ = jnp.tanh(gi_n + r * gh_n)
        return (1.0 - z) * nn_ + z * x

    def _L3_gnn_ref(word, adj, W1, W2, w3):
        import jax, jax.numpy as jnp
        import numpy as np
        ALPHA = 0.2
        NEG_INF = -9000000000000000.0
        O = W1.shape[1]
        deg = jnp.sum(adj, axis=-1, keepdims=True)
        deg = jnp.where(deg > 0, deg, jnp.ones_like(deg))
        mp = jnp.matmul(adj / deg, word)
        w3a = w3[:O, 0]
        w3b = w3[O:, 0]
        s1 = jnp.einsum('bnf,fo,o->bn', word, W1, w3a)
        s2 = jnp.einsum('bnf,fo,o->bn', mp, W2, w3b)
        pre = adj * (s2[:, :, None] + s1[:, None, :])
        alpha = jnp.exp(jax.nn.leaky_relu(pre, ALPHA))
        attention = jnp.where(adj > 0, alpha, NEG_INF)
        attention_edge = jax.nn.softmax(attention, axis=2)
        edge = jnp.matmul(attention_edge, word)
        return edge
    h = jnp.maximum(_layernorm(x, axis=-1), 0.0)
    x = x + _L0_gnn_ref(h, adj, L0_gnn_epsilon, L0_gnn_W1, L0_gnn_b1, L0_gnn_rms_weight, L0_gnn_W2, L0_gnn_b2)
    h = jnp.maximum(_layernorm(x, axis=-1), 0.0)
    x = x + _L1_gnn_ref(h, adj, L1_gnn_W, L1_gnn_conv_w, L1_gnn_conv_b)
    h = jnp.maximum(_layernorm(x, axis=-1), 0.0)
    x = x + _L2_gnn_ref(h, adj, L2_gnn_w_se, L2_gnn_b_se, L2_gnn_conv1_w, L2_gnn_bn1_g, L2_gnn_bn1_b, L2_gnn_bn1_m, L2_gnn_bn1_v, L2_gnn_conv2_w, L2_gnn_bn2_g, L2_gnn_bn2_b, L2_gnn_bn2_m, L2_gnn_bn2_v, L2_gnn_w_msg, L2_gnn_b_msg, L2_gnn_w_ih, L2_gnn_b_ih, L2_gnn_w_hh, L2_gnn_b_hh)
    h = jnp.maximum(_layernorm(x, axis=-1), 0.0)
    x = x + _L3_gnn_ref(h, adj, L3_gnn_W1, L3_gnn_W2, L3_gnn_w3)
    return x

_drawn_inputs = setup_inputs


def setup_inputs(seed=0):
    import zlib

    import numpy as np

    out = dict(_drawn_inputs(seed))
    spreads = {'L0_gnn_b1': (0.0, 0.1),
     'L0_gnn_rms_weight': (1.0, 0.2),
     'L0_gnn_b2': (0.0, 0.1),
     'L2_gnn_b_se': (0.0, 0.8),
     'L2_gnn_bn1_g': (1.0, 0.6),
     'L2_gnn_bn1_b': (0.0, 0.36),
     'L2_gnn_bn1_m': (0.0, 0.312),
     'L2_gnn_bn1_v': (1.0, 0.6),
     'L2_gnn_bn2_g': (1.0, 0.6),
     'L2_gnn_bn2_b': (0.0, 0.569),
     'L2_gnn_bn2_m': (0.0, 0.536),
     'L2_gnn_bn2_v': (1.0, 0.6),
     'L2_gnn_b_msg': (0.0, 0.343),
     'L2_gnn_b_ih': (0.0, 0.1),
     'L2_gnn_b_hh': (0.0, 0.384)}
    factors = {'L2_gnn_w_se': 3.763, 'L3_gnn_W1': 3.234, 'L3_gnn_W2': 6.432, 'L3_gnn_w3': 3.201}
    for name, (base, spread) in spreads.items():
        noise = np.random.default_rng([zlib.crc32(name.encode()), seed]).standard_normal(out[name].shape)
        drawn = base * np.exp(spread * noise) if base else spread * noise
        out[name] = jnp.asarray(drawn.astype(out[name].dtype))
    for name, factor in factors.items():
        out[name] = (out[name] * factor).astype(out[name].dtype)
    return out
```

```python
from contextlib import ExitStack

import concourse.bass as bass
from concourse import mybir

ALU = mybir.AluOpType
ACT = mybir.ActivationFunctionType
F32 = mybir.dt.float32
F32R = mybir.dt.float32r
BF16 = mybir.dt.bfloat16

P = 128
B, N, D, H = 8, 1024, 128, 512
NB = N // P
HALF = N // 2
HB = NB // 2
HC = H // P
TAPS = 17
PAD = TAPS // 2
HOPS = 3
LN_EPS, RMS_EPS, DEG_EPS, BN_EPS = 1e-5, 1e-6, 1e-9, 1e-5
NEG_INF = -9e15

W_MLP1, W_MLP2, W_HOP, W_CONV1, W_CONV2 = 0, HC, 2 * HC, 2 * HC + 1, 2 * HC + 2
W_MSG = W_CONV2 + TAPS
W_SE = W_MSG + 1
W_IH = W_SE + 1
W_HH = W_IH + 6
NW_IN = W_HH + 3
W_S1, W_S2 = NW_IN, NW_IN + 1
NW = NW_IN + 2

COLS = dict(b1=(0, HC), rms=(4, HC), b2=(8, 1), bn1=(9, 4), bn2=(13, 4), bih=(17, 3), bhh=(20, 3),
            hop=(23, HOPS + 1), hop_b=(27, 1), eps=(28, 1), bse=(29, 1))
NCOL = 30
C_ID, C_ONE, C_PL, C_PR, C_MSG = range(5)


class Signal:

    def __init__(self, ctx, nc, name, per=1):
        self.sem, self.per = ctx.enter_context(nc.semaphore(name)), per

    def at(self, b, n):
        return self.sem, b * self.per + n


def order():
    p = [("p_load",), ("p_ln0",)] + [("p_adj", k) for k in range(NB)] + [("p_h0t",), ("p_deg",)]
    p += [("p_prod", 0, f) for f in range(2)] + [("p_agg",)]
    for f in range(2):
        p += [("p_z", f), ("p_rms", f), ("p_silu", f)]
    p += [("p_x1",), ("p_ln1",)]
    for h in range(1, HOPS + 1):
        p += [("p_prod", h, f) for f in range(2)] + [("p_hop", h)]
    q = [("q_ln2",), ("q_ht", 0), ("q_s",), ("q_msg",)] + [("q_ker", m) for m in range(NB)]
    q += [("q_nmp",), ("q_conv1",)]
    q += [("q_conv2", f, t) for f in range(2) for t in range(4)]
    q += [("q_gru", f) for f in range(2)] + [("q_x3",), ("q_ln3",), ("q_ht", 1), ("q_rep",)]
    for f in range(2):
        for j in range(HB + 1):
            i = f * HB + j
            q.append(("q_att", i if j < HB else None, i - 1 if j > 0 else None))
        q.append(("q_edge", f))
    return p, q


P_STEPS, Q_STEPS = order()
P_LAST = [("p_out",)]
BODY = P_STEPS + Q_STEPS + P_LAST
TAP_PARTS = [range(0, 5), range(5, 9), range(9, 13), range(13, TAPS)]


def build(nc, x, adj, adj_t, wpack, l3pack, cpack, cols, out):
    ctx = ExitStack()
    with ctx:
        base = (nc.sbuf_base + 63) // 64 * 64
        top = [base]

        def room(nbytes):
            at = top[0]
            top[0] += (nbytes + 63) // 64 * 64
            return at

        def tile(name, shape, dt, at=None):
            n = 4 if dt in (F32, F32R) else 2
            for s in shape[1:]:
                n *= s
            return nc.alloc_sbuf_tensor_at(name, shape, dt, offset=room(n) if at is None else at)

        KB4 = 4 * N
        w_hi = tile("w_hi", [P, NW, P], F32R)
        w_lo = tile("w_lo", [P, NW, P], F32R)
        const = tile("const", [P, 5, P], F32)
        pat = tile("pat", [P, 2, P], F32R)
        col = tile("col", [P, NCOL], F32)
        colx = tile("colx", [P, 16], F32)
        halves = tile("halves", [P, NB], F32)
        adj_hi = tile("adj_hi", [P, NB, N], F32R)
        at_lo = room(NB * KB4)
        adj_lo = tile("adj_lo", [P, NB, N], F32R, at_lo)
        stage_w = tile("stage_w", [P, NW_IN, P], F32, at_lo)
        stage_l3 = tile("stage_l3", [P, 4, P], F32, at_lo + NW_IN * 512)
        stage_v = tile("stage_v", [P, 2, P], F32, at_lo + (NW_IN + 4) * 512)
        adj_in = tile("adj_in", [P, 2, N], F32)
        row_in = tile("row_in", [P, 2, N], F32)

        xp = tile("xp", [P, NB, D], F32)
        y_hi = tile("y_hi", [P, N], F32R)
        y_lo = tile("y_lo", [P, N], F32R)
        at = room(KB4)
        hrow = tile("hrow", [P, N], F32, at)
        th = tile("th", [P, 2, HALF], F32, at)
        ta = tile("ta", [P, N], F32)
        at = room(HC * HALF * 4)
        zb = tile("zb", [P, HC, HALF], F32, at)
        dacc = tile("dacc", [P, N], F32, at)
        tg = tile("tg", [P, N], F32, at)
        sqsum = tile("sqsum", [P, HALF], F32)
        at = room(KB4)
        sqt = tile("sqt", [P, 2, HALF], F32, at)
        s_hi = tile("s_hi", [P, 2, HALF], F32R, at)
        s_lo = tile("s_lo", [P, 2, HALF], F32R)

        xq = tile("xq", [P, NB, D], F32)
        at_h32 = room(KB4)
        ht32 = tile("ht32", [P, N], F32, at_h32)
        s1rep = tile("s1rep", [P, N], F32, at_h32)
        at = room(2 * KB4)
        ht_hi = tile("ht_hi", [P, N], F32R, at)
        ht_lo = tile("ht_lo", [P, N], F32R, at + KB4)
        pt_hi = tile("pt_hi", [P, 2, HALF], F32R, at)
        pt_lo = tile("pt_lo", [P, 2, HALF], F32R, at + KB4)
        WIDE = N + 2 * PAD
        at = room(4 * WIDE * 2 + 2 * KB4)
        c1_hi = tile("c1_hi", [P, WIDE], F32R, at)
        c1_lo = tile("c1_lo", [P, WIDE], F32R, at + 4 * WIDE)
        ker_r = tile("ker_r", [P, N], F32R, at + 4 * PAD)
        ker_l = tile("ker_l", [P, N], F32R, at + 4 * WIDE + 4 * PAD)
        at3 = at + 8 * WIDE
        nmp_hi = tile("nmp_hi", [P, N], F32R, at3)
        nmp_lo = tile("nmp_lo", [P, N], F32R, at3 + KB4)
        ss_hi = tile("ss_hi", [P, N], F32R, at3)
        ss_lo = tile("ss_lo", [P, N], F32R, at3 + KB4)
        a_hi = tile("a_hi", [P, 2, HALF], F32R, at3)
        a_lo = tile("a_lo", [P, 2, HALF], F32R, at3 + KB4)
        prow = [tile(f"prow{n}", [P, N], F32, o) for n, o in
                enumerate((at + 4 * PAD, at + 4 * WIDE + 4 * PAD, at3, at3 + KB4))]
        g_hi = tile("g_hi", [P, N], F32R)
        g_lo = tile("g_lo", [P, N], F32R)
        at = room(KB4)
        t1 = tile("t1", [P, N], F32, at)
        urep = tile("urep", [P, N], F32, at)
        at = room(2 * KB4 + 2 * HALF * 4)
        hq = tile("hq", [P, N], F32, at)
        tmp1 = tile("tmp1", [P, N], F32, at)
        tmp2 = tile("tmp2", [P, N], F32, at + KB4)
        a_f = tile("a_f", [P, 2, HALF], F32, at)
        gate = tile("gate", [P, 3, HALF], F32, at)
        pre = tile("pre", [P, 2, N], F32, at)
        ot = tile("ot", [P, HALF], F32, at + 2 * KB4)

        stat = [tile(f"stat{s}", [P, NB, 6], F32) for s in "pq"]
        mv = [tile(f"mv{s}", [P, NB, 2], F32) for s in "pq"]
        ve = [tile(f"ve{s}", [P, NB], F32) for s in "pq"]
        rstd = [tile(f"rstd{s}", [P, NB], F32) for s in "pq"]
        ve4 = tile("ve4", [P, HB], F32)
        r4 = tile("r4", [P, HB], F32)
        dg = tile("dg", [P, 6, NB], F32)
        rdeg = tile("rdeg", [P, NB], F32)
        s2raw = tile("s2raw", [P, NB], F32)
        s2 = tile("s2", [P, NB], F32)
        amax = tile("amax", [P, NB], F32)
        nmax = tile("nmax", [P, NB], F32)
        psum3 = tile("psum3", [P, NB], F32)
        rinv = tile("rinv", [P, NB], F32)
        carrier = tile("carrier", [P, 2], F32)
        nc_left = nc.sbuf_usable_end - top[0]
        assert nc_left >= 0, nc_left

        ident, ones = const[:, C_ID, :], const[:, C_ONE, :]

        def psum(name):
            return ctx.enter_context(nc.psum_tensor(name, [P, 2, HALF], F32))

        acc_p, tr_p, acc_q, tr_q = psum("acc_p"), psum("tr_p"), psum("acc_q"), psum("tr_q")

        def flat(t):
            return t[:, :, :].rearrange("p f n -> p (f n)")

        def blocks(t):
            if len(t.shape) == 3:
                return t[:, :, :].rearrange("p f (j c) -> p (f j) c", c=P)
            return t[:, :].rearrange("p (j c) -> p j c", c=P)

        def c_(name, n=0):
            at = COLS[name][0] + n
            return col[:, at:at + 1]

        X_SC1, X_B1, X_SC2, X_B2, X_BR, X_BZ, X_BHN, X_RMS, X_V = 0, 1, 2, 3, 4, 5, 6, 8, 12

        def x_(n):
            return colx[:, n:n + 1]

        def fs(f):
            return slice(f * HALF, (f + 1) * HALF)

        def ks(k):
            return slice(k * P, (k + 1) * P)

        S = {}

        def sig(name, per=1):
            S[name] = Signal(ctx, nc, name, per)
            return S[name]

        setup_in = sig("setup_in"); w_hi_ok = sig("w_hi_ok"); w_ok = sig("w_ok"); pool_const = sig("pool_const")
        bn_v = sig("bn_v"); bn_r = sig("bn_r"); set_ch = sig("set_ch"); set_act = sig("set_act")
        x_in = sig("x_in", 16)
        adj_got = [sig(f"adj_got{s}", 16 * NB // 2) for s in range(2)]
        row_got = [sig(f"row_got{s}", 16 * NB) for s in range(2)]
        out_sent = sig("out_sent", 16)
        LN = [dict(stats=sig(f"ln{i}_stats"), mean=sig(f"ln{i}_mean"), var=sig(f"ln{i}_var"),
                   rstd=sig(f"ln{i}_rstd"), scaled=sig(f"ln{i}_scaled"), h=sig(f"ln{i}_h")) for i in range(4)]
        adj_hi_ok = sig("adj_hi_ok", NB); adj_lo_ok = sig("adj_lo_ok", NB); deg_added = sig("deg_added", NB)
        Y_H0, Y_AGG, Y_W3H, Y_HOP1, Y_HOP2, Y_T = range(1, 7)
        y_hi_ok = sig("y_hi_ok", 6); y_lo_ok = sig("y_lo_ok", 6)
        h0_turned = sig("h0_turned"); eh_ok = sig("eh_ok"); deg_summed = sig("deg_summed"); deg_ok = sig("deg_ok")
        deg_ch = sig("deg_ch", 6)
        prod_done = sig("prod_done", 2 * (HOPS + 1)); agg_ok = sig("agg_ok", 2)
        z_done = sig("z_done", 2 * HC); zb_ok = sig("zb_ok", 2 * HC); sq_ok = sig("sq_ok", 2 * HC)
        sq_added = sig("sq_added", 2 * (HC - 1))
        ms_done = sig("ms_done", 2); ms_read = sig("ms_read", 2); r4_ok = sig("r4_ok", 2); diag_ok = sig("diag_ok", 2)
        rep_done = sig("rep_done", 2); u_ok = sig("u_ok", 2 * HC); th_ok = sig("th_ok", 2 * HC)
        silu_ok = sig("silu_ok", 2 * HC); s_hi_ok = sig("s_hi_ok", 2 * HC); s_lo_ok = sig("s_lo_ok", 2 * HC)
        w2_done = sig("w2_done", 2 * HC); y0_ok = sig("y0_ok", 2)
        y0_turned = sig("y0_turned"); x1_ok = sig("x1_ok")
        hop_copied = sig("hop_copied", 2 * HOPS); hop_turned = sig("hop_turned", 2 * HOPS)
        hop_scaled = sig("hop_scaled", 2 * HOPS); hop_ok = sig("hop_ok", 2 * HOPS)
        yt_turned = sig("yt_turned"); l1_done = sig("l1_done"); l1_biased = sig("l1_biased"); l1_leaky = sig("l1_leaky")
        rdeg_ok = sig("rdeg_ok"); x2_ok = sig("x2_ok")
        ht_turned = sig("ht_turned", 2); ht32_ok = sig("ht32_ok"); ht_hi_ok = sig("ht_hi_ok", 2); ht_lo_ok = sig("ht_lo_ok", 2)
        s_done = sig("s_done"); s_ok = sig("s_ok"); ss_ok = sig("ss_ok"); ss_hi_ok = sig("ss_hi_ok"); ss_lo_ok = sig("ss_lo_ok")
        rl_done = sig("rl_done"); r32_ok = sig("r32_ok"); l32_ok = sig("l32_ok"); r_hi_ok = sig("r_hi_ok"); l_hi_ok = sig("l_hi_ok")
        rl_ok = sig("rl_ok")
        msg_done = sig("msg_done"); msg_b = sig("msg_b"); msg_hi_ok = sig("msg_hi_ok"); msg_lo_ok = sig("msg_lo_ok")
        dist_done = sig("dist_done", 2 * NB); a_f_ok = sig("a_f_ok", 2 * NB); a_m_ok = sig("a_m_ok", 2 * NB); a_hi_ok = sig("a_hi_ok", 2 * NB)
        a_lo_ok = sig("a_lo_ok", 2 * NB); ker_done = sig("ker_done", 2 * NB)
        nmp_hi_ok = sig("nmp_hi_ok"); nmp_lo_ok = sig("nmp_lo_ok")
        c1_done = sig("c1_done"); c1_f_ok = sig("c1_f_ok"); c1_hi_ok = sig("c1_hi_ok"); c1_lo_ok = sig("c1_lo_ok")
        c2_done = sig("c2_done", 2); xc_sum = sig("xc_sum", 2); xc_ok = sig("xc_ok", 2); xc_hi_ok = sig("xc_hi_ok", 2); xc_lo_ok = sig("xc_lo_ok", 2)
        gate_done = sig("gate_done", 2); gate_th = sig("gate_th", 2); gate_r = sig("gate_r", 2); gate_n_in = sig("gate_n_in", 2)
        gate_n = sig("gate_n", 2); gate_d = sig("gate_d", 2); gate_zd = sig("gate_zd", 2); gru_ok = sig("gru_ok", 2)
        gru_turned = sig("gru_turned"); x3_ok = sig("x3_ok"); h3_hi_ok = sig("h3_hi_ok"); h3_lo_ok = sig("h3_lo_ok")
        rep_s_done = sig("rep_s_done"); rep_s_ok = sig("rep_s_ok", 2)
        s2_raw_ok = sig("s2_raw_ok", NB); s2_ok = sig("s2_ok", NB); pre_ok = sig("pre_ok", NB); leaky_ok = sig("leaky_ok", NB)
        alpha_ok = sig("alpha_ok", NB); mask_ok = sig("mask_ok", NB); att_ok = sig("att_ok", NB); nmax_ok = sig("nmax_ok", NB); prow_ok = sig("prow_ok", NB)
        p_turned = sig("p_turned", 2 * NB); pt_hi_ok = sig("pt_hi_ok", 2 * NB); pt_lo_ok = sig("pt_lo_ok", 2 * NB); edge_done = sig("edge_done", 2 * NB)
        ot_ok = sig("ot_ok", 2); ot_turned = sig("ot_turned", 2); rinv_ok = sig("rinv_ok", 2); out_ok = sig("out_ok", 2)

        block = ctx.enter_context(nc.Block())

        def walk(eng, steps):
            def go(names, bp, bq):
                for name, *args in names:
                    if name in steps:
                        steps[name](bp if name[0] == "p" else bq, *args)
            go(P_STEPS + P_LAST, 0, None)
            with eng.Fori(1, B) as i:
                go(BODY, i, i - 1)
            go(Q_STEPS, None, B - 1)

        @block.sync
        def _(sp):
            sp.dma_start(stage_w[:, :, :].rearrange("p a b -> p (a b)"), wpack).then_inc(setup_in.sem, 16)
            sp.dma_start(stage_l3[:, :, :].rearrange("p a b -> p (a b)"), l3pack).then_inc(setup_in.sem, 16)
            sp.dma_start(const[:, :, :].rearrange("p a b -> p (a b)"), cpack).then_inc(setup_in.sem, 16)
            sp.dma_start(col[:, :], cols).then_inc(setup_in.sem, 16)

            def p_load(b):
                sp.wait_ge(*x2_ok.at(b, 0))
                sp.dma_start(xp[:, :, :], x[b].rearrange("(j p) d -> p j d", p=P)).then_inc(x_in.sem, 16)

            def p_adj(b, k):
                sp.wait_ge(*adj_lo_ok.at(b, max(k - 1, 0)))
                sp.wait_ge(*deg_added.at(b, max(k - 1, 0)))
                sp.dma_start(adj_in[:, k % 2, :], adj_t[b, k * P:(k + 1) * P, :]).then_inc(adj_got[k % 2].sem, 16)

            def q_ker(b, m):
                if m >= 2:
                    sp.wait_ge(*a_m_ok.at(b, 2 * (m - 1)))
                else:
                    sp.wait_ge(*x2_ok.at(b, 1))
                sp.dma_start(row_in[:, m % 2, :], adj_t[b, m * P:(m + 1) * P, :]).then_inc(row_got[m % 2].sem, 16)

            def q_att(b, i, j):
                if i is None:
                    return
                if i >= 2:
                    sp.wait_ge(*mask_ok.at(b, i - 1))
                else:
                    sp.wait_ge(*a_m_ok.at(b, 2 * (NB - 1 + i)))
                sp.dma_start(row_in[:, i % 2, :], adj[b, i * P:(i + 1) * P, :]).then_inc(row_got[i % 2].sem, 16)

            def q_edge(b, f):
                if f == 1:
                    sp.wait_ge(*out_ok.at(b, 2))
                    sp.dma_start(out[b].rearrange("(j p) d -> p j d", p=P), xq[:, :, :]).then_inc(out_sent.sem, 16)

            walk(sp, dict(p_load=p_load, p_adj=p_adj, q_ker=q_ker, q_att=q_att, q_edge=q_edge))
            sp.wait_ge(*out_sent.at(B, 0))

        @block.gpsimd
        def _(pool):
            pool.memset(halves[:, :], -0.5).then_inc(pool_const.sem, 1)
            pool.wait_ge(pool_const.sem, 1)
            pool.wait_ge(bn_v.sem, 1)
            pool.tensor_tensor(colx[:, X_V + 2:X_V + 4], colx[:, X_V:X_V + 2], halves[:, 0:2], ALU.pow).then_inc(bn_r.sem, 1)

            def ln(i, b):
                g = i // 2
                pool.wait_ge(*LN[i]["var"].at(b, 1))
                pool.tensor_tensor(rstd[g][:, :], ve[g][:, :], halves[:, :], ALU.pow).then_inc(LN[i]["rstd"].sem, 1)

            def p_adj(b, k):
                pool.wait_ge(*adj_got[k % 2].at(b, 16 * (k // 2 + 1)))
                if k == 1:
                    pool.wait_ge(*x2_ok.at(b, 0))
                    pool.tensor_tensor(dacc[:, :], adj_in[:, 0, :], adj_in[:, 1, :], ALU.add).then_inc(deg_added.sem, 2)
                if k > 1:
                    pool.wait_ge(*deg_added.at(b, k))
                    pool.tensor_tensor(dacc[:, :], dacc[:, :], adj_in[:, k % 2, :], ALU.add).then_inc(deg_added.sem, 1)

            def p_z(b, f):
                for c in range(1, HC):
                    pool.wait_ge(*sq_ok.at(b, HC * f + c + 1))
                    if c > 1:
                        pool.wait_ge(*sq_added.at(b, (HC - 1) * f + c - 1))
                    pool.tensor_tensor(sqsum[:, :], sqsum[:, :], sqt[:, c % 2, :], ALU.add).then_inc(sq_added.sem, 1)

            def p_rms(b, f):
                pool.wait_ge(*ms_read.at(b, f + 1))
                pool.tensor_tensor(r4[:, :], ve4[:, :], halves[:, 0:HB], ALU.pow).then_inc(r4_ok.sem, 1)

            def q_gru(b, f):
                pool.wait_ge(*gate_n.at(b, f + 1))
                pool.tensor_tensor(gate[:, 0, :], ht32[:, fs(f)], gate[:, 2, :], ALU.subtract).then_inc(gate_d.sem, 1)

            walk(pool, dict(p_ln0=lambda b: ln(0, b), p_ln1=lambda b: ln(1, b), q_ln2=lambda b: ln(2, b),
                            q_ln3=lambda b: ln(3, b), p_adj=p_adj, p_z=p_z, p_rms=p_rms, q_gru=q_gru))

        @block.scalar
        def _(act):
            act.wait_ge(setup_in.sem, 64)
            act.activation(w_hi[:, 0:NW_IN, :], stage_w[:, :, :], ACT.Copy).then_inc(w_hi_ok.sem, 1)
            act.activation(pat[:, :, :], const[:, C_PL:C_PR + 1, :], ACT.Copy).then_inc(set_act.sem, 1)

            def relu_rows(i, b, h):
                act.wait_ge(*LN[i]["scaled"].at(b, 1))
                act.activation(h[:, :], h[:, :], ACT.Relu).then_inc(LN[i]["h"].sem, 1)
                act.wait_ge(*LN[i]["h"].at(b, 1))

            def p_ln0(b):
                relu_rows(0, b, hrow)
                act.activation(y_hi[:, :], hrow[:, :], ACT.Copy).then_inc(y_hi_ok.sem, 1)

            def p_adj(b, k):
                act.wait_ge(*adj_got[k % 2].at(b, 16 * (k // 2 + 1)))
                if k == 0:
                    act.wait_ge(*prod_done.at(b, 0))
                    act.wait_ge(w_ok.sem, 1)
                act.activation(adj_hi[:, k, :], adj_in[:, k % 2, :], ACT.Copy).then_inc(adj_hi_ok.sem, 1)

            def p_h0t(b):
                act.wait_ge(*h0_turned.at(b, 1))
                act.activation(ta[:, :], flat(tr_p), ACT.Identity, scale=c_("eps")).then_inc(eh_ok.sem, 1)

            def p_agg(b):
                act.wait_ge(*agg_ok.at(b, 2))
                act.activation(y_hi[:, :], ta[:, :], ACT.Copy).then_inc(y_hi_ok.sem, 1)

            def p_z(b, f):
                for c in range(HC):
                    act.wait_ge(*z_done.at(b, HC * f + c + 1))
                    if c == 0 and f == 0:
                        act.wait_ge(*deg_summed.at(b, 1))
                    if c == 0 and f == 1:
                        act.wait_ge(*silu_ok.at(b, HC))
                    act.activation(zb[:, c, :], tr_p[:, c % 2, :], ACT.Identity, bias=c_("b1", c)).then_inc(zb_ok.sem, 1)
                    if c == 3:
                        act.wait_ge(*sq_added.at(b, (HC - 1) * f + 1))
                    dst = sqsum[:, :] if c == 0 else sqt[:, c % 2, :]
                    act.activation(dst, tr_p[:, c % 2, :], ACT.Square, bias=c_("b1", c)).then_inc(sq_ok.sem, 1)

            def p_silu(b, f):
                def tanh(c):
                    act.wait_ge(*u_ok.at(b, HC * f + c + 1))
                    if c >= 2:
                        act.wait_ge(*s_lo_ok.at(b, HC * f + c - 1))
                    act.activation(th[:, c % 2, :], zb[:, c, :], ACT.Tanh).then_inc(th_ok.sem, 1)

                if f == 0:
                    act.wait_ge(*h0_turned.at(b, 1))
                tanh(0)
                tanh(1)
                for c in range(HC):
                    act.wait_ge(*silu_ok.at(b, HC * f + c + 1))
                    if HC * f + c >= 2:
                        act.wait_ge(*w2_done.at(b, HC * f + c - 1))
                    act.activation(s_hi[:, c % 2, :], th[:, c % 2, :], ACT.Copy).then_inc(s_hi_ok.sem, 1)
                    if c % 2 == 1 and c + 1 < HC:
                        tanh(c + 1)
                        tanh(c + 2)
                act.wait_ge(*w2_done.at(b, HC * (f + 1)))
                act.activation(ta[:, fs(f)], acc_p[:, 1, :], ACT.Identity, bias=c_("b2")).then_inc(y0_ok.sem, 1)

            def p_ln1(b):
                relu_rows(1, b, hrow)
                act.activation(y_hi[:, :], hrow[:, :], ACT.Identity, scale=c_("hop", HOPS)).then_inc(y_hi_ok.sem, 1)

            def p_hop(b, h):
                for f in range(2):
                    act.wait_ge(*prod_done.at(b, 2 * h + f + 1))
                    act.activation(ta[:, fs(f)], acc_p[:, f, :], ACT.Copy).then_inc(hop_copied.sem, 1)
                if h < HOPS:
                    act.wait_ge(*hop_ok.at(b, 2 * h))
                    act.activation(y_hi[:, :], tg[:, :], ACT.Copy).then_inc(y_hi_ok.sem, 1)
                else:
                    act.wait_ge(*yt_turned.at(b, 1))
                    act.activation(y_hi[:, :], flat(tr_p), ACT.Copy).then_inc(y_hi_ok.sem, 1)

            def p_out(b):
                act.wait_ge(*l1_done.at(b, 1))
                act.activation(tg[:, :], flat(acc_p), ACT.Identity, bias=c_("hop_b")).then_inc(l1_biased.sem, 1)

            def q_ht(b, n):
                act.wait_ge(*ht_turned.at(b, n + 1))
                if n == 0:
                    act.activation(ht32[:, :], flat(tr_q), ACT.Copy).then_inc(ht32_ok.sem, 1)
                act.activation(ht_hi[:, :], flat(tr_q), ACT.Copy).then_inc(ht_hi_ok.sem, 1)

            def q_s(b):
                act.wait_ge(*s_done.at(b, 1))
                act.activation(t1[:, :], flat(acc_q), ACT.Identity, bias=c_("bse")).then_inc(s_ok.sem, 1)
                act.activation(tmp1[:, :], flat(acc_q), ACT.Square, bias=c_("bse")).then_inc(ss_ok.sem, 1)
                act.wait_ge(*ss_ok.at(b, 1))
                act.activation(ss_hi[:, :], tmp1[:, :], ACT.Copy).then_inc(ss_hi_ok.sem, 1)
                act.wait_ge(*r32_ok.at(b, 1))
                act.activation(ker_r[:, :], tmp1[:, :], ACT.Copy).then_inc(r_hi_ok.sem, 1)
                act.wait_ge(*l32_ok.at(b, 1))
                act.activation(ker_l[:, :], tmp2[:, :], ACT.Copy).then_inc(l_hi_ok.sem, 1)

            def q_msg(b):
                act.wait_ge(*msg_b.at(b, 1))
                act.activation(g_hi[:, :], t1[:, :], ACT.Relu).then_inc(msg_hi_ok.sem, 1)

            def q_ker(b, m):
                for u in (2 * m, 2 * m + 1):
                    act.wait_ge(*dist_done.at(b, u + 1))
                    if u >= 2:
                        act.wait_ge(*a_lo_ok.at(b, u - 1))
                    act.activation(a_f[:, u % 2, :], tr_q[:, u % 2, :], ACT.Exp).then_inc(a_f_ok.sem, 1)
                    act.wait_ge(*a_m_ok.at(b, u + 1))
                    if u >= 2:
                        act.wait_ge(*ker_done.at(b, u - 1))
                    act.activation(a_hi[:, u % 2, :], a_f[:, u % 2, :], ACT.Copy).then_inc(a_hi_ok.sem, 1)

            def q_nmp(b):
                act.wait_ge(*ker_done.at(b, 2 * NB))
                act.activation(nmp_hi[:, :], flat(acc_q), ACT.Copy).then_inc(nmp_hi_ok.sem, 1)

            def q_conv1(b):
                act.wait_ge(*c1_done.at(b, 1))
                act.activation(t1[:, :], flat(tr_q), ACT.Relu, bias=x_(X_B1), scale=x_(X_SC1)).then_inc(c1_f_ok.sem, 1)
                act.wait_ge(*c1_f_ok.at(b, 1))
                act.activation(c1_hi[:, PAD:PAD + N], t1[:, :], ACT.Copy).then_inc(c1_hi_ok.sem, 1)

            def q_conv2(b, f, t):
                if t == len(TAP_PARTS) - 1:
                    act.wait_ge(*xc_sum.at(b, f + 1))
                    act.activation(t1[:, fs(f)], t1[:, fs(f)], ACT.Relu, bias=x_(X_B2)).then_inc(xc_ok.sem, 1)
                    act.wait_ge(*xc_ok.at(b, f + 1))
                    act.activation(g_hi[:, fs(f)], t1[:, fs(f)], ACT.Copy).then_inc(xc_hi_ok.sem, 1)

            def q_gru(b, f):
                act.wait_ge(*gate_done.at(b, f + 1))
                if f == 1:
                    act.wait_ge(*gru_ok.at(b, 1))
                act.activation(gate[:, 0, :], tr_q[:, 0, :], ACT.Tanh, bias=x_(X_BR), scale=0.5)
                act.activation(gate[:, 1, :], tr_q[:, 1, :], ACT.Tanh, bias=x_(X_BZ), scale=0.5)
                act.activation(gate[:, 2, :], acc_q[:, 1, :], ACT.Identity, bias=x_(X_BHN), scale=0.5).then_inc(gate_th.sem, 1)
                act.wait_ge(*gate_n_in.at(b, f + 1))
                act.activation(gate[:, 2, :], gate[:, 2, :], ACT.Tanh, bias=c_("bih", 2)).then_inc(gate_n.sem, 1)

            def q_ln3(b):
                relu_rows(3, b, hq)
                act.activation(g_hi[:, :], hq[:, :], ACT.Copy).then_inc(h3_hi_ok.sem, 1)

            def q_rep(b):
                act.wait_ge(*rep_s_done.at(b, 1))
                act.activation(s1rep[:, :], flat(acc_q), ACT.Copy).then_inc(rep_s_ok.sem, 1)
                act.activation(urep[:, :], flat(tr_q), ACT.Copy).then_inc(rep_s_ok.sem, 1)

            def q_att(b, i, j):
                if i is not None:
                    act.wait_ge(*leaky_ok.at(b, i + 1))
                    act.activation(pre[:, i % 2, :], pre[:, i % 2, :], ACT.Exp).then_inc(alpha_ok.sem, 1)
                if j is not None:
                    act.wait_ge(*nmax_ok.at(b, j + 1))
                    act.activation(prow[j % 4][:, :], pre[:, j % 2, :], ACT.Exp, bias=nmax[:, j:j + 1],
                                   accum_out=psum3[:, j:j + 1]).then_inc(prow_ok.sem, 1)

            def q_edge(b, f):
                for m in range(NB):
                    n = NB * f + m
                    act.wait_ge(*p_turned.at(b, n + 1))
                    if n >= 2:
                        act.wait_ge(*edge_done.at(b, n - 1))
                    act.activation(pt_hi[:, m % 2, :], tr_q[:, m % 2, :], ACT.Copy).then_inc(pt_hi_ok.sem, 1)
                act.wait_ge(*edge_done.at(b, NB * (f + 1)))
                if f == 1:
                    act.wait_ge(*ot_turned.at(b, 1))
                act.activation(ot[:, :], acc_q[:, f, :], ACT.Copy).then_inc(ot_ok.sem, 1)

            walk(act, dict(p_ln0=p_ln0, p_adj=p_adj, p_h0t=p_h0t, p_agg=p_agg, p_z=p_z, p_silu=p_silu, p_ln1=p_ln1,
                           p_hop=p_hop, p_out=p_out, q_ln2=lambda b: relu_rows(2, b, hq), q_ht=q_ht, q_s=q_s,
                           q_msg=q_msg, q_ker=q_ker, q_nmp=q_nmp, q_conv1=q_conv1, q_conv2=q_conv2, q_gru=q_gru,
                           q_ln3=q_ln3, q_rep=q_rep, q_att=q_att, q_edge=q_edge))

        @block.vector
        def _(dve):
            steps_done = [0]

            def then(ins):
                steps_done[0] += 1
                ins.then_inc(set_ch.sem, 1)
                dve.wait_ge(set_ch.sem, steps_done[0])

            dve.wait_ge(setup_in.sem, 64)
            bn = {1: COLS["bn1"][0], 2: COLS["bn2"][0]}
            dve.tensor_scalar(colx[:, X_V:X_V + 1], col[:, bn[1] + 3:bn[1] + 4], BN_EPS, None, ALU.add)
            dve.tensor_scalar(colx[:, X_V + 1:X_V + 2], col[:, bn[2] + 3:bn[2] + 4], BN_EPS, None, ALU.add).then_inc(bn_v.sem, 1)
            dve.wait_ge(bn_r.sem, 1)
            for n, (sc, sh) in {1: (X_SC1, X_B1), 2: (X_SC2, X_B2)}.items():
                g = bn[n]
                then(dve.tensor_tensor(x_(sc), col[:, g:g + 1], colx[:, X_V + 1 + n:X_V + 2 + n], ALU.mult))
                then(dve.tensor_tensor(x_(sh), col[:, g + 2:g + 3], x_(sc), ALU.mult))
                then(dve.tensor_tensor(x_(sh), col[:, g + 1:g + 2], x_(sh), ALU.subtract))
            for g, at in ((0, X_BR), (1, X_BZ)):
                then(dve.tensor_tensor(x_(at), c_("bih", g), c_("bhh", g), ALU.add))
                then(dve.tensor_scalar(x_(at), x_(at), 0.5, None, ALU.mult))
            then(dve.tensor_scalar(x_(X_BHN), c_("bhh", 2), 0.5, None, ALU.mult))
            then(dve.tensor_scalar(colx[:, X_RMS:X_RMS + HC], col[:, COLS["rms"][0]:COLS["rms"][0] + HC], 0.5, None, ALU.mult))
            then(dve.memset(c1_hi[:, 0:PAD].bitcast(F32), 0.0))
            then(dve.memset(c1_hi[:, PAD + N:WIDE].bitcast(F32), 0.0))
            then(dve.memset(c1_lo[:, 0:PAD].bitcast(F32), 0.0))
            then(dve.memset(c1_lo[:, PAD + N:WIDE].bitcast(F32), 0.0))
            for n in range(2):
                then(dve.tensor_tensor_reduce(out=stage_v[:, 0, :], in0=stage_l3[:, n, :], in1=stage_l3[:, 2 + n, :],
                                              scale=1.0, scalar=0.0, op0=ALU.mult, op1=ALU.add,
                                              accum_out=colx[:, X_V + n:X_V + n + 1]))
                then(dve.tensor_scalar(stage_v[:, 1, :], ones, x_(X_V + n), None, ALU.mult))
                then(dve.tensor_copy(w_hi[:, NW_IN + n, :], stage_v[:, 1, :]))
                then(dve.tensor_tensor(w_lo[:, NW_IN + n, :], stage_v[:, 1, :], w_hi[:, NW_IN + n, :], ALU.subtract))
            dve.wait_ge(w_hi_ok.sem, 1)
            dve.tensor_tensor(w_lo[:, 0:NW_IN, :], stage_w[:, :, :], w_hi[:, 0:NW_IN, :], ALU.subtract).then_inc(w_ok.sem, 1)

            def ln(i, b, src, dst):
                g, s = i // 2, LN[i]
                for j in range(NB):
                    last = dve.bn_stats(stat[g][:, j, :], src[:, j, :])
                last.then_inc(s["stats"].sem, 1)
                dve.wait_ge(*s["stats"].at(b, 1))
                dve.memset(carrier[:, 0:1], 0.0)
                for j in range(NB):
                    last = dve.bn_aggr(mv[g][:, j, :], stat[g][:, j, :])
                last.then_inc(s["mean"].sem, 1)
                dve.wait_ge(*s["mean"].at(b, 1))
                dve.tensor_scalar(ve[g][:, :], mv[g][:, :, 1], LN_EPS, None, ALU.add).then_inc(s["var"].sem, 1)
                dve.wait_ge(*s["rstd"].at(b, 1))
                for j in range(NB):
                    last = dve.tensor_scalar(dst[:, ks(j)], src[:, j, :], mv[g][:, j, 0:1], rstd[g][:, j:j + 1],
                                             ALU.subtract, ALU.mult)
                last.then_inc(s["scaled"].sem, 1)

            def p_ln0(b):
                dve.wait_ge(*x_in.at(b, 16))
                ln(0, b, xp, hrow)
                dve.wait_ge(*y_hi_ok.at(b, Y_H0))
                dve.tensor_tensor(y_lo[:, :], hrow[:, :], y_hi[:, :], ALU.subtract).then_inc(y_lo_ok.sem, 1)

            def p_adj(b, k):
                dve.wait_ge(*adj_hi_ok.at(b, k + 1))
                dve.tensor_tensor(adj_lo[:, k, :], adj_in[:, k % 2, :], adj_hi[:, k, :], ALU.subtract).then_inc(adj_lo_ok.sem, 1)

            def p_deg(b):
                dve.wait_ge(*deg_summed.at(b, 1))
                dve.tensor_scalar(dg[:, 0, :], tr_p[:, 0, 0:NB], 1.0, None, ALU.mult).then_inc(deg_ch.sem, 1)
                dve.wait_ge(*deg_ch.at(b, 1))
                dve.tensor_scalar(dg[:, 1, :], dg[:, 0, :], DEG_EPS, None, ALU.add)
                dve.tensor_scalar(dg[:, 3, :], dg[:, 0, :], 0.0, None, ALU.is_gt).then_inc(deg_ch.sem, 1)
                dve.wait_ge(*deg_ch.at(b, 2))
                dve.reciprocal(dg[:, 2, :], dg[:, 1, :])
                dve.tensor_tensor(dg[:, 4, :], dg[:, 0, :], dg[:, 3, :], ALU.mult).then_inc(deg_ch.sem, 1)
                dve.wait_ge(*deg_ch.at(b, 3))
                dve.tensor_scalar(dg[:, 3, :], dg[:, 3, :], -1.0, 1.0, ALU.mult, ALU.add).then_inc(deg_ch.sem, 1)
                dve.wait_ge(*deg_ch.at(b, 4))
                dve.tensor_tensor(dg[:, 4, :], dg[:, 4, :], dg[:, 3, :], ALU.add).then_inc(deg_ch.sem, 1)
                dve.wait_ge(*deg_ch.at(b, 5))
                dve.reciprocal(dg[:, 5, :], dg[:, 4, :]).then_inc(deg_ch.sem, 1)

            def p_agg(b):
                dve.wait_ge(*eh_ok.at(b, 1))
                for f in range(2):
                    dve.wait_ge(*prod_done.at(b, f + 1))
                    dve.tensor_tensor(ta[:, fs(f)], acc_p[:, f, :], ta[:, fs(f)], ALU.add).then_inc(agg_ok.sem, 1)
                dve.wait_ge(*y_hi_ok.at(b, Y_AGG))
                dve.tensor_tensor(y_lo[:, :], ta[:, :], y_hi[:, :], ALU.subtract).then_inc(y_lo_ok.sem, 1)

            def p_rms(b, f):
                dve.wait_ge(*ms_done.at(b, f + 1))
                dve.tensor_scalar(ve4[:, :], tr_p[:, 0, 0:HB], 1.0 / H, RMS_EPS, ALU.mult, ALU.add).then_inc(ms_read.sem, 1)
                dve.wait_ge(*r4_ok.at(b, f + 1))
                shape = [P, HB, P]
                dve.tensor_tensor(sqsum[:, :].rearrange("p (j c) -> p j c", c=P), const[:, C_ID:C_ID + 1, :].to_broadcast(shape),
                                  r4[:, :].unsqueeze(2).to_broadcast(shape), ALU.mult).then_inc(diag_ok.sem, 1)
                dve.wait_ge(*rep_done.at(b, f + 1))
                dve.wait_ge(*zb_ok.at(b, HC * (f + 1)))
                for c in range(HC):
                    dve.scalar_tensor_tensor(zb[:, c, :], zb[:, c, :], x_(X_RMS + c), acc_p[:, 0, :],
                                             ALU.mult, ALU.mult).then_inc(u_ok.sem, 1)

            def p_silu(b, f):
                def silu(c):
                    dve.wait_ge(*th_ok.at(b, HC * f + c + 1))
                    dve.scalar_tensor_tensor(th[:, c % 2, :], th[:, c % 2, :], 1.0, zb[:, c, :],
                                             ALU.add, ALU.mult).then_inc(silu_ok.sem, 1)

                def low(c):
                    dve.wait_ge(*s_hi_ok.at(b, HC * f + c + 1))
                    dve.tensor_tensor(s_lo[:, c % 2, :], th[:, c % 2, :], s_hi[:, c % 2, :], ALU.subtract).then_inc(s_lo_ok.sem, 1)

                for c in (0, 2):
                    silu(c)
                    silu(c + 1)
                    low(c)
                    low(c + 1)

            def p_x1(b):
                dve.wait_ge(*y0_turned.at(b, 1))
                dve.tensor_tensor(xp[:, :, :], xp[:, :, :], blocks(tr_p), ALU.add).then_inc(x1_ok.sem, 1)

            def p_ln1(b):
                dve.wait_ge(*x1_ok.at(b, 1))
                ln(1, b, xp, hrow)
                dve.wait_ge(*y_hi_ok.at(b, Y_W3H))
                dve.scalar_tensor_tensor(y_lo[:, :], hrow[:, :], c_("hop", HOPS), y_hi[:, :],
                                         ALU.mult, ALU.subtract).then_inc(y_lo_ok.sem, 1)

            def p_hop(b, h):
                for f in range(2):
                    n = 2 * (h - 1) + f + 1
                    dve.wait_ge(*hop_turned.at(b, n))
                    shape = [P, HB, P]
                    dve.tensor_tensor(tg[:, fs(f)].rearrange("p (j c) -> p j c", c=P),
                                      tr_p[:, f, :].rearrange("p (j c) -> p j c", c=P),
                                      dg[:, 2, f * HB:(f + 1) * HB].unsqueeze(2).to_broadcast(shape), ALU.mult).then_inc(hop_scaled.sem, 1)
                    dve.wait_ge(*hop_scaled.at(b, n))
                    dve.scalar_tensor_tensor(tg[:, fs(f)], hrow[:, fs(f)], c_("hop", HOPS - h), tg[:, fs(f)],
                                             ALU.mult, ALU.add).then_inc(hop_ok.sem, 1)
                if h < HOPS:
                    dve.wait_ge(*y_hi_ok.at(b, Y_W3H + h))
                    dve.tensor_tensor(y_lo[:, :], tg[:, :], y_hi[:, :], ALU.subtract).then_inc(y_lo_ok.sem, 1)
                else:
                    dve.wait_ge(*y_hi_ok.at(b, Y_T))
                    dve.tensor_tensor(y_lo[:, :], flat(tr_p), y_hi[:, :], ALU.subtract).then_inc(y_lo_ok.sem, 1)

            def p_out(b):
                dve.wait_ge(*l1_biased.at(b, 1))
                dve.scalar_tensor_tensor(tg[:, :], tg[:, :], 0.2, tg[:, :], ALU.mult, ALU.max).then_inc(l1_leaky.sem, 1)
                dve.wait_ge(*deg_ch.at(b, 6))
                dve.wait_ge(*out_sent.at(b, 0))
                dve.tensor_copy(rdeg[:, :], dg[:, 5, :]).then_inc(rdeg_ok.sem, 1)
                dve.wait_ge(*l1_leaky.at(b, 1))
                dve.tensor_tensor(xq[:, :, :], xp[:, :, :], blocks(tg), ALU.add).then_inc(x2_ok.sem, 1)

            def q_ln2(b):
                dve.wait_ge(*x2_ok.at(b, 1))
                ln(2, b, xq, hq)

            def q_ht(b, n):
                dve.wait_ge(*ht_hi_ok.at(b, n + 1))
                dve.tensor_tensor(ht_lo[:, :], flat(tr_q), ht_hi[:, :], ALU.subtract).then_inc(ht_lo_ok.sem, 1)

            def q_s(b):
                dve.wait_ge(*ss_hi_ok.at(b, 1))
                dve.tensor_tensor(ss_lo[:, :], tmp1[:, :], ss_hi[:, :], ALU.subtract).then_inc(ss_lo_ok.sem, 1)
                dve.wait_ge(*rl_done.at(b, 1))
                dve.wait_ge(*ss_lo_ok.at(b, 1))
                dve.tensor_tensor(tmp1[:, :], t1[:, :], flat(tr_q), ALU.add).then_inc(r32_ok.sem, 1)
                dve.scalar_tensor_tensor(tmp2[:, :], t1[:, :], 2.0, flat(acc_q), ALU.mult, ALU.add).then_inc(l32_ok.sem, 1)
                dve.wait_ge(*r_hi_ok.at(b, 1))
                for a in (32, 96):
                    dve.tensor_tensor(ker_r[a:a + 32, :], tmp1[a:a + 32, :], ker_r[a:a + 32, :], ALU.subtract)
                dve.wait_ge(*l_hi_ok.at(b, 1))
                dve.tensor_tensor(ker_l[64:128, :], tmp2[64:128, :], ker_l[64:128, :], ALU.subtract).then_inc(rl_ok.sem, 1)

            def q_msg(b):
                dve.wait_ge(*msg_done.at(b, 1))
                dve.tensor_tensor(blocks(t1), blocks(acc_q), const[:, C_MSG:C_MSG + 1, :].to_broadcast([P, NB, P]),
                                  ALU.add).then_inc(msg_b.sem, 1)
                dve.wait_ge(*msg_hi_ok.at(b, 1))
                dve.scalar_tensor_tensor(g_lo[:, :], t1[:, :], 0.0, g_hi[:, :], ALU.max, ALU.subtract).then_inc(msg_lo_ok.sem, 1)

            def q_ker(b, m):
                for u in (2 * m, 2 * m + 1):
                    if u % 2 == 0:
                        dve.wait_ge(*row_got[m % 2].at(b, 16 * (m // 2 + 1)))
                    dve.wait_ge(*a_f_ok.at(b, u + 1))
                    dve.tensor_tensor(a_f[:, u % 2, :], a_f[:, u % 2, :], row_in[:, m % 2, fs(u % 2)], ALU.mult).then_inc(a_m_ok.sem, 1)
                    dve.wait_ge(*a_hi_ok.at(b, u + 1))
                    dve.tensor_tensor(a_lo[:, u % 2, :], a_f[:, u % 2, :], a_hi[:, u % 2, :], ALU.subtract).then_inc(a_lo_ok.sem, 1)

            def q_nmp(b):
                dve.wait_ge(*nmp_hi_ok.at(b, 1))
                dve.tensor_tensor(nmp_lo[:, :], flat(acc_q), nmp_hi[:, :], ALU.subtract).then_inc(nmp_lo_ok.sem, 1)

            def q_conv1(b):
                dve.wait_ge(*c1_hi_ok.at(b, 1))
                dve.tensor_tensor(c1_lo[:, PAD:PAD + N], t1[:, :], c1_hi[:, PAD:PAD + N], ALU.subtract).then_inc(c1_lo_ok.sem, 1)

            def q_conv2(b, f, t):
                if t == len(TAP_PARTS) - 1:
                    if f == 0:
                        dve.wait_ge(*c1_lo_ok.at(b, 1))
                    dve.wait_ge(*c2_done.at(b, f + 1))
                    dve.scalar_tensor_tensor(t1[:, fs(f)], acc_q[:, f, :], x_(X_SC2), ht32[:, fs(f)],
                                             ALU.mult, ALU.add).then_inc(xc_sum.sem, 1)
                    dve.wait_ge(*xc_hi_ok.at(b, f + 1))
                    dve.tensor_tensor(g_lo[:, fs(f)], t1[:, fs(f)], g_hi[:, fs(f)], ALU.subtract).then_inc(xc_lo_ok.sem, 1)

            def q_gru(b, f):
                dve.wait_ge(*gate_th.at(b, f + 1))
                dve.scalar_tensor_tensor(gate[:, 2, :], gate[:, 0, :], 1.0, gate[:, 2, :], ALU.add, ALU.mult).then_inc(gate_r.sem, 1)
                dve.wait_ge(*gate_r.at(b, f + 1))
                dve.tensor_tensor(gate[:, 2, :], acc_q[:, 0, :], gate[:, 2, :], ALU.add).then_inc(gate_n_in.sem, 1)
                dve.wait_ge(*gate_d.at(b, f + 1))
                dve.scalar_tensor_tensor(gate[:, 1, :], gate[:, 1, :], 1.0, gate[:, 0, :], ALU.add, ALU.mult).then_inc(gate_zd.sem, 1)
                dve.wait_ge(*gate_zd.at(b, f + 1))
                dve.scalar_tensor_tensor(t1[:, fs(f)], gate[:, 1, :], 0.5, gate[:, 2, :], ALU.mult, ALU.add).then_inc(gru_ok.sem, 1)

            def q_x3(b):
                dve.wait_ge(*gru_turned.at(b, 1))
                dve.tensor_tensor(xq[:, :, :], xq[:, :, :], blocks(tr_q), ALU.add).then_inc(x3_ok.sem, 1)

            def q_ln3(b):
                dve.wait_ge(*x3_ok.at(b, 1))
                ln(3, b, xq, hq)
                dve.wait_ge(*h3_hi_ok.at(b, 1))
                dve.tensor_tensor(g_lo[:, :], hq[:, :], g_hi[:, :], ALU.subtract).then_inc(h3_lo_ok.sem, 1)

            def q_att(b, i, j):
                if i is not None:
                    s = i % 2
                    dve.wait_ge(*row_got[s].at(b, 16 * (NB // 2 + i // 2 + 1)))
                    if i == 0:
                        dve.wait_ge(*rep_s_ok.at(b, 2))
                        dve.wait_ge(*rdeg_ok.at(b, 1))
                    if i >= 2:
                        dve.wait_ge(*prow_ok.at(b, i - 1))
                    dve.tensor_tensor_reduce(out=pre[:, s, :], in0=row_in[:, s, :], in1=urep[:, :], scale=1.0, scalar=0.0,
                                             op0=ALU.mult, op1=ALU.add, accum_out=s2raw[:, i:i + 1]).then_inc(s2_raw_ok.sem, 1)
                    dve.wait_ge(*s2_raw_ok.at(b, i + 1))
                    dve.tensor_tensor(s2[:, i:i + 1], s2raw[:, i:i + 1], rdeg[:, i:i + 1], ALU.mult).then_inc(s2_ok.sem, 1)
                    if i >= 4:
                        dve.wait_ge(*p_turned.at(b, NB))
                    elif i == 0:
                        dve.wait_ge(*gate_done.at(b, 2))
                    dve.tensor_scalar(prow[i % 4][:, :], row_in[:, s, :], 0.0, NEG_INF, ALU.is_le, ALU.mult)
                    dve.wait_ge(*s2_ok.at(b, i + 1))
                    dve.scalar_tensor_tensor(pre[:, s, :], s1rep[:, :], s2[:, i:i + 1], row_in[:, s, :],
                                             ALU.add, ALU.mult).then_inc(mask_ok.sem, 1)
                    dve.wait_ge(*mask_ok.at(b, i + 1))
                    if j is not None:
                        dve.wait_ge(*alpha_ok.at(b, j + 1))
                    dve.scalar_tensor_tensor(pre[:, s, :], pre[:, s, :], 0.2, pre[:, s, :], ALU.mult, ALU.max).then_inc(leaky_ok.sem, 1)
                if j is not None:
                    s = j % 2
                    if i is None:
                        dve.wait_ge(*alpha_ok.at(b, j + 1))
                        dve.memset(carrier[:, 1:2], 0.0)
                    dve.tensor_tensor_reduce(out=pre[:, s, :], in0=pre[:, s, :], in1=prow[j % 4][:, :], scale=1.0,
                                             scalar=-3e38, op0=ALU.add, op1=ALU.max, accum_out=amax[:, j:j + 1]).then_inc(att_ok.sem, 1)
                    dve.wait_ge(*att_ok.at(b, j + 1))
                    dve.tensor_scalar(nmax[:, j:j + 1], amax[:, j:j + 1], -1.0, None, ALU.mult).then_inc(nmax_ok.sem, 1)

            def q_edge(b, f):
                for m in range(NB):
                    dve.wait_ge(*pt_hi_ok.at(b, NB * f + m + 1))
                    dve.tensor_tensor(pt_lo[:, m % 2, :], tr_q[:, m % 2, :], pt_hi[:, m % 2, :], ALU.subtract).then_inc(pt_lo_ok.sem, 1)
                dve.wait_ge(*prow_ok.at(b, HB * (f + 1)))
                dve.reciprocal(rinv[:, f * HB:(f + 1) * HB], psum3[:, f * HB:(f + 1) * HB]).then_inc(rinv_ok.sem, 1)
                dve.wait_ge(*rinv_ok.at(b, f + 1))
                dve.wait_ge(*ot_turned.at(b, f + 1))
                for j in range(HB):
                    n = f * HB + j
                    last = dve.scalar_tensor_tensor(xq[:, n, :], tr_q[:, 0, ks(j)], rinv[:, n:n + 1], xq[:, n, :], ALU.mult, ALU.add)
                last.then_inc(out_ok.sem, 1)

            walk(dve, dict(p_ln0=p_ln0, p_adj=p_adj, p_deg=p_deg, p_agg=p_agg, p_rms=p_rms, p_silu=p_silu, p_x1=p_x1,
                           p_ln1=p_ln1, p_hop=p_hop, p_out=p_out, q_ln2=q_ln2, q_ht=q_ht, q_s=q_s, q_msg=q_msg,
                           q_ker=q_ker, q_nmp=q_nmp, q_conv1=q_conv1, q_conv2=q_conv2, q_gru=q_gru, q_x3=q_x3,
                           q_ln3=q_ln3, q_att=q_att, q_edge=q_edge))

        @block.tensor
        def _(pe):
            pe.wait_ge(setup_in.sem, 64)
            pe.wait_ge(w_ok.sem, 1)
            pe.wait_ge(set_act.sem, 1)

            def three(dst, l_hi, l_lo, r_hi, r_lo, first, last):
                pe.matmul(dst, l_lo, r_hi, start=first, stop=False)
                pe.matmul(dst, l_hi, r_lo, start=False, stop=False)
                return pe.matmul(dst, l_hi, r_hi, start=False, stop=last)

            def weight(dst, n, r_hi, r_lo, first=True, last=True):
                return three(dst, w_hi[:, n, :], w_lo[:, n, :], r_hi, r_lo, first, last)

            def turn(dst, src, n=NB):
                for j in range(n):
                    last = pe.transpose(dst[:, j // HB, ks(j % HB)], src[:, ks(j)], ident)
                return last

            def p_h0t(b):
                pe.wait_ge(*LN[0]["h"].at(b, 1))
                pe.wait_ge(*y_lo_ok.at(b, 0))
                turn(tr_p, hrow).then_inc(h0_turned.sem, 1)

            def p_deg(b):
                pe.wait_ge(*deg_added.at(b, NB))
                pe.wait_ge(*eh_ok.at(b, 1))
                for j in range(NB):
                    last = pe.matmul(tr_p[:, 0, j:j + 1], dacc[:, ks(j)], const[:, C_ONE, 0:1], start=True, stop=True)
                last.then_inc(deg_summed.sem, 1)

            def p_prod(b, h, f):
                if f == 0:
                    pe.wait_ge(*y_lo_ok.at(b, {0: Y_H0}.get(h, Y_W3H + h - 1)))
                if h == 0 and f == 0:
                    pe.wait_ge(*adj_lo_ok.at(b, NB))
                    pe.wait_ge(*l1_biased.at(b, 0))
                if h == 1:
                    pe.wait_ge(*(u_ok.at(b, 2 * HC) if f == 0 else y0_ok.at(b, 2)))
                if h > 1:
                    pe.wait_ge(*hop_copied.at(b, 2 * (h - 2) + f + 1))
                for k in range(NB):
                    last = three(acc_p[:, f, :], y_hi[:, ks(k)], y_lo[:, ks(k)], adj_hi[:, k, fs(f)], adj_lo[:, k, fs(f)],
                                 k == 0, k == NB - 1)
                last.then_inc(prod_done.sem, 1)

            def p_z(b, f):
                if f == 0:
                    pe.wait_ge(*y_lo_ok.at(b, Y_AGG))
                    pe.wait_ge(*deg_ch.at(b, 1))
                else:
                    pe.wait_ge(*ms_read.at(b, 1))
                for c in range(HC):
                    if HC * f + c >= 2:
                        pe.wait_ge(*sq_ok.at(b, HC * f + c - 1))
                    weight(tr_p[:, c % 2, :], W_MLP1 + c, y_hi[:, fs(f)], y_lo[:, fs(f)]).then_inc(z_done.sem, 1)

            def p_rms(b, f):
                pe.wait_ge(*sq_added.at(b, (HC - 1) * (f + 1)))
                pe.wait_ge(*sq_ok.at(b, HC * f + 3))
                for j in range(HB):
                    last = pe.matmul(tr_p[:, 0, j:j + 1], sqsum[:, ks(j)], const[:, C_ONE, 0:1], start=True, stop=True)
                last.then_inc(ms_done.sem, 1)
                pe.wait_ge(*diag_ok.at(b, f + 1))
                if f == 0:
                    pe.wait_ge(*agg_ok.at(b, 2))
                else:
                    pe.wait_ge(*u_ok.at(b, HC))
                pe.matmul(acc_p[:, 0, :], ones, sqsum[:, :], start=True, stop=True).then_inc(rep_done.sem, 1)

            def p_silu(b, f):
                if f == 1:
                    pe.wait_ge(*y0_ok.at(b, 1))
                for c in range(HC):
                    pe.wait_ge(*s_lo_ok.at(b, HC * f + c + 1))
                    weight(acc_p[:, 1, :], W_MLP2 + c, s_hi[:, c % 2, :], s_lo[:, c % 2, :], c == 0, c == HC - 1).then_inc(w2_done.sem, 1)

            def p_x1(b):
                pe.wait_ge(*y0_ok.at(b, 2))
                pe.wait_ge(*ms_read.at(b, 2))
                turn(tr_p, ta).then_inc(y0_turned.sem, 1)

            def p_hop(b, h):
                for f in range(2):
                    pe.wait_ge(*hop_copied.at(b, 2 * (h - 1) + f + 1))
                    if h == 1:
                        pe.wait_ge(*x1_ok.at(b, 1))
                    for j in range(HB):
                        last = pe.transpose(tr_p[:, f, ks(j)], ta[:, ks(f * HB + j)], ident)
                    last.then_inc(hop_turned.sem, 1)
                if h == HOPS:
                    pe.wait_ge(*hop_ok.at(b, 2 * HOPS))
                    turn(tr_p, tg).then_inc(yt_turned.sem, 1)

            def p_out(b):
                pe.wait_ge(*y_lo_ok.at(b, Y_T))
                pe.wait_ge(*hop_copied.at(b, 2 * HOPS))
                for j in range(NB):
                    last = three(acc_p[:, j // HB, ks(j % HB)], y_hi[:, ks(j)], y_lo[:, ks(j)],
                                 w_hi[:, W_HOP, :], w_lo[:, W_HOP, :], True, True)
                last.then_inc(l1_done.sem, 1)

            def q_ht(b, n):
                if n == 0:
                    pe.wait_ge(*LN[2]["h"].at(b, 1))
                else:
                    pe.wait_ge(*LN[3]["h"].at(b, 1))
                    pe.wait_ge(*x3_ok.at(b, 1))
                turn(tr_q, hq).then_inc(ht_turned.sem, 1)

            def q_s(b):
                pe.wait_ge(*ht_lo_ok.at(b, 1))
                for f in range(2):
                    last = weight(acc_q[:, f, :], W_SE, ht_hi[:, fs(f)], ht_lo[:, fs(f)])
                last.then_inc(s_done.sem, 1)
                pe.wait_ge(*ss_lo_ok.at(b, 1))
                for n, dst in ((1, tr_q), (0, acc_q)):
                    for f in range(2):
                        pe.matmul(dst[:, f, :], pat[:, n, :], ss_lo[:, fs(f)], start=True, stop=False)
                        last = pe.matmul(dst[:, f, :], pat[:, n, :], ss_hi[:, fs(f)], start=False, stop=True)
                last.then_inc(rl_done.sem, 1)

            def q_msg(b):
                pe.wait_ge(*l32_ok.at(b, 1))
                for j in range(NB):
                    last = three(acc_q[:, j // HB, ks(j % HB)], ht_hi[:, ks(j)], ht_lo[:, ks(j)],
                                 w_hi[:, W_MSG, :], w_lo[:, W_MSG, :], True, True)
                last.then_inc(msg_done.sem, 1)

            def q_ker(b, m):
                def dist(u):
                    if u >= 2:
                        pe.wait_ge(*a_f_ok.at(b, u - 1))
                    pe.matmul(tr_q[:, u % 2, :], ker_l[:, ks(u // 2)], ker_r[:, fs(u % 2)], start=True, stop=True).then_inc(dist_done.sem, 1)

                if m == 0:
                    pe.wait_ge(*rl_ok.at(b, 1))
                    dist(0)
                    dist(1)
                    pe.wait_ge(*msg_lo_ok.at(b, 1))
                for f in range(2):
                    u = 2 * m + f
                    if u + 2 < 2 * NB:
                        dist(u + 2)
                    pe.wait_ge(*a_lo_ok.at(b, u + 1))
                    three(acc_q[:, f, :], g_hi[:, ks(m)], g_lo[:, ks(m)], a_hi[:, f, :], a_lo[:, f, :],
                          m == 0, m == NB - 1).then_inc(ker_done.sem, 1)

            def q_conv1(b):
                pe.wait_ge(*a_f_ok.at(b, 2 * NB))
                for f in range(2):
                    last = weight(tr_q[:, f, :], W_CONV1, ht_hi[:, fs(f)], ht_lo[:, fs(f)])
                last.then_inc(c1_done.sem, 1)

            def q_conv2(b, f, part):
                if f == 0 and part == 0:
                    pe.wait_ge(*c1_lo_ok.at(b, 1))
                    pe.wait_ge(*nmp_lo_ok.at(b, 1))
                for t in TAP_PARTS[part]:
                    at = f * HALF + t
                    last = weight(acc_q[:, f, :], W_CONV2 + t, c1_hi[:, at:at + HALF], c1_lo[:, at:at + HALF], t == 0, t == TAPS - 1)
                if part == len(TAP_PARTS) - 1:
                    last.then_inc(c2_done.sem, 1)

            def q_gru(b, f):
                ht = ht_hi[:, fs(f)], ht_lo[:, fs(f)]
                nmp = nmp_hi[:, fs(f)], nmp_lo[:, fs(f)]
                xc = g_hi[:, fs(f)], g_lo[:, fs(f)]
                if f == 1:
                    pe.wait_ge(*gate_th.at(b, 1))
                for g in range(2):
                    weight(tr_q[:, g, :], W_HH + g, *ht, True, False)
                    weight(tr_q[:, g, :], W_IH + 2 * g + 1, *nmp, False, False)
                if f == 0:
                    pe.wait_ge(*xc_lo_ok.at(b, 2))
                else:
                    pe.wait_ge(*gate_n_in.at(b, 1))
                weight(acc_q[:, 1, :], W_HH + 2, *ht, True, True)
                weight(acc_q[:, 0, :], W_IH + 5, *nmp, True, False)
                weight(acc_q[:, 0, :], W_IH + 4, *xc, False, True)
                for g in range(2):
                    last = weight(tr_q[:, g, :], W_IH + 2 * g, *xc, False, True)
                last.then_inc(gate_done.sem, 1)

            def q_x3(b):
                pe.wait_ge(*gru_ok.at(b, 2))
                turn(tr_q, t1).then_inc(gru_turned.sem, 1)

            def q_rep(b):
                pe.wait_ge(*ht_lo_ok.at(b, 2))
                for dst, w in ((acc_q, W_S1), (tr_q, W_S2)):
                    for f in range(2):
                        last = weight(dst[:, f, :], w, ht_hi[:, fs(f)], ht_lo[:, fs(f)])
                last.then_inc(rep_s_done.sem, 1)

            def q_edge(b, f):
                def turn_p(m):
                    n = NB * f + m
                    if n >= 2:
                        pe.wait_ge(*pt_lo_ok.at(b, n - 1))
                    for j in range(HB):
                        last = pe.transpose(tr_q[:, m % 2, ks(j)], prow[j][:, ks(m)], ident)
                    last.then_inc(p_turned.sem, 1)

                pe.wait_ge(*prow_ok.at(b, HB * (f + 1)))
                if f == 0:
                    pe.wait_ge(*rep_s_ok.at(b, 2))
                    pe.wait_ge(*h3_lo_ok.at(b, 1))
                else:
                    pe.wait_ge(*out_ok.at(b, 1))
                turn_p(0)
                for m in range(NB):
                    if m + 1 < NB:
                        turn_p(m + 1)
                    pe.wait_ge(*pt_lo_ok.at(b, NB * f + m + 1))
                    three(acc_q[:, f, :], g_hi[:, ks(m)], g_lo[:, ks(m)], pt_hi[:, m % 2, :], pt_lo[:, m % 2, :],
                          m == 0, m == NB - 1).then_inc(edge_done.sem, 1)
                pe.wait_ge(*ot_ok.at(b, f + 1))
                for j in range(HB):
                    last = pe.transpose(tr_q[:, 0, ks(j)], ot[:, ks(j)], ident)
                last.then_inc(ot_turned.sem, 1)

            walk(pe, dict(p_h0t=p_h0t, p_deg=p_deg, p_prod=p_prod, p_z=p_z, p_rms=p_rms, p_silu=p_silu, p_x1=p_x1,
                          p_hop=p_hop, p_out=p_out, q_ht=q_ht, q_s=q_s, q_msg=q_msg, q_ker=q_ker, q_conv1=q_conv1,
                          q_conv2=q_conv2, q_gru=q_gru, q_x3=q_x3, q_rep=q_rep, q_edge=q_edge))


def kernel(**inputs):
    import numpy as np
    import concourse.bacc as bacc
    from concourse.bass_utils import run_bass_kernel_spmd

    a = {k: np.ascontiguousarray(v) for k, v in inputs.items()}
    f32 = np.float32

    mats = [a["L0_gnn_W1"][:, c * P:(c + 1) * P] for c in range(HC)]
    mats += [a["L0_gnn_W2"][c * P:(c + 1) * P, :] for c in range(HC)]
    mats += [a["L1_gnn_W"].T, a["L2_gnn_conv1_w"][:, :, 0].T]
    mats += [a["L2_gnn_conv2_w"][:, :, t].T for t in range(TAPS)]
    mats += [a["L2_gnn_w_msg"].T]
    se = np.zeros((D, P), f32)
    bse = np.zeros((P,), f32)
    for q in range(4):
        se[:, 32 * q:32 * q + 3] = a["L2_gnn_w_se"].T
        bse[32 * q:32 * q + 3] = a["L2_gnn_b_se"]
        bse[32 * q + 3] = 1.0
    mats += [se]
    mats += [a["L2_gnn_w_ih"][g * P:(g + 1) * P, h * P:(h + 1) * P].T for g in range(3) for h in range(2)]
    mats += [a["L2_gnn_w_hh"][g * P:(g + 1) * P, :].T for g in range(3)]
    wpack = np.stack(mats, axis=1).reshape(P, NW_IN * P)
    w3 = a["L3_gnn_w3"][:, 0]
    rep = [np.broadcast_to(w3[n * P:(n + 1) * P], (P, P)) for n in range(2)]
    l3pack = np.stack([a["L3_gnn_W1"], a["L3_gnn_W2"], *rep], axis=1).reshape(P, 4 * P)

    pat_l, pat_r = np.zeros((P, P), f32), np.zeros((P, P), f32)
    for q in range(4):
        pat_r[0:3, 32 * q + 3] = -1.0
        pat_r[3, 32 * q + 3] = -1.0
        pat_r[3, 32 * q + 4] = 1.0
        pat_l[0:3, 32 * q + 4] = -1.0
        pat_l[3, 32 * q + 3] = -1.0
    cpack = np.stack([np.eye(P, dtype=f32), np.ones((P, P), f32), pat_l, pat_r,
                      np.broadcast_to(a["L2_gnn_b_msg"], (P, P))], axis=1).reshape(P, 5 * P)
    columns = [a["L0_gnn_b1"].reshape(HC, P), a["L0_gnn_rms_weight"].reshape(HC, P), a["L0_gnn_b2"][None]]
    columns += [a[f"L2_gnn_bn{n}_{v}"][None] for n in (1, 2) for v in "gbmv"]
    columns += [a["L2_gnn_b_ih"].reshape(3, P), a["L2_gnn_b_hh"].reshape(3, P)]
    columns += [np.broadcast_to(a["L1_gnn_conv_w"][:, None], (HOPS + 1, P)),
                np.broadcast_to(a["L1_gnn_conv_b"][:, None], (1, P)),
                np.broadcast_to(a["L0_gnn_epsilon"].reshape(1, 1), (1, P)), bse[None]]
    cols = np.concatenate(columns, axis=0).T

    arrays = dict(x=a["x"], adj=a["adj"], adj_t=a["adj"].transpose(0, 2, 1), wpack=wpack, l3pack=l3pack,
                  cpack=cpack, cols=cols)
    arrays = {f"in_{k}": np.ascontiguousarray(v) for k, v in arrays.items()}
    nc = bacc.Bacc("TRN2", target_bir_lowering=False, num_devices=1, dynamic_dma_scratch_size=1024)
    args = [nc.dram_tensor(k, v.shape, F32, kind="ExternalInput").ap() for k, v in arrays.items()]
    out = nc.dram_tensor("out", (B, N, D), F32, kind="ExternalOutput").ap()
    build(nc, *args, out)
    r = run_bass_kernel_spmd(nc, [arrays], core_ids=[0])
    return r.results[0]["out"]
```

```python
from contextlib import ExitStack

import concourse.bass as bass
from concourse import mybir

ALU = mybir.AluOpType
ACT = mybir.ActivationFunctionType
F32 = mybir.dt.float32
F32R = mybir.dt.float32r
BF16 = mybir.dt.bfloat16

P = 128
B, N, D, H = 8, 1024, 128, 512
NB = N // P
HALF = N // 2
HB = NB // 2
HC = H // P
TAPS = 17
PAD = TAPS // 2
HOPS = 3
LN_EPS, RMS_EPS, DEG_EPS, BN_EPS = 1e-5, 1e-6, 1e-9, 1e-5
NEG_INF = -9e15

W_MLP1, W_MLP2, W_HOP, W_CONV1, W_CONV2 = 0, HC, 2 * HC, 2 * HC + 1, 2 * HC + 2
W_MSG = W_CONV2 + TAPS
W_SE = W_MSG + 1
W_IH = W_SE + 1
W_HH = W_IH + 6
NW_IN = W_HH + 3
W_S1, W_S2 = NW_IN, NW_IN + 1
NW = NW_IN + 2

COLS = dict(b1=(0, HC), rms=(4, HC), b2=(8, 1), bn1=(9, 4), bn2=(13, 4), bih=(17, 3), bhh=(20, 3),
            hop=(23, HOPS + 1), hop_b=(27, 1), eps=(28, 1), bse=(29, 1))
NCOL = 30
C_ID, C_ONE, C_PL, C_PR, C_MSG = range(5)


class Signal:

    def __init__(self, ctx, nc, name, per=1):
        self.sem, self.per = ctx.enter_context(nc.semaphore(name)), per

    def at(self, b, n):
        return self.sem, b * self.per + n


def order():
    p = [("p_load",)] + [("p_ln", 0, t) for t in range(3)] + [("p_h0t", t) for t in range(2)]
    for k in range(NB + 1):
        p += [("p_adj", k)] if k < NB else []
        p += [("p_prod0", k - 1)] if k > 0 else []
    p += [("p_deg",)] + [("p_agg", t) for t in range(3)]
    z = [[("p_z", f, c) for c in range(HC)] for f in range(2)]
    rms = [[("p_rms", f, t) for t in range(3)] for f in range(2)]
    silu = [[("p_silu", f, t) for t in range(9)] for f in range(2)]
    p += z[0] + rms[0] + silu[0][:3] + z[1][:2] + silu[0][3:6] + z[1][2:] + silu[0][6:] + rms[1] + silu[1]
    p += [("p_x1", t) for t in range(2)] + [("p_ln", 1, t) for t in range(3)]
    for h in range(1, HOPS + 1):
        p += [("p_prod", h, 0), ("p_hop", h, 0), ("p_prod", h, 1)] + [("p_hop", h, t) for t in range(1, 6)]
    q = [("q_ln", 2, t) for t in range(2)] + [("q_ht", 0, t) for t in range(3)] + [("q_s", t) for t in range(7)]
    q += [("q_msg", t) for t in range(4)] + [("q_ker", u) for u in range(2 * NB + 2)]
    q += [("q_nmp", t) for t in range(2)] + [("q_conv1", t) for t in range(3)]
    for f in range(2):
        q += [("q_conv2", f, t) for t in range(len(TAP_PARTS))] + [("q_xc", f, t) for t in range(3)]
    q += [("q_gru", f, t) for f in range(2) for t in range(5)] + [("q_x3", t) for t in range(2)]
    q += [("q_ln", 3, t) for t in range(3)] + [("q_ht", 1, t) for t in range(3)] + [("q_rep", t) for t in range(2)]
    for s in range(NB + 2):
        for t in (2, 1, 0):
            if 0 <= s - t < NB:
                q.append(("q_att", s - t, t))
        if s >= 3 and s % 2 == 1:
            q += [("q_edge", s // 2 - 1, v) for v in range(4)]
            if s % 4 == 1:
                q += [("q_edge", s // 2 - 1, v) for v in (4, 5)]
    return p, q


TAP_PARTS = [range(0, 3), range(3, 6), range(6, 9), range(9, 12), range(12, 15), range(15, TAPS)]
P_STEPS, Q_STEPS = order()
P_LAST = [("p_out", t) for t in range(4)]


def beside(p, q, places):
    out, n = [], 0
    for m in range(len(q) + 1):
        while n < len(p) and places[n] <= m:
            out.append(p[n])
            n += 1
        out += q[m:m + 1]
    return out


BODY = beside(P_STEPS, Q_STEPS, [round(n * len(Q_STEPS) / len(P_STEPS)) for n in range(len(P_STEPS))]) + P_LAST


def build(nc, x, adj, adj_t, wpack, l3pack, cpack, cols, out):
    ctx = ExitStack()
    with ctx:
        base = (nc.sbuf_base + 63) // 64 * 64
        top = [base]

        def room(nbytes):
            at = top[0]
            top[0] += (nbytes + 63) // 64 * 64
            return at

        def tile(name, shape, dt, at=None):
            n = 4 if dt in (F32, F32R) else 2
            for s in shape[1:]:
                n *= s
            return nc.alloc_sbuf_tensor_at(name, shape, dt, offset=room(n) if at is None else at)

        KB4 = 4 * N
        w_hi = tile("w_hi", [P, NW, P], F32R)
        w_lo = tile("w_lo", [P, NW, P], F32R)
        const = tile("const", [P, 5, P], F32)
        pat = tile("pat", [P, 2, P], F32R)
        col = tile("col", [P, NCOL], F32)
        colx = tile("colx", [P, 16], F32)
        halves = tile("halves", [P, NB], F32)
        adj_hi = tile("adj_hi", [P, NB, N], F32R)
        at_lo = room(NB * KB4)
        adj_lo = tile("adj_lo", [P, NB, N], F32R, at_lo)
        stage_w = tile("stage_w", [P, NW_IN, P], F32, at_lo)
        stage_l3 = tile("stage_l3", [P, 4, P], F32, at_lo + NW_IN * 512)
        stage_v = tile("stage_v", [P, 2, P], F32, at_lo + (NW_IN + 4) * 512)
        adj_in = tile("adj_in", [P, 2, N], F32)
        row_in = tile("row_in", [P, 2, N], F32)

        xp = tile("xp", [P, NB, D], F32)
        y_hi = tile("y_hi", [P, N], F32R)
        y_lo = tile("y_lo", [P, N], F32R)
        at = room(KB4)
        hrow = tile("hrow", [P, N], F32, at)
        th = tile("th", [P, 2, HALF], F32, at)
        at = room(KB4)
        ta = tile("ta", [P, N], F32, at)
        sqt = tile("sqt", [P, HALF], F32, at + 4 * HALF)
        at = room(HC * HALF * 4)
        zb = tile("zb", [P, HC, HALF], F32, at)
        dacc = tile("dacc", [P, N], F32, at)
        tg = tile("tg", [P, N], F32, at)
        sqsum = tile("sqsum", [P, HALF], F32)
        at = room(KB4)
        s_hi = tile("s_hi", [P, 2, HALF], F32R, at)
        s_lo = tile("s_lo", [P, 2, HALF], F32R)

        xq = tile("xq", [P, NB, D], F32)
        at_h32 = room(KB4)
        ht32 = tile("ht32", [P, N], F32, at_h32)
        s1rep = tile("s1rep", [P, N], F32, at_h32)
        at = room(2 * KB4)
        ht_hi = tile("ht_hi", [P, N], F32R, at)
        ht_lo = tile("ht_lo", [P, N], F32R, at + KB4)
        pt_hi = tile("pt_hi", [P, 2, HALF], F32R, at)
        pt_lo = tile("pt_lo", [P, 2, HALF], F32R, at + KB4)
        WIDE = N + 2 * PAD
        at = room(4 * WIDE * 2 + 2 * KB4)
        c1_hi = tile("c1_hi", [P, WIDE], F32R, at)
        c1_lo = tile("c1_lo", [P, WIDE], F32R, at + 4 * WIDE)
        ker_r = tile("ker_r", [P, N], F32R, at + 4 * PAD)
        ker_l = tile("ker_l", [P, N], F32R, at + 4 * WIDE + 4 * PAD)
        at3 = at + 8 * WIDE
        nmp_hi = tile("nmp_hi", [P, N], F32R, at3)
        nmp_lo = tile("nmp_lo", [P, N], F32R, at3 + KB4)
        ss_hi = tile("ss_hi", [P, N], F32R, at3)
        ss_lo = tile("ss_lo", [P, N], F32R, at3 + KB4)
        a_lo = tile("a_lo", [P, 3, HALF], F32R, at3)
        prow = [tile(f"prow{n}", [P, N], F32, o) for n, o in
                enumerate((at + 4 * PAD, at + 4 * WIDE + 4 * PAD, at3, at3 + KB4))]
        g_hi = tile("g_hi", [P, N], F32R)
        g_lo = tile("g_lo", [P, N], F32R)
        at = room(KB4)
        t1 = tile("t1", [P, N], F32, at)
        urep = tile("urep", [P, N], F32, at)
        at = room(2 * KB4 + 2 * HALF * 4)
        hq = tile("hq", [P, N], F32, at)
        tmp1 = tile("tmp1", [P, N], F32, at)
        tmp2 = tile("tmp2", [P, N], F32, at + KB4)
        a_f = tile("a_f", [P, 3, HALF], F32, at)
        a_hi = tile("a_hi", [P, 3, HALF], F32R, at + 12 * HALF)
        gate = tile("gate", [P, 3, HALF], F32, at)
        pre = tile("pre", [P, 2, N], F32, at)
        ot = tile("ot", [P, HALF], F32, at + 2 * KB4)

        stat = [tile(f"stat{s}", [P, NB, 6], F32) for s in "pq"]
        mv = [tile(f"mv{s}", [P, NB, 2], F32) for s in "pq"]
        ve = [tile(f"ve{s}", [P, NB], F32) for s in "pq"]
        rstd = [tile(f"rstd{s}", [P, NB], F32) for s in "pq"]
        ve4 = tile("ve4", [P, HB], F32)
        r4 = tile("r4", [P, HB], F32)
        dg = tile("dg", [P, 6, NB], F32)
        rdeg = tile("rdeg", [P, NB], F32)
        s2raw = tile("s2raw", [P, NB], F32)
        s2 = tile("s2", [P, NB], F32)
        amax = tile("amax", [P, NB], F32)
        nmax = tile("nmax", [P, NB], F32)
        psum3 = tile("psum3", [P, NB], F32)
        rinv = tile("rinv", [P, NB], F32)
        carrier = tile("carrier", [P, 2], F32)
        nc_left = nc.sbuf_usable_end - top[0]
        assert nc_left >= 0, nc_left

        ident, ones = const[:, C_ID, :], const[:, C_ONE, :]

        def psum(name):
            return ctx.enter_context(nc.psum_tensor(name, [P, 2, HALF], F32))

        acc_p, tr_p, acc_q, tr_q = psum("acc_p"), psum("tr_p"), psum("acc_q"), psum("tr_q")

        def flat(t):
            return t[:, :, :].rearrange("p f n -> p (f n)")

        def blocks(t):
            if len(t.shape) == 3:
                return t[:, :, :].rearrange("p f (j c) -> p (f j) c", c=P)
            return t[:, :].rearrange("p (j c) -> p j c", c=P)

        def c_(name, n=0):
            at = COLS[name][0] + n
            return col[:, at:at + 1]

        X_SC1, X_B1, X_SC2, X_B2, X_BR, X_BZ, X_BHN, X_RMS, X_V = 0, 1, 2, 3, 4, 5, 6, 8, 12

        def x_(n):
            return colx[:, n:n + 1]

        def fs(f):
            return slice(f * HALF, (f + 1) * HALF)

        def ks(k):
            return slice(k * P, (k + 1) * P)

        S = {}

        def sig(name, per=1):
            S[name] = Signal(ctx, nc, name, per)
            return S[name]

        setup_in = sig("setup_in"); w_hi_ok = sig("w_hi_ok"); w_ok = sig("w_ok"); pool_const = sig("pool_const")
        bn_v = sig("bn_v"); bn_r = sig("bn_r"); set_ch = sig("set_ch"); set_act = sig("set_act")
        x_in = sig("x_in", 16)
        adj_got = [sig(f"adj_got{s}", 16 * NB // 2) for s in range(2)]
        row_got = [sig(f"row_got{s}", 16 * NB) for s in range(2)]
        out_sent = sig("out_sent", 16)
        LN = [dict(stats=sig(f"ln{i}_stats"), mean=sig(f"ln{i}_mean"), var=sig(f"ln{i}_var"),
                   rstd=sig(f"ln{i}_rstd"), scaled=sig(f"ln{i}_scaled"), h=sig(f"ln{i}_h")) for i in range(4)]
        adj_hi_ok = sig("adj_hi_ok", NB); adj_lo_ok = sig("adj_lo_ok", NB); deg_added = sig("deg_added", NB)
        Y_H0, Y_AGG, Y_W3H, Y_HOP1, Y_HOP2, Y_T = range(1, 7)
        y_hi_ok = sig("y_hi_ok", 6); y_lo_ok = sig("y_lo_ok", 6)
        h0_turned = sig("h0_turned"); eh_ok = sig("eh_ok"); deg_summed = sig("deg_summed"); deg_ok = sig("deg_ok")
        deg_ch = sig("deg_ch", 6)
        prod_done = sig("prod_done", 2 * (HOPS + 1)); agg_ok = sig("agg_ok", 2)
        z_done = sig("z_done", 2 * HC); zb_ok = sig("zb_ok", 2 * HC); sq_ok = sig("sq_ok", 2 * HC)
        sq_added = sig("sq_added", 2 * (HC - 1))
        ms_done = sig("ms_done", 2); ms_read = sig("ms_read", 2); r4_ok = sig("r4_ok", 2); diag_ok = sig("diag_ok", 2)
        rep_done = sig("rep_done", 2); u_ok = sig("u_ok", 2 * HC); th_ok = sig("th_ok", 2 * HC)
        silu_ok = sig("silu_ok", 2 * HC); s_hi_ok = sig("s_hi_ok", 2 * HC); s_lo_ok = sig("s_lo_ok", 2 * HC)
        w2_done = sig("w2_done", 2 * HC); y0_ok = sig("y0_ok", 2)
        y0_turned = sig("y0_turned"); x1_ok = sig("x1_ok")
        hop_copied = sig("hop_copied", 2 * HOPS); hop_turned = sig("hop_turned", 2 * HOPS)
        hop_scaled = sig("hop_scaled", 2 * HOPS); hop_ok = sig("hop_ok", 2 * HOPS)
        yt_turned = sig("yt_turned"); l1_done = sig("l1_done"); l1_biased = sig("l1_biased"); l1_leaky = sig("l1_leaky")
        rdeg_ok = sig("rdeg_ok"); x2_ok = sig("x2_ok")
        ht_turned = sig("ht_turned", 2); ht32_ok = sig("ht32_ok"); ht_hi_ok = sig("ht_hi_ok", 2); ht_lo_ok = sig("ht_lo_ok", 2)
        s_done = sig("s_done"); s_ok = sig("s_ok"); ss_ok = sig("ss_ok"); ss_hi_ok = sig("ss_hi_ok"); ss_lo_ok = sig("ss_lo_ok")
        rl_done = sig("rl_done"); r32_ok = sig("r32_ok"); l32_ok = sig("l32_ok"); r_hi_ok = sig("r_hi_ok"); l_hi_ok = sig("l_hi_ok")
        rl_ok = sig("rl_ok")
        msg_done = sig("msg_done"); msg_b = sig("msg_b"); msg_hi_ok = sig("msg_hi_ok"); msg_lo_ok = sig("msg_lo_ok")
        dist_done = sig("dist_done", 2 * NB); a_f_ok = sig("a_f_ok", 2 * NB); a_m_ok = sig("a_m_ok", 2 * NB); a_hi_ok = sig("a_hi_ok", 2 * NB)
        a_lo_ok = sig("a_lo_ok", 2 * NB); ker_done = sig("ker_done", 2 * NB)
        nmp_hi_ok = sig("nmp_hi_ok"); nmp_lo_ok = sig("nmp_lo_ok")
        c1_done = sig("c1_done"); c1_f_ok = sig("c1_f_ok"); c1_hi_ok = sig("c1_hi_ok"); c1_lo_ok = sig("c1_lo_ok")
        c2_done = sig("c2_done", 2); xc_sum = sig("xc_sum", 2); xc_ok = sig("xc_ok", 2); xc_hi_ok = sig("xc_hi_ok", 2); xc_lo_ok = sig("xc_lo_ok", 2)
        gate_done = sig("gate_done", 2); gate_th = sig("gate_th", 2); gate_r = sig("gate_r", 2); gate_n_in = sig("gate_n_in", 2)
        gate_n = sig("gate_n", 2); gate_d = sig("gate_d", 2); gate_zd = sig("gate_zd", 2); gru_ok = sig("gru_ok", 2)
        gru_turned = sig("gru_turned"); x3_ok = sig("x3_ok"); h3_hi_ok = sig("h3_hi_ok"); h3_lo_ok = sig("h3_lo_ok")
        rep_s_done = sig("rep_s_done"); rep_s_ok = sig("rep_s_ok", 2)
        s2_raw_ok = sig("s2_raw_ok", NB); s2_ok = sig("s2_ok", NB); pre_ok = sig("pre_ok", NB); leaky_ok = sig("leaky_ok", NB)
        alpha_ok = sig("alpha_ok", NB); mask_ok = sig("mask_ok", NB); att_ok = sig("att_ok", NB); nmax_ok = sig("nmax_ok", NB); prow_ok = sig("prow_ok", NB)
        p_turned = sig("p_turned", 2 * NB); pt_hi_ok = sig("pt_hi_ok", 2 * NB); pt_lo_ok = sig("pt_lo_ok", 2 * NB); edge_done = sig("edge_done", 2 * NB)
        ot_ok = sig("ot_ok", 2); ot_turned = sig("ot_turned", 2); rinv_ok = sig("rinv_ok", 2); out_ok = sig("out_ok", 2)

        block = ctx.enter_context(nc.Block())

        def walk(eng, steps):
            def go(names, bp, bq):
                for name, *args in names:
                    if name in steps:
                        steps[name](bp if name[0] == "p" else bq, *args)
            go(P_STEPS + P_LAST, 0, None)
            with eng.Fori(1, B) as i:
                go(BODY, i, i - 1)
            go(Q_STEPS, None, B - 1)

        @block.sync
        def _(sp):
            sp.dma_start(stage_w[:, :, :].rearrange("p a b -> p (a b)"), wpack).then_inc(setup_in.sem, 16)
            sp.dma_start(stage_l3[:, :, :].rearrange("p a b -> p (a b)"), l3pack).then_inc(setup_in.sem, 16)
            sp.dma_start(const[:, :, :].rearrange("p a b -> p (a b)"), cpack).then_inc(setup_in.sem, 16)
            sp.dma_start(col[:, :], cols).then_inc(setup_in.sem, 16)

            def p_load(b):
                sp.wait_ge(*x2_ok.at(b, 0))
                sp.dma_start(xp[:, :, :], x[b].rearrange("(j p) d -> p j d", p=P)).then_inc(x_in.sem, 16)

            def p_adj(b, k):
                sp.wait_ge(*adj_lo_ok.at(b, max(k - 1, 0)))
                sp.wait_ge(*deg_added.at(b, max(k - 1, 0)))
                sp.dma_start(adj_in[:, k % 2, :], adj_t[b, k * P:(k + 1) * P, :]).then_inc(adj_got[k % 2].sem, 16)

            def q_ker(b, u):
                if u % 2 == 1 or u >= 2 * NB:
                    return
                m = u // 2
                if m >= 2:
                    sp.wait_ge(*a_m_ok.at(b, 2 * (m - 1)))
                else:
                    sp.wait_ge(*x2_ok.at(b, 1))
                sp.dma_start(row_in[:, m % 2, :], adj_t[b, m * P:(m + 1) * P, :]).then_inc(row_got[m % 2].sem, 16)

            def q_att(b, i, t):
                if t != 0:
                    return
                if i >= 2:
                    sp.wait_ge(*mask_ok.at(b, i - 1))
                else:
                    sp.wait_ge(*a_m_ok.at(b, 2 * (NB - 1 + i)))
                sp.dma_start(row_in[:, i % 2, :], adj[b, i * P:(i + 1) * P, :]).then_inc(row_got[i % 2].sem, 16)

            def q_edge(b, q, v):
                if q == 3 and v == 5:
                    sp.wait_ge(*out_ok.at(b, 2))
                    sp.dma_start(out[b].rearrange("(j p) d -> p j d", p=P), xq[:, :, :]).then_inc(out_sent.sem, 16)

            walk(sp, dict(p_load=p_load, p_adj=p_adj, q_ker=q_ker, q_att=q_att, q_edge=q_edge))
            sp.wait_ge(*out_sent.at(B, 0))

        @block.gpsimd
        def _(pool):
            pool.memset(halves[:, :], -0.5).then_inc(pool_const.sem, 1)
            pool.wait_ge(pool_const.sem, 1)
            pool.wait_ge(bn_v.sem, 1)
            pool.tensor_tensor(colx[:, X_V + 2:X_V + 4], colx[:, X_V:X_V + 2], halves[:, 0:2], ALU.pow).then_inc(bn_r.sem, 1)

            def ln(b, i, t):
                if t != 0:
                    return
                g = i // 2
                pool.wait_ge(*LN[i]["var"].at(b, 1))
                pool.tensor_tensor(rstd[g][:, :], ve[g][:, :], halves[:, :], ALU.pow).then_inc(LN[i]["rstd"].sem, 1)

            def p_adj(b, k):
                pool.wait_ge(*adj_got[k % 2].at(b, 16 * (k // 2 + 1)))
                if k == 1:
                    pool.wait_ge(*x2_ok.at(b, 0))
                    pool.tensor_tensor(dacc[:, :], adj_in[:, 0, :], adj_in[:, 1, :], ALU.add).then_inc(deg_added.sem, 2)
                if k > 1:
                    pool.wait_ge(*deg_added.at(b, k))
                    pool.tensor_tensor(dacc[:, :], dacc[:, :], adj_in[:, k % 2, :], ALU.add).then_inc(deg_added.sem, 1)

            def p_z(b, f, c):
                if c > 0:
                    pool.wait_ge(*sq_ok.at(b, HC * f + c + 1))
                    pool.tensor_tensor(sqsum[:, :], sqsum[:, :], sqt[:, :], ALU.add).then_inc(sq_added.sem, 1)

            def p_rms(b, f, t):
                if t == 0:
                    pool.wait_ge(*ms_read.at(b, f + 1))
                    pool.tensor_tensor(r4[:, :], ve4[:, :], halves[:, 0:HB], ALU.pow).then_inc(r4_ok.sem, 1)

            def q_gru(b, f, t):
                if t != 3:
                    return
                pool.wait_ge(*gate_n.at(b, f + 1))
                pool.tensor_tensor(gate[:, 0, :], ht32[:, fs(f)], gate[:, 2, :], ALU.subtract).then_inc(gate_d.sem, 1)

            walk(pool, dict(p_ln=ln, q_ln=ln, p_adj=p_adj, p_z=p_z, p_rms=p_rms, q_gru=q_gru))

        @block.scalar
        def _(act):
            act.wait_ge(setup_in.sem, 64)
            act.activation(w_hi[:, 0:NW_IN, :], stage_w[:, :, :], ACT.Copy).then_inc(w_hi_ok.sem, 1)
            act.activation(pat[:, :, :], const[:, C_PL:C_PR + 1, :], ACT.Copy).then_inc(set_act.sem, 1)

            def ln(b, i, t):
                h = hrow if i < 2 else hq
                if t == 1:
                    act.wait_ge(*LN[i]["scaled"].at(b, 1))
                    act.activation(h[:, :], h[:, :], ACT.Relu).then_inc(LN[i]["h"].sem, 1)
                    if i != 2:
                        act.wait_ge(*LN[i]["h"].at(b, 1))
                    if i == 0:
                        act.activation(y_hi[:, :], h[:, :], ACT.Copy).then_inc(y_hi_ok.sem, 1)
                    if i == 1:
                        act.activation(y_hi[:, :], h[:, :], ACT.Identity, scale=c_("hop", HOPS)).then_inc(y_hi_ok.sem, 1)
                    if i == 3:
                        act.activation(g_hi[:, :], h[:, :], ACT.Copy).then_inc(h3_hi_ok.sem, 1)

            def p_adj(b, k):
                act.wait_ge(*adj_got[k % 2].at(b, 16 * (k // 2 + 1)))
                if k == 0:
                    act.wait_ge(*prod_done.at(b, 0))
                    act.wait_ge(w_ok.sem, 1)
                act.activation(adj_hi[:, k, :], adj_in[:, k % 2, :], ACT.Copy).then_inc(adj_hi_ok.sem, 1)

            def p_h0t(b, t):
                if t == 1:
                    act.wait_ge(*h0_turned.at(b, 1))
                    act.activation(ta[:, :], flat(tr_p), ACT.Identity, scale=c_("eps")).then_inc(eh_ok.sem, 1)

            def p_agg(b, t):
                if t == 1:
                    act.wait_ge(*agg_ok.at(b, 2))
                    act.activation(y_hi[:, :], ta[:, :], ACT.Copy).then_inc(y_hi_ok.sem, 1)

            def p_z(b, f, c):
                act.wait_ge(*z_done.at(b, HC * f + c + 1))
                if c == 0 and f == 0:
                    act.wait_ge(*deg_summed.at(b, 1))
                    act.wait_ge(*y_lo_ok.at(b, Y_AGG))
                if f == 1:
                    act.wait_ge(*silu_ok.at(b, c + 1))
                act.activation(zb[:, c, :], tr_p[:, c % 2, :], ACT.Identity, bias=c_("b1", c)).then_inc(zb_ok.sem, 1)
                if c > 1:
                    act.wait_ge(*sq_added.at(b, (HC - 1) * f + c - 1))
                dst = sqsum[:, :] if c == 0 else sqt[:, :]
                act.activation(dst, tr_p[:, c % 2, :], ACT.Square, bias=c_("b1", c)).then_inc(sq_ok.sem, 1)

            def p_silu(b, f, t):
                if t in (0, 4):
                    for c in (t // 2, t // 2 + 1):
                        act.wait_ge(*u_ok.at(b, HC * f + c + 1))
                        if HC * f + c >= 2:
                            act.wait_ge(*s_lo_ok.at(b, HC * f + c - 1))
                        act.activation(th[:, c % 2, :], zb[:, c, :], ACT.Tanh).then_inc(th_ok.sem, 1)
                if t in (2, 6):
                    for c in ((t - 2) // 2, (t - 2) // 2 + 1):
                        act.wait_ge(*silu_ok.at(b, HC * f + c + 1))
                        if HC * f + c >= 2:
                            act.wait_ge(*w2_done.at(b, HC * f + c - 1))
                        act.activation(s_hi[:, c % 2, :], th[:, c % 2, :], ACT.Copy).then_inc(s_hi_ok.sem, 1)
                if t == 8:
                    act.wait_ge(*w2_done.at(b, HC * (f + 1)))
                    act.activation(ta[:, fs(f)], acc_p[:, 1, :], ACT.Identity, bias=c_("b2")).then_inc(y0_ok.sem, 1)

            def p_hop(b, h, t):
                if t < 2:
                    act.wait_ge(*prod_done.at(b, 2 * h + t + 1))
                    act.activation(ta[:, fs(t)], acc_p[:, t, :], ACT.Copy).then_inc(hop_copied.sem, 1)
                if t == 3 and h < HOPS:
                    act.wait_ge(*hop_ok.at(b, 2 * h))
                    act.activation(y_hi[:, :], tg[:, :], ACT.Copy).then_inc(y_hi_ok.sem, 1)
                if t == 4 and h == HOPS:
                    act.wait_ge(*yt_turned.at(b, 1))
                    act.activation(y_hi[:, :], flat(tr_p), ACT.Copy).then_inc(y_hi_ok.sem, 1)

            def p_out(b, t):
                if t == 1:
                    act.wait_ge(*l1_done.at(b, 1))
                    act.activation(tg[:, :], flat(acc_p), ACT.Identity, bias=c_("hop_b")).then_inc(l1_biased.sem, 1)

            def q_ht(b, n, t):
                if t == 1:
                    act.wait_ge(*ht_turned.at(b, n + 1))
                    act.activation(ht_hi[:, :], flat(tr_q), ACT.Copy).then_inc(ht_hi_ok.sem, 1)
                    if n == 0:
                        act.activation(ht32[:, :], flat(tr_q), ACT.Copy).then_inc(ht32_ok.sem, 1)

            def q_s(b, t):
                if t == 1:
                    act.wait_ge(*s_done.at(b, 1))
                    act.activation(tmp1[:, :], flat(acc_q), ACT.Square, bias=c_("bse")).then_inc(ss_ok.sem, 1)
                    act.activation(t1[:, :], flat(acc_q), ACT.Identity, bias=c_("bse")).then_inc(s_ok.sem, 1)
                    act.wait_ge(*ss_ok.at(b, 1))
                    act.activation(ss_hi[:, :], tmp1[:, :], ACT.Copy).then_inc(ss_hi_ok.sem, 1)
                if t == 5:
                    act.wait_ge(*r32_ok.at(b, 1))
                    act.activation(ker_r[:, :], tmp1[:, :], ACT.Copy).then_inc(r_hi_ok.sem, 1)
                    act.wait_ge(*l32_ok.at(b, 1))
                    act.activation(ker_l[:, :], tmp2[:, :], ACT.Copy).then_inc(l_hi_ok.sem, 1)

            def q_msg(b, t):
                if t == 2:
                    act.wait_ge(*msg_b.at(b, 1))
                    act.activation(g_hi[:, :], t1[:, :], ACT.Relu).then_inc(msg_hi_ok.sem, 1)

            def q_ker(b, s):
                if s < 2 * NB:
                    act.wait_ge(*dist_done.at(b, s + 1))
                    if s >= 3:
                        act.wait_ge(*a_lo_ok.at(b, s - 2))
                    act.activation(a_f[:, s % 3, :], tr_q[:, s % 2, :], ACT.Exp).then_inc(a_f_ok.sem, 1)
                u = s - 1
                if 0 <= u < 2 * NB:
                    act.wait_ge(*a_m_ok.at(b, u + 1))
                    if u >= 3:
                        act.wait_ge(*ker_done.at(b, u - 2))
                    act.activation(a_hi[:, u % 3, :], a_f[:, u % 3, :], ACT.Copy).then_inc(a_hi_ok.sem, 1)

            def q_nmp(b, t):
                if t == 0:
                    act.wait_ge(*ker_done.at(b, 2 * NB))
                    act.activation(nmp_hi[:, :], flat(acc_q), ACT.Copy).then_inc(nmp_hi_ok.sem, 1)

            def q_conv1(b, t):
                if t == 1:
                    act.wait_ge(*c1_done.at(b, 1))
                    act.activation(t1[:, :], flat(tr_q), ACT.Relu, bias=x_(X_B1), scale=x_(X_SC1)).then_inc(c1_f_ok.sem, 1)
                    act.wait_ge(*c1_f_ok.at(b, 1))
                    act.activation(c1_hi[:, PAD:PAD + N], t1[:, :], ACT.Copy).then_inc(c1_hi_ok.sem, 1)

            def q_xc(b, f, t):
                if t == 1:
                    act.wait_ge(*xc_sum.at(b, f + 1))
                    act.activation(t1[:, fs(f)], t1[:, fs(f)], ACT.Relu, bias=x_(X_B2)).then_inc(xc_ok.sem, 1)
                    act.wait_ge(*xc_ok.at(b, f + 1))
                    act.activation(g_hi[:, fs(f)], t1[:, fs(f)], ACT.Copy).then_inc(xc_hi_ok.sem, 1)

            def q_gru(b, f, t):
                if t == 1:
                    act.wait_ge(*gate_done.at(b, f + 1))
                    if f == 1:
                        act.wait_ge(*gru_ok.at(b, 1))
                    act.activation(gate[:, 0, :], tr_q[:, 0, :], ACT.Tanh, bias=x_(X_BR), scale=0.5)
                    act.activation(gate[:, 2, :], acc_q[:, 1, :], ACT.Identity, bias=x_(X_BHN), scale=0.5)
                    act.activation(gate[:, 1, :], tr_q[:, 1, :], ACT.Tanh, bias=x_(X_BZ), scale=0.5).then_inc(gate_th.sem, 1)
                if t == 3:
                    act.wait_ge(*gate_n_in.at(b, f + 1))
                    act.activation(gate[:, 2, :], gate[:, 2, :], ACT.Tanh, bias=c_("bih", 2)).then_inc(gate_n.sem, 1)

            def q_rep(b, t):
                if t == 1:
                    act.wait_ge(*rep_s_done.at(b, 1))
                    act.activation(urep[:, :], flat(tr_q), ACT.Copy).then_inc(rep_s_ok.sem, 1)
                    act.activation(s1rep[:, :], flat(acc_q), ACT.Copy).then_inc(rep_s_ok.sem, 1)

            def q_att(b, i, t):
                if t == 1:
                    act.wait_ge(*leaky_ok.at(b, i + 1))
                    act.activation(pre[:, i % 2, :], pre[:, i % 2, :], ACT.Exp).then_inc(alpha_ok.sem, 1)
                if t == 2:
                    act.wait_ge(*nmax_ok.at(b, i + 1))
                    act.activation(prow[i % 4][:, :], pre[:, i % 2, :], ACT.Exp, bias=nmax[:, i:i + 1],
                                   accum_out=psum3[:, i:i + 1]).then_inc(prow_ok.sem, 1)

            def q_edge(b, q, v):
                if v < 4:
                    n = 4 * q + v
                    act.wait_ge(*p_turned.at(b, n + 1))
                    if n >= 2:
                        act.wait_ge(*edge_done.at(b, n - 1))
                    act.activation(pt_hi[:, n % 2, :], tr_q[:, n % 2, :], ACT.Copy).then_inc(pt_hi_ok.sem, 1)
                if v == 4:
                    act.wait_ge(*edge_done.at(b, 4 * (q + 1)))
                    if q == 3:
                        act.wait_ge(*ot_turned.at(b, 1))
                    act.activation(ot[:, :], acc_q[:, q // 2, :], ACT.Copy).then_inc(ot_ok.sem, 1)

            walk(act, dict(p_ln=ln, p_adj=p_adj, p_h0t=p_h0t, p_agg=p_agg, p_z=p_z, p_silu=p_silu,
                           p_hop=p_hop, p_out=p_out, q_ln=ln, q_ht=q_ht, q_s=q_s,
                           q_msg=q_msg, q_ker=q_ker, q_nmp=q_nmp, q_conv1=q_conv1, q_xc=q_xc, q_gru=q_gru,
                           q_rep=q_rep, q_att=q_att, q_edge=q_edge))

        @block.vector
        def _(dve):
            steps_done = [0]

            def then(ins):
                steps_done[0] += 1
                ins.then_inc(set_ch.sem, 1)
                dve.wait_ge(set_ch.sem, steps_done[0])

            dve.wait_ge(setup_in.sem, 64)
            bn = {1: COLS["bn1"][0], 2: COLS["bn2"][0]}
            dve.tensor_scalar(colx[:, X_V:X_V + 1], col[:, bn[1] + 3:bn[1] + 4], BN_EPS, None, ALU.add)
            dve.tensor_scalar(colx[:, X_V + 1:X_V + 2], col[:, bn[2] + 3:bn[2] + 4], BN_EPS, None, ALU.add).then_inc(bn_v.sem, 1)
            dve.wait_ge(bn_r.sem, 1)
            for n, (sc, sh) in {1: (X_SC1, X_B1), 2: (X_SC2, X_B2)}.items():
                g = bn[n]
                then(dve.tensor_tensor(x_(sc), col[:, g:g + 1], colx[:, X_V + 1 + n:X_V + 2 + n], ALU.mult))
                then(dve.tensor_tensor(x_(sh), col[:, g + 2:g + 3], x_(sc), ALU.mult))
                then(dve.tensor_tensor(x_(sh), col[:, g + 1:g + 2], x_(sh), ALU.subtract))
            for g, at in ((0, X_BR), (1, X_BZ)):
                then(dve.tensor_tensor(x_(at), c_("bih", g), c_("bhh", g), ALU.add))
                then(dve.tensor_scalar(x_(at), x_(at), 0.5, None, ALU.mult))
            then(dve.tensor_scalar(x_(X_BHN), c_("bhh", 2), 0.5, None, ALU.mult))
            then(dve.tensor_scalar(colx[:, X_RMS:X_RMS + HC], col[:, COLS["rms"][0]:COLS["rms"][0] + HC], 0.5, None, ALU.mult))
            then(dve.memset(c1_hi[:, 0:PAD].bitcast(F32), 0.0))
            then(dve.memset(c1_hi[:, PAD + N:WIDE].bitcast(F32), 0.0))
            then(dve.memset(c1_lo[:, 0:PAD].bitcast(F32), 0.0))
            then(dve.memset(c1_lo[:, PAD + N:WIDE].bitcast(F32), 0.0))
            for n in range(2):
                then(dve.tensor_tensor_reduce(out=stage_v[:, 0, :], in0=stage_l3[:, n, :], in1=stage_l3[:, 2 + n, :],
                                              scale=1.0, scalar=0.0, op0=ALU.mult, op1=ALU.add,
                                              accum_out=colx[:, X_V + n:X_V + n + 1]))
                then(dve.tensor_scalar(stage_v[:, 1, :], ones, x_(X_V + n), None, ALU.mult))
                then(dve.tensor_copy(w_hi[:, NW_IN + n, :], stage_v[:, 1, :]))
                then(dve.tensor_tensor(w_lo[:, NW_IN + n, :], stage_v[:, 1, :], w_hi[:, NW_IN + n, :], ALU.subtract))
            dve.wait_ge(w_hi_ok.sem, 1)
            dve.tensor_tensor(w_lo[:, 0:NW_IN, :], stage_w[:, :, :], w_hi[:, 0:NW_IN, :], ALU.subtract).then_inc(w_ok.sem, 1)

            def ln(b, i, t):
                g, s = i // 2, LN[i]
                src, dst = (xp, hrow) if i < 2 else (xq, hq)
                if t == 0:
                    dve.wait_ge(*{0: x_in.at(b, 16), 1: x1_ok.at(b, 1), 2: x2_ok.at(b, 1), 3: x3_ok.at(b, 1)}[i])
                    for j in range(NB):
                        last = dve.bn_stats(stat[g][:, j, :], src[:, j, :])
                    last.then_inc(s["stats"].sem, 1)
                    dve.wait_ge(*s["stats"].at(b, 1))
                    dve.memset(carrier[:, 0:1], 0.0)
                    for j in range(NB):
                        last = dve.bn_aggr(mv[g][:, j, :], stat[g][:, j, :])
                    last.then_inc(s["mean"].sem, 1)
                    dve.wait_ge(*s["mean"].at(b, 1))
                    dve.tensor_scalar(ve[g][:, :], mv[g][:, :, 1], LN_EPS, None, ALU.add).then_inc(s["var"].sem, 1)
                if t == 1:
                    dve.wait_ge(*s["rstd"].at(b, 1))
                    for j in range(NB):
                        last = dve.tensor_scalar(dst[:, ks(j)], src[:, j, :], mv[g][:, j, 0:1], rstd[g][:, j:j + 1],
                                                 ALU.subtract, ALU.mult)
                    last.then_inc(s["scaled"].sem, 1)
                if t == 2 and i == 0:
                    dve.wait_ge(*y_hi_ok.at(b, Y_H0))
                    dve.tensor_tensor(y_lo[:, :], hrow[:, :], y_hi[:, :], ALU.subtract).then_inc(y_lo_ok.sem, 1)
                if t == 2 and i == 1:
                    dve.wait_ge(*y_hi_ok.at(b, Y_W3H))
                    dve.scalar_tensor_tensor(y_lo[:, :], hrow[:, :], c_("hop", HOPS), y_hi[:, :],
                                             ALU.mult, ALU.subtract).then_inc(y_lo_ok.sem, 1)
                if t == 2 and i == 3:
                    dve.wait_ge(*h3_hi_ok.at(b, 1))
                    dve.tensor_tensor(g_lo[:, :], hq[:, :], g_hi[:, :], ALU.subtract).then_inc(h3_lo_ok.sem, 1)

            def p_adj(b, k):
                dve.wait_ge(*adj_hi_ok.at(b, k + 1))
                dve.tensor_tensor(adj_lo[:, k, :], adj_in[:, k % 2, :], adj_hi[:, k, :], ALU.subtract).then_inc(adj_lo_ok.sem, 1)

            def p_deg(b):
                dve.wait_ge(*deg_summed.at(b, 1))
                dve.tensor_scalar(dg[:, 0, :], tr_p[:, 0, 0:NB], 1.0, None, ALU.mult).then_inc(deg_ch.sem, 1)
                dve.wait_ge(*deg_ch.at(b, 1))
                dve.tensor_scalar(dg[:, 1, :], dg[:, 0, :], DEG_EPS, None, ALU.add)
                dve.tensor_scalar(dg[:, 3, :], dg[:, 0, :], 0.0, None, ALU.is_gt).then_inc(deg_ch.sem, 1)
                dve.wait_ge(*deg_ch.at(b, 2))
                dve.reciprocal(dg[:, 2, :], dg[:, 1, :])
                dve.tensor_tensor(dg[:, 4, :], dg[:, 0, :], dg[:, 3, :], ALU.mult).then_inc(deg_ch.sem, 1)
                dve.wait_ge(*deg_ch.at(b, 3))
                dve.tensor_scalar(dg[:, 3, :], dg[:, 3, :], -1.0, 1.0, ALU.mult, ALU.add).then_inc(deg_ch.sem, 1)
                dve.wait_ge(*deg_ch.at(b, 4))
                dve.tensor_tensor(dg[:, 4, :], dg[:, 4, :], dg[:, 3, :], ALU.add).then_inc(deg_ch.sem, 1)
                dve.wait_ge(*deg_ch.at(b, 5))
                dve.reciprocal(dg[:, 5, :], dg[:, 4, :]).then_inc(deg_ch.sem, 1)

            def p_agg(b, t):
                if t == 0:
                    dve.wait_ge(*eh_ok.at(b, 1))
                    for f in range(2):
                        dve.wait_ge(*prod_done.at(b, f + 1))
                        dve.tensor_tensor(ta[:, fs(f)], acc_p[:, f, :], ta[:, fs(f)], ALU.add).then_inc(agg_ok.sem, 1)
                if t == 2:
                    dve.wait_ge(*y_hi_ok.at(b, Y_AGG))
                    dve.tensor_tensor(y_lo[:, :], ta[:, :], y_hi[:, :], ALU.subtract).then_inc(y_lo_ok.sem, 1)

            def p_rms(b, f, t):
                if t == 0:
                    dve.wait_ge(*ms_done.at(b, f + 1))
                    dve.tensor_scalar(ve4[:, :], tr_p[:, 0, 0:HB], 1.0 / H, RMS_EPS, ALU.mult, ALU.add).then_inc(ms_read.sem, 1)
                if t == 1:
                    dve.wait_ge(*r4_ok.at(b, f + 1))
                    shape = [P, HB, P]
                    dve.tensor_tensor(sqsum[:, :].rearrange("p (j c) -> p j c", c=P), const[:, C_ID:C_ID + 1, :].to_broadcast(shape),
                                      r4[:, :].unsqueeze(2).to_broadcast(shape), ALU.mult).then_inc(diag_ok.sem, 1)
                if t == 2:
                    dve.wait_ge(*rep_done.at(b, f + 1))
                    dve.wait_ge(*zb_ok.at(b, HC * (f + 1)))
                    for c in range(HC):
                        dve.scalar_tensor_tensor(zb[:, c, :], zb[:, c, :], x_(X_RMS + c), acc_p[:, 0, :],
                                                 ALU.mult, ALU.mult).then_inc(u_ok.sem, 1)

            def p_silu(b, f, t):
                if t in (1, 5):
                    for c in ((t - 1) // 2, (t - 1) // 2 + 1):
                        dve.wait_ge(*th_ok.at(b, HC * f + c + 1))
                        dve.scalar_tensor_tensor(th[:, c % 2, :], th[:, c % 2, :], 1.0, zb[:, c, :],
                                                 ALU.add, ALU.mult).then_inc(silu_ok.sem, 1)
                if t in (3, 7):
                    for c in ((t - 3) // 2, (t - 3) // 2 + 1):
                        dve.wait_ge(*s_hi_ok.at(b, HC * f + c + 1))
                        dve.tensor_tensor(s_lo[:, c % 2, :], th[:, c % 2, :], s_hi[:, c % 2, :], ALU.subtract).then_inc(s_lo_ok.sem, 1)

            def p_x1(b, t):
                if t == 1:
                    dve.wait_ge(*y0_turned.at(b, 1))
                    dve.tensor_tensor(xp[:, :, :], xp[:, :, :], blocks(tr_p), ALU.add).then_inc(x1_ok.sem, 1)

            def p_hop(b, h, t):
                if t == 2:
                    for f in range(2):
                        n = 2 * (h - 1) + f + 1
                        dve.wait_ge(*hop_turned.at(b, n))
                        shape = [P, HB, P]
                        dve.tensor_tensor(tg[:, fs(f)].rearrange("p (j c) -> p j c", c=P),
                                          tr_p[:, f, :].rearrange("p (j c) -> p j c", c=P),
                                          dg[:, 2, f * HB:(f + 1) * HB].unsqueeze(2).to_broadcast(shape), ALU.mult).then_inc(hop_scaled.sem, 1)
                    for f in range(2):
                        n = 2 * (h - 1) + f + 1
                        dve.wait_ge(*hop_scaled.at(b, n))
                        dve.scalar_tensor_tensor(tg[:, fs(f)], hrow[:, fs(f)], c_("hop", HOPS - h), tg[:, fs(f)],
                                                 ALU.mult, ALU.add).then_inc(hop_ok.sem, 1)
                if t == 4 and h < HOPS:
                    dve.wait_ge(*y_hi_ok.at(b, Y_W3H + h))
                    dve.tensor_tensor(y_lo[:, :], tg[:, :], y_hi[:, :], ALU.subtract).then_inc(y_lo_ok.sem, 1)
                if t == 5 and h == HOPS:
                    dve.wait_ge(*y_hi_ok.at(b, Y_T))
                    dve.tensor_tensor(y_lo[:, :], flat(tr_p), y_hi[:, :], ALU.subtract).then_inc(y_lo_ok.sem, 1)

            def p_out(b, t):
                if t == 2:
                    dve.wait_ge(*l1_biased.at(b, 1))
                    dve.scalar_tensor_tensor(tg[:, :], tg[:, :], 0.2, tg[:, :], ALU.mult, ALU.max).then_inc(l1_leaky.sem, 1)
                if t == 3:
                    dve.wait_ge(*deg_ch.at(b, 6))
                    dve.wait_ge(*out_sent.at(b, 0))
                    dve.tensor_copy(rdeg[:, :], dg[:, 5, :]).then_inc(rdeg_ok.sem, 1)
                    dve.wait_ge(*l1_leaky.at(b, 1))
                    dve.tensor_tensor(xq[:, :, :], xp[:, :, :], blocks(tg), ALU.add).then_inc(x2_ok.sem, 1)

            def q_ht(b, n, t):
                if t == 2:
                    dve.wait_ge(*ht_hi_ok.at(b, n + 1))
                    if n == 0:
                        dve.wait_ge(*ht32_ok.at(b, 1))
                    dve.tensor_tensor(ht_lo[:, :], ht32[:, :] if n == 0 else flat(tr_q), ht_hi[:, :], ALU.subtract).then_inc(ht_lo_ok.sem, 1)

            def q_s(b, t):
                if t == 2:
                    dve.wait_ge(*ss_hi_ok.at(b, 1))
                    dve.tensor_tensor(ss_lo[:, :], tmp1[:, :], ss_hi[:, :], ALU.subtract).then_inc(ss_lo_ok.sem, 1)
                if t == 4:
                    dve.wait_ge(*rl_done.at(b, 1))
                    dve.wait_ge(*ss_lo_ok.at(b, 1))
                    dve.tensor_tensor(tmp1[:, :], t1[:, :], flat(tr_q), ALU.add).then_inc(r32_ok.sem, 1)
                    dve.scalar_tensor_tensor(tmp2[:, :], t1[:, :], 2.0, flat(acc_q), ALU.mult, ALU.add).then_inc(l32_ok.sem, 1)
                if t == 6:
                    dve.wait_ge(*r_hi_ok.at(b, 1))
                    for a in (32, 96):
                        dve.tensor_tensor(ker_r[a:a + 32, :], tmp1[a:a + 32, :], ker_r[a:a + 32, :], ALU.subtract)
                    dve.wait_ge(*l_hi_ok.at(b, 1))
                    dve.tensor_tensor(ker_l[64:128, :], tmp2[64:128, :], ker_l[64:128, :], ALU.subtract).then_inc(rl_ok.sem, 1)

            def q_msg(b, t):
                if t == 1:
                    dve.wait_ge(*msg_done.at(b, 1))
                    dve.tensor_tensor(blocks(t1), blocks(acc_q), const[:, C_MSG:C_MSG + 1, :].to_broadcast([P, NB, P]),
                                      ALU.add).then_inc(msg_b.sem, 1)
                if t == 3:
                    dve.wait_ge(*msg_hi_ok.at(b, 1))
                    dve.scalar_tensor_tensor(g_lo[:, :], t1[:, :], 0.0, g_hi[:, :], ALU.max, ALU.subtract).then_inc(msg_lo_ok.sem, 1)

            def q_ker(b, s):
                if s < 2 * NB:
                    m = s // 2
                    if s % 2 == 0:
                        dve.wait_ge(*row_got[m % 2].at(b, 16 * (m // 2 + 1)))
                    dve.wait_ge(*a_f_ok.at(b, s + 1))
                    dve.tensor_tensor(a_f[:, s % 3, :], a_f[:, s % 3, :], row_in[:, m % 2, fs(s % 2)], ALU.mult).then_inc(a_m_ok.sem, 1)
                u = s - 1
                if 0 <= u < 2 * NB:
                    dve.wait_ge(*a_hi_ok.at(b, u + 1))
                    dve.tensor_tensor(a_lo[:, u % 3, :], a_f[:, u % 3, :], a_hi[:, u % 3, :], ALU.subtract).then_inc(a_lo_ok.sem, 1)

            def q_nmp(b, t):
                if t == 1:
                    dve.wait_ge(*nmp_hi_ok.at(b, 1))
                    dve.tensor_tensor(nmp_lo[:, :], flat(acc_q), nmp_hi[:, :], ALU.subtract).then_inc(nmp_lo_ok.sem, 1)

            def q_conv1(b, t):
                if t == 2:
                    dve.wait_ge(*c1_hi_ok.at(b, 1))
                    dve.tensor_tensor(c1_lo[:, PAD:PAD + N], t1[:, :], c1_hi[:, PAD:PAD + N], ALU.subtract).then_inc(c1_lo_ok.sem, 1)

            def q_xc(b, f, t):
                if t == 0:
                    if f == 0:
                        dve.wait_ge(*c1_lo_ok.at(b, 1))
                    dve.wait_ge(*c2_done.at(b, f + 1))
                    dve.scalar_tensor_tensor(t1[:, fs(f)], acc_q[:, f, :], x_(X_SC2), ht32[:, fs(f)],
                                             ALU.mult, ALU.add).then_inc(xc_sum.sem, 1)
                if t == 2:
                    dve.wait_ge(*xc_hi_ok.at(b, f + 1))
                    dve.tensor_tensor(g_lo[:, fs(f)], t1[:, fs(f)], g_hi[:, fs(f)], ALU.subtract).then_inc(xc_lo_ok.sem, 1)

            def q_gru(b, f, t):
                if t == 2:
                    dve.wait_ge(*gate_th.at(b, f + 1))
                    dve.scalar_tensor_tensor(gate[:, 2, :], gate[:, 0, :], 1.0, gate[:, 2, :], ALU.add, ALU.mult).then_inc(gate_r.sem, 1)
                    dve.wait_ge(*gate_r.at(b, f + 1))
                    dve.tensor_tensor(gate[:, 2, :], acc_q[:, 0, :], gate[:, 2, :], ALU.add).then_inc(gate_n_in.sem, 1)
                if t == 4:
                    dve.wait_ge(*gate_d.at(b, f + 1))
                    dve.scalar_tensor_tensor(gate[:, 1, :], gate[:, 1, :], 1.0, gate[:, 0, :], ALU.add, ALU.mult).then_inc(gate_zd.sem, 1)
                    dve.wait_ge(*gate_zd.at(b, f + 1))
                    dve.scalar_tensor_tensor(t1[:, fs(f)], gate[:, 1, :], 0.5, gate[:, 2, :], ALU.mult, ALU.add).then_inc(gru_ok.sem, 1)

            def q_x3(b, t):
                if t == 1:
                    dve.wait_ge(*gru_turned.at(b, 1))
                    dve.tensor_tensor(xq[:, :, :], xq[:, :, :], blocks(tr_q), ALU.add).then_inc(x3_ok.sem, 1)

            def q_att(b, i, t):
                s = i % 2
                if t == 0:
                    dve.wait_ge(*row_got[s].at(b, 16 * (NB // 2 + i // 2 + 1)))
                    if i == 0:
                        dve.wait_ge(*rep_s_ok.at(b, 2))
                        dve.wait_ge(*rdeg_ok.at(b, 1))
                    if i >= 2:
                        dve.wait_ge(*prow_ok.at(b, i - 1))
                    dve.tensor_tensor_reduce(out=pre[:, s, :], in0=row_in[:, s, :], in1=urep[:, :], scale=1.0, scalar=0.0,
                                             op0=ALU.mult, op1=ALU.add, accum_out=s2raw[:, i:i + 1]).then_inc(s2_raw_ok.sem, 1)
                    dve.wait_ge(*s2_raw_ok.at(b, i + 1))
                    dve.tensor_tensor(s2[:, i:i + 1], s2raw[:, i:i + 1], rdeg[:, i:i + 1], ALU.mult).then_inc(s2_ok.sem, 1)
                if t == 1:
                    if i >= 4:
                        dve.wait_ge(*p_turned.at(b, 4 * (i // 2 - 1)))
                    elif i == 0:
                        dve.wait_ge(*gate_done.at(b, 2))
                    dve.tensor_scalar(prow[i % 4][:, :], row_in[:, s, :], 0.0, NEG_INF, ALU.is_le, ALU.mult)
                    dve.wait_ge(*s2_ok.at(b, i + 1))
                    dve.scalar_tensor_tensor(pre[:, s, :], s1rep[:, :], s2[:, i:i + 1], row_in[:, s, :],
                                             ALU.add, ALU.mult).then_inc(mask_ok.sem, 1)
                    dve.wait_ge(*mask_ok.at(b, i + 1))
                    dve.scalar_tensor_tensor(pre[:, s, :], pre[:, s, :], 0.2, pre[:, s, :], ALU.mult, ALU.max).then_inc(leaky_ok.sem, 1)
                if t == 2:
                    dve.wait_ge(*alpha_ok.at(b, i + 1))
                    dve.memset(carrier[:, 1:2], 0.0)
                    dve.tensor_tensor_reduce(out=pre[:, s, :], in0=pre[:, s, :], in1=prow[i % 4][:, :], scale=1.0,
                                             scalar=-3e38, op0=ALU.add, op1=ALU.max, accum_out=amax[:, i:i + 1]).then_inc(att_ok.sem, 1)
                    dve.wait_ge(*att_ok.at(b, i + 1))
                    dve.tensor_scalar(nmax[:, i:i + 1], amax[:, i:i + 1], -1.0, None, ALU.mult).then_inc(nmax_ok.sem, 1)

            def q_edge(b, q, v):
                f = q // 2
                if v < 4:
                    n = 4 * q + v
                    dve.wait_ge(*pt_hi_ok.at(b, n + 1))
                    dve.tensor_tensor(pt_lo[:, n % 2, :], tr_q[:, n % 2, :], pt_hi[:, n % 2, :], ALU.subtract).then_inc(pt_lo_ok.sem, 1)
                if v == 4:
                    dve.wait_ge(*prow_ok.at(b, HB * (f + 1)))
                    dve.reciprocal(rinv[:, f * HB:(f + 1) * HB], psum3[:, f * HB:(f + 1) * HB]).then_inc(rinv_ok.sem, 1)
                if v == 5:
                    dve.wait_ge(*rinv_ok.at(b, f + 1))
                    dve.wait_ge(*ot_turned.at(b, f + 1))
                    for j in range(HB):
                        n = f * HB + j
                        last = dve.scalar_tensor_tensor(xq[:, n, :], tr_q[:, 0, ks(j)], rinv[:, n:n + 1], xq[:, n, :], ALU.mult, ALU.add)
                    last.then_inc(out_ok.sem, 1)

            walk(dve, dict(p_ln=ln, p_adj=p_adj, p_deg=p_deg, p_agg=p_agg, p_rms=p_rms, p_silu=p_silu, p_x1=p_x1,
                           p_hop=p_hop, p_out=p_out, q_ln=ln, q_ht=q_ht, q_s=q_s, q_msg=q_msg,
                           q_ker=q_ker, q_nmp=q_nmp, q_conv1=q_conv1, q_xc=q_xc, q_gru=q_gru, q_x3=q_x3,
                           q_att=q_att, q_edge=q_edge))

        @block.tensor
        def _(pe):
            pe.wait_ge(setup_in.sem, 64)
            pe.wait_ge(w_ok.sem, 1)
            pe.wait_ge(set_act.sem, 1)

            def three(dst, l_hi, l_lo, r_hi, r_lo, first, last):
                pe.matmul(dst, l_lo, r_hi, start=first, stop=False)
                pe.matmul(dst, l_hi, r_lo, start=False, stop=False)
                return pe.matmul(dst, l_hi, r_hi, start=False, stop=last)

            def weight(dst, n, r_hi, r_lo, first=True, last=True):
                return three(dst, w_hi[:, n, :], w_lo[:, n, :], r_hi, r_lo, first, last)

            def turn(dst, src, n=NB):
                for j in range(n):
                    last = pe.transpose(dst[:, j // HB, ks(j % HB)], src[:, ks(j)], ident)
                return last

            def p_h0t(b, t):
                if t == 0:
                    pe.wait_ge(*LN[0]["h"].at(b, 1))
                    pe.wait_ge(*y_lo_ok.at(b, 0))
                    turn(tr_p, hrow).then_inc(h0_turned.sem, 1)

            def p_prod0(b, k):
                if k == 0:
                    pe.wait_ge(*y_lo_ok.at(b, Y_H0))
                    pe.wait_ge(*l1_biased.at(b, 0))
                pe.wait_ge(*adj_lo_ok.at(b, k + 1))
                for f in range(2):
                    last = three(acc_p[:, f, :], y_hi[:, ks(k)], y_lo[:, ks(k)], adj_hi[:, k, fs(f)], adj_lo[:, k, fs(f)],
                                 k == 0, k == NB - 1)
                    if k == NB - 1:
                        last.then_inc(prod_done.sem, 1)

            def p_deg(b):
                pe.wait_ge(*deg_added.at(b, NB))
                pe.wait_ge(*eh_ok.at(b, 1))
                for j in range(NB):
                    last = pe.matmul(tr_p[:, 0, j:j + 1], dacc[:, ks(j)], const[:, C_ONE, 0:1], start=True, stop=True)
                last.then_inc(deg_summed.sem, 1)

            def p_prod(b, h, f):
                if f == 0:
                    pe.wait_ge(*y_lo_ok.at(b, Y_W3H + h - 1))
                if h == 1:
                    pe.wait_ge(*(u_ok.at(b, 2 * HC) if f == 0 else y0_ok.at(b, 2)))
                if h > 1:
                    pe.wait_ge(*hop_copied.at(b, 2 * (h - 2) + f + 1))
                for k in range(NB):
                    last = three(acc_p[:, f, :], y_hi[:, ks(k)], y_lo[:, ks(k)], adj_hi[:, k, fs(f)], adj_lo[:, k, fs(f)],
                                 k == 0, k == NB - 1)
                last.then_inc(prod_done.sem, 1)

            def p_z(b, f, c):
                if c == 0 and f == 0:
                    pe.wait_ge(*y_lo_ok.at(b, Y_AGG))
                    pe.wait_ge(*deg_ch.at(b, 1))
                if c == 0 and f == 1:
                    pe.wait_ge(*ms_read.at(b, 1))
                if HC * f + c >= 2:
                    pe.wait_ge(*sq_ok.at(b, HC * f + c - 1))
                weight(tr_p[:, c % 2, :], W_MLP1 + c, y_hi[:, fs(f)], y_lo[:, fs(f)]).then_inc(z_done.sem, 1)

            def p_rms(b, f, t):
                if t == 0:
                    pe.wait_ge(*sq_added.at(b, (HC - 1) * (f + 1)))
                    for j in range(HB):
                        last = pe.matmul(tr_p[:, 0, j:j + 1], sqsum[:, ks(j)], const[:, C_ONE, 0:1], start=True, stop=True)
                    last.then_inc(ms_done.sem, 1)
                if t == 1:
                    pe.wait_ge(*diag_ok.at(b, f + 1))
                    pe.wait_ge(*(agg_ok.at(b, 2) if f == 0 else u_ok.at(b, HC)))
                    pe.matmul(acc_p[:, 0, :], ones, sqsum[:, :], start=True, stop=True).then_inc(rep_done.sem, 1)

            def p_silu(b, f, t):
                if t in (3, 7):
                    for c in ((t - 3) // 2, (t - 3) // 2 + 1):
                        if f == 1 and c == 0:
                            pe.wait_ge(*y0_ok.at(b, 1))
                        pe.wait_ge(*s_lo_ok.at(b, HC * f + c + 1))
                        weight(acc_p[:, 1, :], W_MLP2 + c, s_hi[:, c % 2, :], s_lo[:, c % 2, :], c == 0, c == HC - 1).then_inc(w2_done.sem, 1)

            def p_x1(b, t):
                if t == 0:
                    pe.wait_ge(*y0_ok.at(b, 2))
                    pe.wait_ge(*ms_read.at(b, 2))
                    turn(tr_p, ta).then_inc(y0_turned.sem, 1)

            def p_hop(b, h, t):
                if t in (1, 2):
                    f = t - 1
                    pe.wait_ge(*hop_copied.at(b, 2 * (h - 1) + f + 1))
                    if h == 1:
                        pe.wait_ge(*x1_ok.at(b, 1))
                    for j in range(HB):
                        last = pe.transpose(tr_p[:, f, ks(j)], ta[:, ks(f * HB + j)], ident)
                    last.then_inc(hop_turned.sem, 1)
                if t == 3 and h == HOPS:
                    pe.wait_ge(*hop_ok.at(b, 2 * HOPS))
                    turn(tr_p, tg).then_inc(yt_turned.sem, 1)

            def p_out(b, t):
                if t == 0:
                    pe.wait_ge(*y_lo_ok.at(b, Y_T))
                    pe.wait_ge(*hop_copied.at(b, 2 * HOPS))
                    for j in range(NB):
                        last = three(acc_p[:, j // HB, ks(j % HB)], y_hi[:, ks(j)], y_lo[:, ks(j)],
                                     w_hi[:, W_HOP, :], w_lo[:, W_HOP, :], True, True)
                    last.then_inc(l1_done.sem, 1)

            def q_ht(b, n, t):
                if t == 0:
                    pe.wait_ge(*LN[2 + n]["h"].at(b, 1))
                    if n == 1:
                        pe.wait_ge(*x3_ok.at(b, 1))
                    turn(tr_q, hq).then_inc(ht_turned.sem, 1)

            def q_s(b, t):
                if t == 0:
                    pe.wait_ge(*ht_lo_ok.at(b, 1))
                    for f in range(2):
                        last = weight(acc_q[:, f, :], W_SE, ht_hi[:, fs(f)], ht_lo[:, fs(f)])
                    last.then_inc(s_done.sem, 1)
                if t == 3:
                    pe.wait_ge(*ht32_ok.at(b, 1))
                    pe.wait_ge(*ss_lo_ok.at(b, 1))
                    pe.wait_ge(*s_ok.at(b, 1))
                    for n, dst in ((1, tr_q), (0, acc_q)):
                        for f in range(2):
                            pe.matmul(dst[:, f, :], pat[:, n, :], ss_lo[:, fs(f)], start=True, stop=False)
                            last = pe.matmul(dst[:, f, :], pat[:, n, :], ss_hi[:, fs(f)], start=False, stop=True)
                    last.then_inc(rl_done.sem, 1)

            def q_msg(b, t):
                if t == 0:
                    pe.wait_ge(*l32_ok.at(b, 1))
                    for j in range(NB):
                        last = three(acc_q[:, j // HB, ks(j % HB)], ht_hi[:, ks(j)], ht_lo[:, ks(j)],
                                     w_hi[:, W_MSG, :], w_lo[:, W_MSG, :], True, True)
                    last.then_inc(msg_done.sem, 1)

            def q_ker(b, s):
                if s < 2 * NB:
                    if s == 0:
                        pe.wait_ge(*rl_ok.at(b, 1))
                    if s >= 2:
                        pe.wait_ge(*a_f_ok.at(b, s - 1))
                    pe.matmul(tr_q[:, s % 2, :], ker_l[:, ks(s // 2)], ker_r[:, fs(s % 2)], start=True, stop=True).then_inc(dist_done.sem, 1)
                u = s - 2
                if u >= 0:
                    m, f = u // 2, u % 2
                    if u == 0:
                        pe.wait_ge(*msg_lo_ok.at(b, 1))
                    pe.wait_ge(*a_lo_ok.at(b, u + 1))
                    three(acc_q[:, f, :], g_hi[:, ks(m)], g_lo[:, ks(m)], a_hi[:, u % 3, :], a_lo[:, u % 3, :],
                          m == 0, m == NB - 1).then_inc(ker_done.sem, 1)

            def q_conv1(b, t):
                if t == 0:
                    pe.wait_ge(*a_f_ok.at(b, 2 * NB))
                    for f in range(2):
                        last = weight(tr_q[:, f, :], W_CONV1, ht_hi[:, fs(f)], ht_lo[:, fs(f)])
                    last.then_inc(c1_done.sem, 1)

            def q_conv2(b, f, part):
                if f == 0 and part == 0:
                    pe.wait_ge(*c1_lo_ok.at(b, 1))
                    pe.wait_ge(*nmp_lo_ok.at(b, 1))
                for t in TAP_PARTS[part]:
                    at = f * HALF + t
                    last = weight(acc_q[:, f, :], W_CONV2 + t, c1_hi[:, at:at + HALF], c1_lo[:, at:at + HALF], t == 0, t == TAPS - 1)
                if part == len(TAP_PARTS) - 1:
                    last.then_inc(c2_done.sem, 1)

            def q_gru(b, f, t):
                if t != 0:
                    return
                ht = ht_hi[:, fs(f)], ht_lo[:, fs(f)]
                nmp = nmp_hi[:, fs(f)], nmp_lo[:, fs(f)]
                xc = g_hi[:, fs(f)], g_lo[:, fs(f)]
                if f == 1:
                    pe.wait_ge(*gate_th.at(b, 1))
                for g in range(2):
                    weight(tr_q[:, g, :], W_HH + g, *ht, True, False)
                    weight(tr_q[:, g, :], W_IH + 2 * g + 1, *nmp, False, False)
                pe.wait_ge(*(xc_lo_ok.at(b, 2) if f == 0 else gate_n_in.at(b, 1)))
                weight(acc_q[:, 1, :], W_HH + 2, *ht, True, True)
                weight(acc_q[:, 0, :], W_IH + 5, *nmp, True, False)
                weight(acc_q[:, 0, :], W_IH + 4, *xc, False, True)
                for g in range(2):
                    last = weight(tr_q[:, g, :], W_IH + 2 * g, *xc, False, True)
                last.then_inc(gate_done.sem, 1)

            def q_x3(b, t):
                if t == 0:
                    pe.wait_ge(*gru_ok.at(b, 2))
                    turn(tr_q, t1).then_inc(gru_turned.sem, 1)

            def q_rep(b, t):
                if t == 0:
                    pe.wait_ge(*ht_lo_ok.at(b, 2))
                    for dst, w in ((tr_q, W_S2), (acc_q, W_S1)):
                        for f in range(2):
                            last = weight(dst[:, f, :], w, ht_hi[:, fs(f)], ht_lo[:, fs(f)])
                    last.then_inc(rep_s_done.sem, 1)

            def q_edge(b, q, v):
                def turn_p(v):
                    n = 4 * q + v
                    if n >= 2:
                        pe.wait_ge(*pt_lo_ok.at(b, n - 1))
                    for m in range(2):
                        for r in range(2):
                            last = pe.transpose(tr_q[:, n % 2, ks(2 * m + r)], prow[(2 * q + r) % 4][:, ks(2 * v + m)], ident)
                    last.then_inc(p_turned.sem, 1)

                if v == 0:
                    pe.wait_ge(*prow_ok.at(b, 2 * (q + 1)))
                    if q == 0:
                        pe.wait_ge(*rep_s_ok.at(b, 2))
                        pe.wait_ge(*h3_lo_ok.at(b, 1))
                    if q == 2:
                        pe.wait_ge(*out_ok.at(b, 1))
                    turn_p(0)
                if v < 3:
                    turn_p(v + 1)
                if v < 4:
                    n = 4 * q + v
                    pe.wait_ge(*pt_lo_ok.at(b, n + 1))
                    cols_q = slice((q % 2) * 2 * P, (q % 2 + 1) * 2 * P)
                    for m in range(2):
                        half = slice(m * 2 * P, (m + 1) * 2 * P)
                        k = 2 * v + m
                        last = three(acc_q[:, q // 2, cols_q], g_hi[:, ks(k)], g_lo[:, ks(k)], pt_hi[:, n % 2, half], pt_lo[:, n % 2, half],
                                     k == 0, k == NB - 1)
                    last.then_inc(edge_done.sem, 1)
                if v == 4:
                    pe.wait_ge(*ot_ok.at(b, q // 2 + 1))
                    for j in range(HB):
                        last = pe.transpose(tr_q[:, 0, ks(j)], ot[:, ks(j)], ident)
                    last.then_inc(ot_turned.sem, 1)

            walk(pe, dict(p_h0t=p_h0t, p_prod0=p_prod0, p_deg=p_deg, p_prod=p_prod, p_z=p_z, p_rms=p_rms, p_silu=p_silu,
                          p_x1=p_x1, p_hop=p_hop, p_out=p_out, q_ht=q_ht, q_s=q_s, q_msg=q_msg, q_ker=q_ker,
                          q_conv1=q_conv1, q_conv2=q_conv2, q_gru=q_gru, q_x3=q_x3, q_rep=q_rep, q_edge=q_edge))


def kernel(**inputs):
    import numpy as np
    import concourse.bacc as bacc
    from concourse.bass_utils import run_bass_kernel_spmd

    a = {k: np.ascontiguousarray(v) for k, v in inputs.items()}
    f32 = np.float32

    mats = [a["L0_gnn_W1"][:, c * P:(c + 1) * P] for c in range(HC)]
    mats += [a["L0_gnn_W2"][c * P:(c + 1) * P, :] for c in range(HC)]
    mats += [a["L1_gnn_W"].T, a["L2_gnn_conv1_w"][:, :, 0].T]
    mats += [a["L2_gnn_conv2_w"][:, :, t].T for t in range(TAPS)]
    mats += [a["L2_gnn_w_msg"].T]
    se = np.zeros((D, P), f32)
    bse = np.zeros((P,), f32)
    for q in range(4):
        se[:, 32 * q:32 * q + 3] = a["L2_gnn_w_se"].T
        bse[32 * q:32 * q + 3] = a["L2_gnn_b_se"]
        bse[32 * q + 3] = 1.0
    mats += [se]
    mats += [a["L2_gnn_w_ih"][g * P:(g + 1) * P, h * P:(h + 1) * P].T for g in range(3) for h in range(2)]
    mats += [a["L2_gnn_w_hh"][g * P:(g + 1) * P, :].T for g in range(3)]
    wpack = np.stack(mats, axis=1).reshape(P, NW_IN * P)
    w3 = a["L3_gnn_w3"][:, 0]
    rep = [np.broadcast_to(w3[n * P:(n + 1) * P], (P, P)) for n in range(2)]
    l3pack = np.stack([a["L3_gnn_W1"], a["L3_gnn_W2"], *rep], axis=1).reshape(P, 4 * P)

    pat_l, pat_r = np.zeros((P, P), f32), np.zeros((P, P), f32)
    for q in range(4):
        pat_r[0:3, 32 * q + 3] = -1.0
        pat_r[3, 32 * q + 3] = -1.0
        pat_r[3, 32 * q + 4] = 1.0
        pat_l[0:3, 32 * q + 4] = -1.0
        pat_l[3, 32 * q + 3] = -1.0
    cpack = np.stack([np.eye(P, dtype=f32), np.ones((P, P), f32), pat_l, pat_r,
                      np.broadcast_to(a["L2_gnn_b_msg"], (P, P))], axis=1).reshape(P, 5 * P)
    columns = [a["L0_gnn_b1"].reshape(HC, P), a["L0_gnn_rms_weight"].reshape(HC, P), a["L0_gnn_b2"][None]]
    columns += [a[f"L2_gnn_bn{n}_{v}"][None] for n in (1, 2) for v in "gbmv"]
    columns += [a["L2_gnn_b_ih"].reshape(3, P), a["L2_gnn_b_hh"].reshape(3, P)]
    columns += [np.broadcast_to(a["L1_gnn_conv_w"][:, None], (HOPS + 1, P)),
                np.broadcast_to(a["L1_gnn_conv_b"][:, None], (1, P)),
                np.broadcast_to(a["L0_gnn_epsilon"].reshape(1, 1), (1, P)), bse[None]]
    cols = np.concatenate(columns, axis=0).T

    arrays = dict(x=a["x"], adj=a["adj"], adj_t=a["adj"].transpose(0, 2, 1), wpack=wpack, l3pack=l3pack,
                  cpack=cpack, cols=cols)
    arrays = {f"in_{k}": np.ascontiguousarray(v) for k, v in arrays.items()}
    nc = bacc.Bacc("TRN2", target_bir_lowering=False, num_devices=1, dynamic_dma_scratch_size=1024)
    args = [nc.dram_tensor(k, v.shape, F32, kind="ExternalInput").ap() for k, v in arrays.items()]
    out = nc.dram_tensor("out", (B, N, D), F32, kind="ExternalOutput").ap()
    build(nc, *args, out)
    r = run_bass_kernel_spmd(nc, [arrays], core_ids=[0])
    return r.results[0]["out"]
```

```python
from contextlib import ExitStack

import concourse.bass as bass
from concourse import mybir

ALU = mybir.AluOpType
ACT = mybir.ActivationFunctionType
F32 = mybir.dt.float32
F32R = mybir.dt.float32r
BF16 = mybir.dt.bfloat16

P = 128
B, N, D, H = 8, 1024, 128, 512
NB = N // P
HALF = N // 2
HB = NB // 2
HC = H // P
TAPS = 17
PAD = TAPS // 2
HOPS = 3
LN_EPS, RMS_EPS, DEG_EPS, BN_EPS = 1e-5, 1e-6, 1e-9, 1e-5
NEG_INF = -9e15

W_MLP1, W_MLP2, W_HOP, W_CONV1, W_CONV2 = 0, HC, 2 * HC, 2 * HC + 1, 2 * HC + 2
W_MSG = W_CONV2 + TAPS
W_SE = W_MSG + 1
W_IH = W_SE + 1
W_HH = W_IH + 6
NW_IN = W_HH + 3
W_S1, W_S2 = NW_IN, NW_IN + 1
NW = NW_IN + 2

COLS = dict(b1=(0, HC), rms=(4, HC), b2=(8, 1), bn1=(9, 4), bn2=(13, 4), bih=(17, 3), bhh=(20, 3),
            hop=(23, HOPS + 1), hop_b=(27, 1), eps=(28, 1), bse=(29, 1))
NCOL = 30
C_ID, C_ONE, C_PL, C_PR, C_MSG = range(5)


class Signal:

    def __init__(self, ctx, nc, name, per=1):
        self.sem, self.per = ctx.enter_context(nc.semaphore(name)), per

    def at(self, b, n):
        return self.sem, b * self.per + n


def order():
    p = [("p_load",)] + [("p_ln", 0, t) for t in range(3)] + [("p_h0t", t) for t in range(2)]
    for k in range(NB + 1):
        p += [("p_adj", k)] if k < NB else []
        p += [("p_prod0", k - 1)] if k > 0 else []
    p += [("p_deg",)] + [("p_agg", t) for t in range(3)]
    z = [[("p_z", f, c) for c in range(HC)] for f in range(2)]
    rms = [[("p_rms", f, t) for t in range(3)] for f in range(2)]
    silu = [[("p_silu", f, t) for t in range(9)] for f in range(2)]
    p += z[0] + rms[0] + silu[0][:3] + z[1][:2] + silu[0][3:6] + z[1][2:] + silu[0][6:] + rms[1] + silu[1]
    p += [("p_x1", t) for t in range(2)] + [("p_ln", 1, t) for t in range(3)]
    for h in range(1, HOPS + 1):
        p += [("p_prod", h, 0, k) for k in range(0, NB, 2)] + [("p_hop", h, 0)]
        p += [("p_prod", h, 1, k) for k in range(0, NB, 2)] + [("p_hop", h, t) for t in range(1, 6)]
    p += [("p_out", t) for t in range(3)]
    q = [("q_ln", 2, t) for t in range(2)] + [("q_ht", 0, t) for t in range(3)]
    q += [("q_s", 0, 0), ("q_s", 1, 0), ("q_conv1", 0, 0), ("q_s", 0, 1), ("q_s", 1, 1), ("q_s", 0, 2), ("q_s", 0, 3),
          ("q_s", 1, 2), ("q_conv1", 0, 1), ("q_s", 0, 4), ("q_conv1", 1, 0), ("q_s", 1, 3), ("q_s", 0, 5), ("q_s", 1, 4),
          ("q_conv1", 0, 2), ("q_conv1", 1, 1), ("q_s", 1, 5), ("q_s", 0, 6), ("q_s", 1, 6), ("q_msg", 0),
          ("q_conv1", 1, 2), ("q_conv2", 0, 0), ("q_msg", 1), ("q_conv2", 0, 1), ("q_msg", 2), ("q_msg", 3)]
    parts, n = len(TAP_PARTS), 2
    for u in range(2 * NB + 3):
        q += [("q_ker", u)]
        if n < parts:
            q += [("q_conv2", 0, n)]
        if n == parts:
            q += [("q_xc", 0, 0), ("q_xc", 0, 1)]
        if parts < n <= 2 * parts:
            q += [("q_conv2", 1, n - parts - 1)]
        n += 1
    q += [("q_nmp", 0), ("q_xc", 1, 0), ("q_nmp", 1), ("q_xc", 1, 1)] + [("q_xc", f, t) for f in range(2) for t in (2, 3)]
    q += [("q_gru", f, t) for f, t in ((0, 0), (0, 5), (0, 1), (0, 2), (1, 0), (0, 3), (1, 5), (1, 1), (1, 2), (0, 4), (1, 3), (1, 4))] + [("q_x3", t) for t in range(2)]
    q += [("q_ln", 3, t) for t in range(3)] + [("q_ht", 1, t) for t in range(3)] + [("q_rep", t) for t in range(2)]
    q += [("q_att", 0, 0), ("q_att", 0, 1), ("q_att", 1, 0)]
    for s in range(NB + 3):
        n, m = divmod(s - 3, 2)
        edge = [("q_edge", n, 2 * m), ("q_edge", n, 2 * m + 1)] if 0 <= n < NB // 2 else []
        q += [("q_edge", n - 1, 5)] if edge and m == 0 and n % 2 == 0 and n > 0 else []
        q += edge[:1]
        q += [("q_att", s, 2)] if s < NB else []
        q += edge[1:]
        q += [("q_att", s + 1, 1)] if s + 1 < NB else []
        q += [("q_att", s, 3)] if s < NB else []
        q += [("q_att", s + 2, 0)] if s + 2 < NB else []
        q += [("q_att", s - 1, 4)] if 0 <= s - 1 < NB else []
        q += [("q_edge", n, 4)] if edge and m == 1 and n % 2 == 1 else []
    q += [("q_edge", NB // 2 - 1, 5)]
    return p, q


TAP_PARTS = [range(t, min(t + 2, TAPS)) for t in range(0, TAPS, 2)]
P_STEPS, Q_STEPS = order()
P_LAST = [("p_out", 3)]


def beside(p, q, places):
    out, n = [], 0
    for m in range(len(q) + 1):
        while n < len(p) and places[n] <= m:
            out.append(p[n])
            n += 1
        out += q[m:m + 1]
    return out


PLACES = [
    0, 1, 2, 4, 4, 4, 6, 6, 9, 16, 18, 19, 20, 26, 28, 28, 30, 33, 34, 35, 38, 38, 38, 38, 40, 43, 46, 46, 49,
    51, 56, 58, 58, 63, 65, 65, 65, 70, 78, 78, 79, 79, 80, 82, 83, 85, 85, 86, 88, 90, 90, 90, 90, 90, 91,
    91, 92, 92, 96, 97, 98, 100, 104, 106, 108, 108, 110, 111, 111, 111, 111, 111, 114, 115, 117, 117, 118,
    122, 122, 122, 122, 123, 123, 123, 124, 124, 127, 129, 132, 132, 132, 132, 134, 134, 134, 136, 136, 138,
    138, 138, 141, 142, 143, 144, 144, 149, 154, 154]
assert len(PLACES) == len(P_STEPS)
BODY = beside(P_STEPS, Q_STEPS, PLACES) + P_LAST


def build(nc, x, adj, adj_t, wpack, l3pack, cpack, cols, out):
    ctx = ExitStack()
    with ctx:
        base = (nc.sbuf_base + 63) // 64 * 64
        top = [base]

        def room(nbytes):
            at = top[0]
            top[0] += (nbytes + 63) // 64 * 64
            return at

        def tile(name, shape, dt, at=None):
            n = 4 if dt in (F32, F32R) else 2
            for s in shape[1:]:
                n *= s
            return nc.alloc_sbuf_tensor_at(name, shape, dt, offset=room(n) if at is None else at)

        KB4 = 4 * N
        w_hi = tile("w_hi", [P, NW, P], F32R)
        w_lo = tile("w_lo", [P, NW, P], F32R)
        const = tile("const", [P, 5, P], F32)
        pat = tile("pat", [P, 2, P], F32R)
        col = tile("col", [P, NCOL], F32)
        colx = tile("colx", [P, 16], F32)
        halves = tile("halves", [P, NB], F32)
        adj_hi = tile("adj_hi", [P, NB, N], F32R)
        at_lo = room(NB * KB4)
        adj_lo = tile("adj_lo", [P, NB, N], F32R, at_lo)
        stage_w = tile("stage_w", [P, NW_IN, P], F32, at_lo)
        stage_l3 = tile("stage_l3", [P, 4, P], F32, at_lo + NW_IN * 512)
        stage_v = tile("stage_v", [P, 2, P], F32, at_lo + (NW_IN + 4) * 512)
        adj_in = tile("adj_in", [P, 2, N], F32)
        row_in = tile("row_in", [P, 2, N], F32)

        xp = tile("xp", [P, NB, D], F32)
        y_hi = tile("y_hi", [P, N], F32R)
        y_lo = tile("y_lo", [P, N], F32R)
        at = room(KB4)
        hrow = tile("hrow", [P, N], F32, at)
        th = tile("th", [P, 2, HALF], F32, at)
        at = room(KB4)
        ta = tile("ta", [P, N], F32, at)
        sqt = tile("sqt", [P, HALF], F32, at + 4 * HALF)
        at = room(HC * HALF * 4)
        zb = tile("zb", [P, HC, HALF], F32, at)
        dacc = tile("dacc", [P, N], F32, at)
        tg = tile("tg", [P, N], F32, at)
        sqsum = tile("sqsum", [P, HALF], F32)
        at = room(KB4)
        s_hi = tile("s_hi", [P, 2, HALF], F32R, at)
        s_lo = tile("s_lo", [P, 2, HALF], F32R)

        xq = tile("xq", [P, NB, D], F32)
        WIDE = N + 2 * PAD
        at = room(4 * WIDE)
        c1_hi = tile("c1_hi", [P, WIDE], F32R, at)
        s1rep = tile("s1rep", [P, N], F32, at + 4 * PAD)
        at = room(2 * KB4)
        ht_hi = tile("ht_hi", [P, N], F32R, at)
        ht_lo = tile("ht_lo", [P, N], F32R, at + KB4)
        pt_hi = tile("pt_hi", [P, 2, HALF], F32R, at)
        pt_lo = tile("pt_lo", [P, 2, HALF], F32R, at + KB4)
        ot = tile("ot", [P, HALF], F32, at + KB4)
        at = room(4 * KB4)
        ker_r = tile("ker_r", [P, N], F32R, at)
        ker_l = tile("ker_l", [P, N], F32R, at + KB4)
        at3 = at + 2 * KB4
        nmp_hi = tile("nmp_hi", [P, N], F32R, at3)
        nmp_lo = tile("nmp_lo", [P, N], F32R, at3 + KB4)
        ss_hi = tile("ss_hi", [P, N], F32R, at3)
        ss_lo = tile("ss_lo", [P, N], F32R, at3 + KB4)
        msg32 = tile("msg32", [P, N], F32, at3)
        SLOTS = 4
        a_hi = tile("a_hi", [P, SLOTS, HALF], F32R, at3)
        prow = [tile(f"prow{n}", [P, N], F32, at + n * KB4) for n in range(4)]
        g_hi = tile("g_hi", [P, N], F32R)
        at_g_lo = room(KB4)
        g_lo = tile("g_lo", [P, N], F32R, at_g_lo)
        c1_32 = tile("c1_32", [P, N], F32, at_g_lo)
        at = room(KB4)
        t1 = tile("t1", [P, N], F32, at)
        urep = tile("urep", [P, N], F32, at)
        at = room(2 * KB4)
        hq = tile("hq", [P, N], F32, at)
        tmp1 = tile("tmp1", [P, N], F32, at)
        tmp2 = tile("tmp2", [P, N], F32, at + KB4)
        a_f = tile("a_f", [P, SLOTS, HALF], F32, at)
        a_lo = tile("a_lo", [P, SLOTS, HALF], F32R, at)
        gate = [tile(f"gate{f}", [P, 3, HALF], F32, o) for f, o in enumerate((at, at3 - 2 * KB4))]
        pre = tile("pre", [P, 2, N], F32, at)
        at = room(4 * WIDE)
        c1_lo = tile("c1_lo", [P, WIDE], F32R, at)
        ht32 = tile("ht32", [P, N], F32, at + 4 * PAD)
        prod = tile("prod", [P, N], F32, at + 4 * PAD)
        last_half = tile("last_half", [P, HB, D], F32, at + 4 * PAD)

        stat = [tile(f"stat{s}", [P, NB, 6], F32) for s in "pq"]
        mv = [tile(f"mv{s}", [P, NB, 2], F32) for s in "pq"]
        ve = [tile(f"ve{s}", [P, NB], F32) for s in "pq"]
        rstd = [tile(f"rstd{s}", [P, NB], F32) for s in "pq"]
        ve4 = tile("ve4", [P, HB], F32)
        r4 = tile("r4", [P, HB], F32)
        dg = tile("dg", [P, 6, NB], F32)
        rdeg = tile("rdeg", [P, NB], F32)
        s2 = tile("s2", [P, NB], F32)
        amax = tile("amax", [P, NB], F32)
        nmax = tile("nmax", [P, NB], F32)
        psum3 = tile("psum3", [P, NB], F32)
        rinv = tile("rinv", [P, NB], F32)
        carrier = tile("carrier", [P, 2], F32)
        nc_left = nc.sbuf_usable_end - top[0]
        assert nc_left >= 0, nc_left

        ident, ones = const[:, C_ID, :], const[:, C_ONE, :]

        def psum(name):
            return ctx.enter_context(nc.psum_tensor(name, [P, 2, HALF], F32))

        acc_p, tr_p, acc_q, tr_q = psum("acc_p"), psum("tr_p"), psum("acc_q"), psum("tr_q")

        def flat(t):
            return t[:, :, :].rearrange("p f n -> p (f n)")

        def blocks(t):
            if len(t.shape) == 3:
                return t[:, :, :].rearrange("p f (j c) -> p (f j) c", c=P)
            return t[:, :].rearrange("p (j c) -> p j c", c=P)

        def c_(name, n=0):
            at = COLS[name][0] + n
            return col[:, at:at + 1]

        X_SC1, X_B1, X_SC2, X_B2, X_BR, X_BZ, X_BHN, X_RMS, X_V = 0, 1, 2, 3, 4, 5, 6, 8, 12

        def x_(n):
            return colx[:, n:n + 1]

        def fs(f):
            return slice(f * HALF, (f + 1) * HALF)

        def ks(k):
            return slice(k * P, (k + 1) * P)

        S = {}

        def sig(name, per=1):
            S[name] = Signal(ctx, nc, name, per)
            return S[name]

        setup_in = sig("setup_in"); w_hi_ok = sig("w_hi_ok"); w_ok = sig("w_ok"); pool_const = sig("pool_const")
        bn_v = sig("bn_v"); bn_r = sig("bn_r"); set_ch = sig("set_ch"); set_act = sig("set_act")
        x_in = sig("x_in", 16)
        adj_got = [sig(f"adj_got{s}", 16 * NB // 2) for s in range(2)]
        row_got = [sig(f"row_got{s}", 16 * NB) for s in range(2)]
        out_sent = sig("out_sent", 16)
        half_free = sig("half_free", 16)
        LN = [dict(stats=sig(f"ln{i}_stats"), mean=sig(f"ln{i}_mean"), var=sig(f"ln{i}_var"),
                   rstd=sig(f"ln{i}_rstd"), scaled=sig(f"ln{i}_scaled"), h=sig(f"ln{i}_h")) for i in range(4)]
        adj_hi_ok = sig("adj_hi_ok", NB); adj_lo_ok = sig("adj_lo_ok", NB); deg_added = sig("deg_added", NB)
        Y_H0, Y_AGG, Y_W3H, Y_HOP1, Y_HOP2, Y_T = range(1, 7)
        y_hi_ok = sig("y_hi_ok", 6); y_lo_ok = sig("y_lo_ok", 6)
        h0_turned = sig("h0_turned"); eh_ok = sig("eh_ok"); deg_summed = sig("deg_summed"); deg_ok = sig("deg_ok")
        deg_ch = sig("deg_ch", 6)
        prod_done = sig("prod_done", 2 * (HOPS + 1)); agg_ok = sig("agg_ok", 2)
        z_done = sig("z_done", 2 * HC); zb_ok = sig("zb_ok", 2 * HC); sq_ok = sig("sq_ok", 2 * HC)
        sq_added = sig("sq_added", 2 * (HC - 1))
        ms_done = sig("ms_done", 2); ms_read = sig("ms_read", 2); r4_ok = sig("r4_ok", 2); diag_ok = sig("diag_ok", 2)
        rep_done = sig("rep_done", 2); u_ok = sig("u_ok", 2 * HC); th_ok = sig("th_ok", 2 * HC)
        silu_ok = sig("silu_ok", 2 * HC); s_hi_ok = sig("s_hi_ok", 2 * HC); s_lo_ok = sig("s_lo_ok", 2 * HC)
        w2_done = sig("w2_done", 2 * HC); y0_ok = sig("y0_ok", 2)
        y0_turned = sig("y0_turned"); x1_ok = sig("x1_ok")
        hop_copied = sig("hop_copied", 2 * HOPS); hop_turned = sig("hop_turned", 2 * HOPS)
        hop_scaled = sig("hop_scaled", 2 * HOPS); hop_ok = sig("hop_ok", 2 * HOPS)
        yt_turned = sig("yt_turned"); l1_done = sig("l1_done"); l1_biased = sig("l1_biased"); l1_leaky = sig("l1_leaky")
        rdeg_ok = sig("rdeg_ok"); x2_ok = sig("x2_ok")
        ht_turned = sig("ht_turned", 2); ht32_ok = sig("ht32_ok"); ht_hi_ok = sig("ht_hi_ok", 2); ht_lo_ok = sig("ht_lo_ok", 2)
        s_done = sig("s_done", 2); s_ok = sig("s_ok", 2); ss_ok = sig("ss_ok", 2); ss_hi_ok = sig("ss_hi_ok", 2); ss_lo_ok = sig("ss_lo_ok", 2)
        rl_done = sig("rl_done", 2); r32_ok = sig("r32_ok", 2); l32_ok = sig("l32_ok", 2); r_hi_ok = sig("r_hi_ok", 2); l_hi_ok = sig("l_hi_ok", 2)
        rl_ok = sig("rl_ok", 2)
        msg_done = sig("msg_done"); msg_b = sig("msg_b"); msg_hi_ok = sig("msg_hi_ok"); msg_lo_ok = sig("msg_lo_ok")
        dist_done = sig("dist_done", 2 * NB); a_f_ok = sig("a_f_ok", 2 * NB); a_m_ok = sig("a_m_ok", 2 * NB); a_hi_ok = sig("a_hi_ok", 2 * NB)
        a_lo_ok = sig("a_lo_ok", 2 * NB); ker_done = sig("ker_done", 2 * NB)
        nmp_hi_ok = sig("nmp_hi_ok"); nmp_lo_ok = sig("nmp_lo_ok")
        c1_done = sig("c1_done", 2); c1_f_ok = sig("c1_f_ok", 2); c1_hi_ok = sig("c1_hi_ok", 2); c1_lo_ok = sig("c1_lo_ok", 2)
        c2_done = sig("c2_done", 2); xc_part = sig("xc_part", 2); xc_sum = sig("xc_sum", 2); xc_ok = sig("xc_ok", 2); xc_hi_ok = sig("xc_hi_ok", 2); xc_lo_ok = sig("xc_lo_ok", 2)
        gate_done = sig("gate_done", 2); gate_th = sig("gate_th", 2); gate_r = sig("gate_r", 2); gate_n_in = sig("gate_n_in", 2)
        gate_n = sig("gate_n", 2); gate_d = sig("gate_d", 2); gate_zd = sig("gate_zd", 2); gru_ok = sig("gru_ok", 2)
        gru_turned = sig("gru_turned"); x3_ok = sig("x3_ok"); h3_hi_ok = sig("h3_hi_ok"); h3_lo_ok = sig("h3_lo_ok")
        rep_s_done = sig("rep_s_done"); rep_s_ok = sig("rep_s_ok", 2)
        s2_prod_ok = sig("s2_prod_ok", NB); s2_ok = sig("s2_ok", NB); pre_ok = sig("pre_ok", NB); leaky_ok = sig("leaky_ok", NB)
        alpha_ok = sig("alpha_ok", NB); mask_ok = sig("mask_ok", NB); att_ok = sig("att_ok", NB); nmax_ok = sig("nmax_ok", NB); prow_ok = sig("prow_ok", NB)
        p_turned = sig("p_turned", 2 * NB); pt_hi_ok = sig("pt_hi_ok", 2 * NB); pt_lo_ok = sig("pt_lo_ok", 2 * NB); edge_done = sig("edge_done", 2 * NB)
        ot_ok = sig("ot_ok", 2); ot_turned = sig("ot_turned", 2); rinv_ok = sig("rinv_ok", 2); out_ok = sig("out_ok", 2)

        block = ctx.enter_context(nc.Block())

        def walk(eng, steps):
            def go(names, bp, bq):
                for name, *args in names:
                    if name in steps:
                        steps[name](bp if name[0] == "p" else bq, *args)
            go(P_STEPS + P_LAST, 0, None)
            with eng.Fori(1, B) as i:
                go(BODY, i, i - 1)
            go(Q_STEPS, None, B - 1)

        @block.sync
        def _(sp):
            sp.dma_start(stage_w[:, :, :].rearrange("p a b -> p (a b)"), wpack).then_inc(setup_in.sem, 16)
            sp.dma_start(stage_l3[:, :, :].rearrange("p a b -> p (a b)"), l3pack).then_inc(setup_in.sem, 16)
            sp.dma_start(const[:, :, :].rearrange("p a b -> p (a b)"), cpack).then_inc(setup_in.sem, 16)
            sp.dma_start(col[:, :], cols).then_inc(setup_in.sem, 16)

            def p_load(b):
                sp.wait_ge(*x2_ok.at(b, 0))
                sp.dma_start(xp[:, :, :], x[b].rearrange("(j p) d -> p j d", p=P)).then_inc(x_in.sem, 16)

            def p_adj(b, k):
                sp.wait_ge(*adj_lo_ok.at(b, max(k - 1, 0)))
                sp.wait_ge(*deg_added.at(b, max(k - 1, 0)))
                sp.dma_start(adj_in[:, k % 2, :], adj_t[b, k * P:(k + 1) * P, :]).then_inc(adj_got[k % 2].sem, 16)

            def q_ker(b, u):
                if u % 2 == 1 or u >= 2 * NB:
                    return
                m = u // 2
                if m >= 2:
                    sp.wait_ge(*a_m_ok.at(b, 2 * (m - 1)))
                else:
                    sp.wait_ge(*x2_ok.at(b, 1))
                sp.dma_start(row_in[:, m % 2, :], adj_t[b, m * P:(m + 1) * P, :]).then_inc(row_got[m % 2].sem, 16)

            def q_att(b, i, t):
                if t != 0:
                    return
                if i >= 2:
                    sp.wait_ge(*mask_ok.at(b, i - 1))
                else:
                    sp.wait_ge(*a_m_ok.at(b, 2 * (NB - 1 + i)))
                sp.dma_start(row_in[:, i % 2, :], adj[b, i * P:(i + 1) * P, :]).then_inc(row_got[i % 2].sem, 16)

            def q_edge(b, q, v):
                if q % 2 == 1 and v == 5:
                    f = q // 2
                    src = (xq[:, 0:HB, :], last_half[:, :, :])[f]
                    sp.wait_ge(*out_ok.at(b, f + 1))
                    sp.dma_start(out[b, f * HALF:(f + 1) * HALF, :].rearrange("(j p) d -> p j d", p=P), src).then_inc((out_sent, half_free)[f].sem, 16)

            walk(sp, dict(p_load=p_load, p_adj=p_adj, q_ker=q_ker, q_att=q_att, q_edge=q_edge))
            sp.wait_ge(*out_sent.at(B, 0))
            sp.wait_ge(*half_free.at(B, 16))

        @block.gpsimd
        def _(pool):
            pool.memset(halves[:, :], -0.5).then_inc(pool_const.sem, 1)
            pool.wait_ge(pool_const.sem, 1)
            pool.wait_ge(bn_v.sem, 1)
            pool.tensor_tensor(colx[:, X_V + 2:X_V + 4], colx[:, X_V:X_V + 2], halves[:, 0:2], ALU.pow).then_inc(bn_r.sem, 1)

            def ln(b, i, t):
                if t == 2 and i == 3:
                    pool.wait_ge(*h3_hi_ok.at(b, 1))
                    pool.tensor_tensor(g_lo[:, :], hq[:, :], g_hi[:, :], ALU.subtract).then_inc(h3_lo_ok.sem, 1)
                if t != 0:
                    return
                g = i // 2
                pool.wait_ge(*LN[i]["var"].at(b, 1))
                pool.tensor_tensor(rstd[g][:, :], ve[g][:, :], halves[:, :], ALU.pow).then_inc(LN[i]["rstd"].sem, 1)

            def p_adj(b, k):
                pool.wait_ge(*adj_got[k % 2].at(b, 16 * (k // 2 + 1)))
                if k == 1:
                    pool.wait_ge(*x2_ok.at(b, 0))
                    pool.tensor_tensor(dacc[:, :], adj_in[:, 0, :], adj_in[:, 1, :], ALU.add).then_inc(deg_added.sem, 2)
                if k > 1:
                    pool.wait_ge(*deg_added.at(b, k))
                    pool.tensor_tensor(dacc[:, :], dacc[:, :], adj_in[:, k % 2, :], ALU.add).then_inc(deg_added.sem, 1)

            def p_z(b, f, c):
                if c > 0:
                    pool.wait_ge(*sq_ok.at(b, HC * f + c + 1))
                    pool.tensor_tensor(sqsum[:, :], sqsum[:, :], sqt[:, :], ALU.add).then_inc(sq_added.sem, 1)

            def p_rms(b, f, t):
                if t == 0:
                    pool.wait_ge(*ms_read.at(b, f + 1))
                    pool.tensor_tensor(r4[:, :], ve4[:, :], halves[:, 0:HB], ALU.pow).then_inc(r4_ok.sem, 1)

            def p_silu(b, f, t):
                if t in (3, 7):
                    for c in ((t - 3) // 2, (t - 3) // 2 + 1):
                        pool.wait_ge(*s_hi_ok.at(b, HC * f + c + 1))
                        pool.tensor_tensor(s_lo[:, c % 2, :], th[:, c % 2, :], s_hi[:, c % 2, :], ALU.subtract).then_inc(s_lo_ok.sem, 1)

            def q_conv1(b, f, t):
                if t == 2:
                    if f == 0:
                        pool.wait_ge(*half_free.at(b, 16))
                    pool.wait_ge(*c1_hi_ok.at(b, f + 1))
                    at = PAD + f * HALF
                    pool.tensor_tensor(c1_lo[:, at:at + HALF], c1_32[:, fs(f)], c1_hi[:, at:at + HALF], ALU.subtract).then_inc(c1_lo_ok.sem, 1)

            def q_ker(b, s):
                u = s - 1
                if 0 <= u < 2 * NB:
                    pool.wait_ge(*a_hi_ok.at(b, u + 1))
                    m = u % SLOTS
                    pool.tensor_tensor(a_lo[:, m, :], a_f[:, m, :], a_hi[:, m, :], ALU.subtract).then_inc(a_lo_ok.sem, 1)

            def q_att(b, i, t):
                if t != 0:
                    return
                s = i % 2
                pool.wait_ge(*row_got[s].at(b, 16 * (NB // 2 + i // 2 + 1)))
                if i == 0:
                    pool.wait_ge(*rep_s_ok.at(b, 1))
                if i == 0:
                    pool.wait_ge(*gru_ok.at(b, 2))
                else:
                    pool.wait_ge(*s2_ok.at(b, i))
                pool.tensor_tensor(prod[:, :], row_in[:, s, :], urep[:, :], ALU.mult).then_inc(s2_prod_ok.sem, 1)

            def q_xc(b, f, t):
                if f == 1 and t == 0:
                    pool.wait_ge(*c2_done.at(b, 2))
                    pool.tensor_tensor(ht32[:, :], ht_hi[:, :], ht_lo[:, :], ALU.add).then_inc(ht32_ok.sem, 1)

            def q_gru(b, f, t):
                if t != 3:
                    return
                pool.wait_ge(*ht32_ok.at(b, 1))
                pool.wait_ge(*gate_n.at(b, f + 1))
                pool.tensor_tensor(gate[f][:, 0, :], ht32[:, fs(f)], gate[f][:, 2, :], ALU.subtract).then_inc(gate_d.sem, 1)

            walk(pool, dict(p_ln=ln, q_ln=ln, p_adj=p_adj, p_z=p_z, p_rms=p_rms, p_silu=p_silu,
                            q_conv1=q_conv1, q_ker=q_ker, q_xc=q_xc, q_gru=q_gru, q_att=q_att))

        @block.scalar
        def _(act):
            act.wait_ge(setup_in.sem, 64)
            act.activation(w_hi[:, 0:NW_IN, :], stage_w[:, :, :], ACT.Copy).then_inc(w_hi_ok.sem, 1)
            act.activation(pat[:, :, :], const[:, C_PL:C_PR + 1, :], ACT.Copy).then_inc(set_act.sem, 1)

            def ln(b, i, t):
                h = hrow if i < 2 else hq
                if t == 1:
                    act.wait_ge(*LN[i]["scaled"].at(b, 1))
                    act.activation(h[:, :], h[:, :], ACT.Relu).then_inc(LN[i]["h"].sem, 1)
                    if i != 2:
                        act.wait_ge(*LN[i]["h"].at(b, 1))
                    if i == 0:
                        act.activation(y_hi[:, :], h[:, :], ACT.Copy).then_inc(y_hi_ok.sem, 1)
                    if i == 1:
                        act.activation(y_hi[:, :], h[:, :], ACT.Identity, scale=c_("hop", HOPS)).then_inc(y_hi_ok.sem, 1)
                    if i == 3:
                        act.activation(g_hi[:, :], h[:, :], ACT.Copy).then_inc(h3_hi_ok.sem, 1)

            def p_adj(b, k):
                act.wait_ge(*adj_got[k % 2].at(b, 16 * (k // 2 + 1)))
                if k == 0:
                    act.wait_ge(*prod_done.at(b, 0))
                    act.wait_ge(w_ok.sem, 1)
                act.activation(adj_hi[:, k, :], adj_in[:, k % 2, :], ACT.Copy).then_inc(adj_hi_ok.sem, 1)

            def p_h0t(b, t):
                if t == 1:
                    act.wait_ge(*h0_turned.at(b, 1))
                    act.activation(ta[:, :], flat(tr_p), ACT.Identity, scale=c_("eps")).then_inc(eh_ok.sem, 1)

            def p_agg(b, t):
                if t == 1:
                    act.wait_ge(*agg_ok.at(b, 2))
                    act.activation(y_hi[:, :], ta[:, :], ACT.Copy).then_inc(y_hi_ok.sem, 1)

            def p_z(b, f, c):
                act.wait_ge(*z_done.at(b, HC * f + c + 1))
                if c == 0 and f == 0:
                    act.wait_ge(*deg_summed.at(b, 1))
                    act.wait_ge(*y_lo_ok.at(b, Y_AGG))
                if f == 1:
                    act.wait_ge(*silu_ok.at(b, c + 1))
                act.activation(zb[:, c, :], tr_p[:, c % 2, :], ACT.Identity, bias=c_("b1", c)).then_inc(zb_ok.sem, 1)
                if c > 1:
                    act.wait_ge(*sq_added.at(b, (HC - 1) * f + c - 1))
                dst = sqsum[:, :] if c == 0 else sqt[:, :]
                act.activation(dst, tr_p[:, c % 2, :], ACT.Square, bias=c_("b1", c)).then_inc(sq_ok.sem, 1)

            def p_silu(b, f, t):
                if t in (0, 4):
                    for c in (t // 2, t // 2 + 1):
                        act.wait_ge(*u_ok.at(b, HC * f + c + 1))
                        if HC * f + c >= 2:
                            act.wait_ge(*s_lo_ok.at(b, HC * f + c - 1))
                        act.activation(th[:, c % 2, :], zb[:, c, :], ACT.Tanh).then_inc(th_ok.sem, 1)
                if t in (2, 6):
                    for c in ((t - 2) // 2, (t - 2) // 2 + 1):
                        act.wait_ge(*silu_ok.at(b, HC * f + c + 1))
                        if HC * f + c >= 2:
                            act.wait_ge(*w2_done.at(b, HC * f + c - 1))
                        act.activation(s_hi[:, c % 2, :], th[:, c % 2, :], ACT.Copy).then_inc(s_hi_ok.sem, 1)
                if t == 8:
                    act.wait_ge(*w2_done.at(b, HC * (f + 1)))
                    act.activation(ta[:, fs(f)], acc_p[:, 1, :], ACT.Identity, bias=c_("b2")).then_inc(y0_ok.sem, 1)

            def p_hop(b, h, t):
                if t < 2:
                    act.wait_ge(*prod_done.at(b, 2 * h + t + 1))
                    act.activation(ta[:, fs(t)], acc_p[:, t, :], ACT.Copy).then_inc(hop_copied.sem, 1)
                if t == 3 and h < HOPS:
                    act.wait_ge(*hop_ok.at(b, 2 * h))
                    act.activation(y_hi[:, :], tg[:, :], ACT.Copy).then_inc(y_hi_ok.sem, 1)
                if t == 4 and h == HOPS:
                    act.wait_ge(*yt_turned.at(b, 1))
                    act.activation(y_hi[:, :], flat(tr_p), ACT.Copy).then_inc(y_hi_ok.sem, 1)

            def p_out(b, t):
                if t == 1:
                    act.wait_ge(*l1_done.at(b, 1))
                    act.activation(tg[:, :], flat(acc_p), ACT.Identity, bias=c_("hop_b")).then_inc(l1_biased.sem, 1)

            def q_ht(b, n, t):
                if t == 1:
                    act.wait_ge(*ht_turned.at(b, n + 1))
                    act.activation(ht_hi[:, :], flat(tr_q), ACT.Copy).then_inc(ht_hi_ok.sem, 1)

            def q_s(b, f, t):
                if t == 1:
                    act.wait_ge(*s_done.at(b, f + 1))
                    act.activation(tmp1[:, fs(f)], acc_q[:, f, :], ACT.Square, bias=c_("bse")).then_inc(ss_ok.sem, 1)
                    act.activation(t1[:, fs(f)], acc_q[:, f, :], ACT.Identity, bias=c_("bse")).then_inc(s_ok.sem, 1)
                    act.wait_ge(*ss_ok.at(b, f + 1))
                    act.activation(ss_hi[:, fs(f)], tmp1[:, fs(f)], ACT.Copy).then_inc(ss_hi_ok.sem, 1)
                if t == 5:
                    act.wait_ge(*r32_ok.at(b, f + 1))
                    act.activation(ker_r[:, fs(f)], tmp1[:, fs(f)], ACT.Copy).then_inc(r_hi_ok.sem, 1)
                    act.wait_ge(*l32_ok.at(b, f + 1))
                    act.activation(ker_l[:, fs(f)], tmp2[:, fs(f)], ACT.Copy).then_inc(l_hi_ok.sem, 1)

            def q_msg(b, t):
                if t == 2:
                    act.wait_ge(*msg_b.at(b, 1))
                    act.activation(g_hi[:, :], msg32[:, :], ACT.Relu).then_inc(msg_hi_ok.sem, 1)

            def q_ker(b, s):
                if s < 2 * NB:
                    act.wait_ge(*dist_done.at(b, s + 1))
                    if s >= SLOTS:
                        act.wait_ge(*ker_done.at(b, s - SLOTS + 1))
                    act.activation(a_f[:, s % SLOTS, :], tr_q[:, 0, :], ACT.Exp).then_inc(a_f_ok.sem, 1)
                u = s - 1
                if 0 <= u < 2 * NB:
                    act.wait_ge(*a_m_ok.at(b, u + 1))
                    if u == 0:
                        act.wait_ge(*msg_lo_ok.at(b, 1))
                    act.activation(a_hi[:, u % SLOTS, :], a_f[:, u % SLOTS, :], ACT.Copy).then_inc(a_hi_ok.sem, 1)

            def q_nmp(b, t):
                if t == 0:
                    act.wait_ge(*ker_done.at(b, 2 * NB))
                    act.activation(nmp_hi[:, :], flat(acc_q), ACT.Copy).then_inc(nmp_hi_ok.sem, 1)

            def q_conv1(b, f, t):
                if t == 1:
                    act.wait_ge(*c1_done.at(b, f + 1))
                    act.activation(c1_32[:, fs(f)], tr_q[:, 1, :], ACT.Relu, bias=x_(X_B1), scale=x_(X_SC1)).then_inc(c1_f_ok.sem, 1)
                    act.wait_ge(*c1_f_ok.at(b, f + 1))
                    at = PAD + f * HALF
                    act.activation(c1_hi[:, at:at + HALF], c1_32[:, fs(f)], ACT.Copy).then_inc(c1_hi_ok.sem, 1)

            def q_xc(b, f, t):
                if t == 1:
                    act.wait_ge(*xc_sum.at(b, f + 1))
                    act.activation(t1[:, fs(f)], t1[:, fs(f)], ACT.Relu, bias=x_(X_B2)).then_inc(xc_ok.sem, 1)
                if t == 2:
                    act.wait_ge(*xc_ok.at(b, f + 1))
                    act.wait_ge(*ker_done.at(b, 2 * NB))
                    act.activation(g_hi[:, fs(f)], t1[:, fs(f)], ACT.Copy).then_inc(xc_hi_ok.sem, 1)

            def q_gru(b, f, t):
                if t == 1:
                    act.wait_ge(*gate_done.at(b, f + 1))
                    act.activation(gate[f][:, 0, :], tr_q[:, 0, :], ACT.Tanh, bias=x_(X_BR), scale=0.5)
                    act.activation(gate[f][:, 2, :], acc_q[:, 1, :], ACT.Identity, bias=x_(X_BHN), scale=0.5)
                    act.activation(gate[f][:, 1, :], tr_q[:, 1, :], ACT.Tanh, bias=x_(X_BZ), scale=0.5).then_inc(gate_th.sem, 1)
                if t == 3:
                    act.wait_ge(*gate_n_in.at(b, f + 1))
                    act.activation(gate[f][:, 2, :], gate[f][:, 2, :], ACT.Tanh, bias=c_("bih", 2)).then_inc(gate_n.sem, 1)

            def q_rep(b, t):
                if t == 1:
                    act.wait_ge(*rep_s_done.at(b, 1))
                    act.activation(urep[:, :], flat(tr_q), ACT.Copy).then_inc(rep_s_ok.sem, 1)
                    act.activation(s1rep[:, :], flat(acc_q), ACT.Copy).then_inc(rep_s_ok.sem, 1)

            def q_att(b, i, t):
                if t == 1:
                    act.wait_ge(*s2_prod_ok.at(b, i + 1))
                    if i == 0:
                        act.wait_ge(*rdeg_ok.at(b, 1))
                    act.activation(prod[:, :], prod[:, :], ACT.Identity, scale=rdeg[:, i:i + 1],
                                   accum_out=s2[:, i:i + 1]).then_inc(s2_ok.sem, 1)
                if t == 3:
                    act.wait_ge(*leaky_ok.at(b, i + 1))
                    act.activation(pre[:, i % 2, :], pre[:, i % 2, :], ACT.Exp).then_inc(alpha_ok.sem, 1)
                if t == 4:
                    act.wait_ge(*nmax_ok.at(b, i + 1))
                    act.activation(prow[i % 4][:, :], pre[:, i % 2, :], ACT.Exp, bias=nmax[:, i:i + 1],
                                   accum_out=psum3[:, i:i + 1]).then_inc(prow_ok.sem, 1)

            def q_edge(b, q, v):
                if v < 4:
                    n = 4 * q + v
                    act.wait_ge(*p_turned.at(b, n + 1))
                    if n >= 2:
                        act.wait_ge(*edge_done.at(b, n - 1))
                    act.activation(pt_hi[:, n % 2, :], tr_q[:, n % 2, :], ACT.Copy).then_inc(pt_hi_ok.sem, 1)
                if v == 4:
                    act.wait_ge(*edge_done.at(b, 4 * (q + 1)))
                    if q == 3:
                        act.wait_ge(*ot_turned.at(b, 1))
                    act.activation(ot[:, :], acc_q[:, q // 2, :], ACT.Copy).then_inc(ot_ok.sem, 1)

            walk(act, dict(p_ln=ln, p_adj=p_adj, p_h0t=p_h0t, p_agg=p_agg, p_z=p_z, p_silu=p_silu,
                           p_hop=p_hop, p_out=p_out, q_ln=ln, q_ht=q_ht, q_s=q_s,
                           q_msg=q_msg, q_ker=q_ker, q_nmp=q_nmp, q_conv1=q_conv1, q_xc=q_xc, q_gru=q_gru,
                           q_rep=q_rep, q_att=q_att, q_edge=q_edge))

        @block.vector
        def _(dve):
            steps_done = [0]

            def then(ins):
                steps_done[0] += 1
                ins.then_inc(set_ch.sem, 1)
                dve.wait_ge(set_ch.sem, steps_done[0])

            dve.wait_ge(setup_in.sem, 64)
            bn = {1: COLS["bn1"][0], 2: COLS["bn2"][0]}
            dve.tensor_scalar(colx[:, X_V:X_V + 1], col[:, bn[1] + 3:bn[1] + 4], BN_EPS, None, ALU.add)
            dve.tensor_scalar(colx[:, X_V + 1:X_V + 2], col[:, bn[2] + 3:bn[2] + 4], BN_EPS, None, ALU.add).then_inc(bn_v.sem, 1)
            dve.wait_ge(bn_r.sem, 1)
            for n, (sc, sh) in {1: (X_SC1, X_B1), 2: (X_SC2, X_B2)}.items():
                g = bn[n]
                then(dve.tensor_tensor(x_(sc), col[:, g:g + 1], colx[:, X_V + 1 + n:X_V + 2 + n], ALU.mult))
                then(dve.tensor_tensor(x_(sh), col[:, g + 2:g + 3], x_(sc), ALU.mult))
                then(dve.tensor_tensor(x_(sh), col[:, g + 1:g + 2], x_(sh), ALU.subtract))
            for g, at in ((0, X_BR), (1, X_BZ)):
                then(dve.tensor_tensor(x_(at), c_("bih", g), c_("bhh", g), ALU.add))
                then(dve.tensor_scalar(x_(at), x_(at), 0.5, None, ALU.mult))
            then(dve.tensor_scalar(x_(X_BHN), c_("bhh", 2), 0.5, None, ALU.mult))
            then(dve.tensor_scalar(colx[:, X_RMS:X_RMS + HC], col[:, COLS["rms"][0]:COLS["rms"][0] + HC], 0.5, None, ALU.mult))
            then(dve.memset(c1_hi[:, 0:PAD].bitcast(F32), 0.0))
            then(dve.memset(c1_hi[:, PAD + N:WIDE].bitcast(F32), 0.0))
            then(dve.memset(c1_lo[:, 0:PAD].bitcast(F32), 0.0))
            then(dve.memset(c1_lo[:, PAD + N:WIDE].bitcast(F32), 0.0))
            dve.memset(carrier[:, 0:1], 0.0).then_inc(half_free.sem, 16)
            for n in range(2):
                then(dve.tensor_tensor_reduce(out=stage_v[:, 0, :], in0=stage_l3[:, n, :], in1=stage_l3[:, 2 + n, :],
                                              scale=1.0, scalar=0.0, op0=ALU.mult, op1=ALU.add,
                                              accum_out=colx[:, X_V + n:X_V + n + 1]))
                then(dve.tensor_scalar(stage_v[:, 1, :], ones, x_(X_V + n), None, ALU.mult))
                then(dve.tensor_copy(w_hi[:, NW_IN + n, :], stage_v[:, 1, :]))
                then(dve.tensor_tensor(w_lo[:, NW_IN + n, :], stage_v[:, 1, :], w_hi[:, NW_IN + n, :], ALU.subtract))
            dve.wait_ge(w_hi_ok.sem, 1)
            dve.tensor_tensor(w_lo[:, 0:NW_IN, :], stage_w[:, :, :], w_hi[:, 0:NW_IN, :], ALU.subtract).then_inc(w_ok.sem, 1)

            def ln(b, i, t):
                g, s = i // 2, LN[i]
                src, dst = (xp, hrow) if i < 2 else (xq, hq)
                if t == 0:
                    dve.wait_ge(*{0: x_in.at(b, 16), 1: x1_ok.at(b, 1), 2: x2_ok.at(b, 1), 3: x3_ok.at(b, 1)}[i])
                    for j in range(NB):
                        last = dve.bn_stats(stat[g][:, j, :], src[:, j, :])
                    last.then_inc(s["stats"].sem, 1)
                    dve.wait_ge(*s["stats"].at(b, 1))
                    dve.memset(carrier[:, 0:1], 0.0)
                    for j in range(NB):
                        last = dve.bn_aggr(mv[g][:, j, :], stat[g][:, j, :])
                    last.then_inc(s["mean"].sem, 1)
                    dve.wait_ge(*s["mean"].at(b, 1))
                    dve.tensor_scalar(ve[g][:, :], mv[g][:, :, 1], LN_EPS, None, ALU.add).then_inc(s["var"].sem, 1)
                if t == 1:
                    dve.wait_ge(*s["rstd"].at(b, 1))
                    for j in range(NB):
                        last = dve.tensor_scalar(dst[:, ks(j)], src[:, j, :], mv[g][:, j, 0:1], rstd[g][:, j:j + 1],
                                                 ALU.subtract, ALU.mult)
                    last.then_inc(s["scaled"].sem, 1)
                if t == 2 and i == 0:
                    dve.wait_ge(*y_hi_ok.at(b, Y_H0))
                    dve.tensor_tensor(y_lo[:, :], hrow[:, :], y_hi[:, :], ALU.subtract).then_inc(y_lo_ok.sem, 1)
                if t == 2 and i == 1:
                    dve.wait_ge(*y_hi_ok.at(b, Y_W3H))
                    dve.scalar_tensor_tensor(y_lo[:, :], hrow[:, :], c_("hop", HOPS), y_hi[:, :],
                                             ALU.mult, ALU.subtract).then_inc(y_lo_ok.sem, 1)

            def p_adj(b, k):
                dve.wait_ge(*adj_hi_ok.at(b, k + 1))
                dve.tensor_tensor(adj_lo[:, k, :], adj_in[:, k % 2, :], adj_hi[:, k, :], ALU.subtract).then_inc(adj_lo_ok.sem, 1)

            def p_deg(b):
                dve.wait_ge(*deg_summed.at(b, 1))
                dve.tensor_scalar(dg[:, 0, :], tr_p[:, 0, 0:NB], 1.0, None, ALU.mult).then_inc(deg_ch.sem, 1)
                dve.wait_ge(*deg_ch.at(b, 1))
                dve.tensor_scalar(dg[:, 1, :], dg[:, 0, :], DEG_EPS, None, ALU.add)
                dve.tensor_scalar(dg[:, 3, :], dg[:, 0, :], 0.0, None, ALU.is_gt).then_inc(deg_ch.sem, 1)
                dve.wait_ge(*deg_ch.at(b, 2))
                dve.reciprocal(dg[:, 2, :], dg[:, 1, :])
                dve.tensor_tensor(dg[:, 4, :], dg[:, 0, :], dg[:, 3, :], ALU.mult).then_inc(deg_ch.sem, 1)
                dve.wait_ge(*deg_ch.at(b, 3))
                dve.tensor_scalar(dg[:, 3, :], dg[:, 3, :], -1.0, 1.0, ALU.mult, ALU.add).then_inc(deg_ch.sem, 1)
                dve.wait_ge(*deg_ch.at(b, 4))
                dve.tensor_tensor(dg[:, 4, :], dg[:, 4, :], dg[:, 3, :], ALU.add).then_inc(deg_ch.sem, 1)
                dve.wait_ge(*deg_ch.at(b, 5))
                dve.reciprocal(dg[:, 5, :], dg[:, 4, :]).then_inc(deg_ch.sem, 1)

            def p_agg(b, t):
                if t == 0:
                    dve.wait_ge(*eh_ok.at(b, 1))
                    for f in range(2):
                        dve.wait_ge(*prod_done.at(b, f + 1))
                        dve.tensor_tensor(ta[:, fs(f)], acc_p[:, f, :], ta[:, fs(f)], ALU.add).then_inc(agg_ok.sem, 1)
                if t == 2:
                    dve.wait_ge(*y_hi_ok.at(b, Y_AGG))
                    dve.tensor_tensor(y_lo[:, :], ta[:, :], y_hi[:, :], ALU.subtract).then_inc(y_lo_ok.sem, 1)

            def p_rms(b, f, t):
                if t == 0:
                    dve.wait_ge(*ms_done.at(b, f + 1))
                    dve.tensor_scalar(ve4[:, :], tr_p[:, 0, 0:HB], 1.0 / H, RMS_EPS, ALU.mult, ALU.add).then_inc(ms_read.sem, 1)
                if t == 1:
                    dve.wait_ge(*r4_ok.at(b, f + 1))
                    shape = [P, HB, P]
                    dve.tensor_tensor(sqsum[:, :].rearrange("p (j c) -> p j c", c=P), const[:, C_ID:C_ID + 1, :].to_broadcast(shape),
                                      r4[:, :].unsqueeze(2).to_broadcast(shape), ALU.mult).then_inc(diag_ok.sem, 1)
                if t == 2:
                    dve.wait_ge(*rep_done.at(b, f + 1))
                    dve.wait_ge(*zb_ok.at(b, HC * (f + 1)))
                    for c in range(HC):
                        dve.scalar_tensor_tensor(zb[:, c, :], zb[:, c, :], x_(X_RMS + c), acc_p[:, 0, :],
                                                 ALU.mult, ALU.mult).then_inc(u_ok.sem, 1)

            def p_silu(b, f, t):
                if t in (1, 5):
                    for c in ((t - 1) // 2, (t - 1) // 2 + 1):
                        dve.wait_ge(*th_ok.at(b, HC * f + c + 1))
                        dve.scalar_tensor_tensor(th[:, c % 2, :], th[:, c % 2, :], 1.0, zb[:, c, :],
                                                 ALU.add, ALU.mult).then_inc(silu_ok.sem, 1)

            def p_x1(b, t):
                if t == 1:
                    dve.wait_ge(*y0_turned.at(b, 1))
                    dve.tensor_tensor(xp[:, :, :], xp[:, :, :], blocks(tr_p), ALU.add).then_inc(x1_ok.sem, 1)

            def p_hop(b, h, t):
                if t == 2:
                    for f in range(2):
                        n = 2 * (h - 1) + f + 1
                        dve.wait_ge(*hop_turned.at(b, n))
                        shape = [P, HB, P]
                        dve.tensor_tensor(tg[:, fs(f)].rearrange("p (j c) -> p j c", c=P),
                                          tr_p[:, f, :].rearrange("p (j c) -> p j c", c=P),
                                          dg[:, 2, f * HB:(f + 1) * HB].unsqueeze(2).to_broadcast(shape), ALU.mult).then_inc(hop_scaled.sem, 1)
                    for f in range(2):
                        n = 2 * (h - 1) + f + 1
                        dve.wait_ge(*hop_scaled.at(b, n))
                        dve.scalar_tensor_tensor(tg[:, fs(f)], hrow[:, fs(f)], c_("hop", HOPS - h), tg[:, fs(f)],
                                                 ALU.mult, ALU.add).then_inc(hop_ok.sem, 1)
                if t == 4 and h < HOPS:
                    dve.wait_ge(*y_hi_ok.at(b, Y_W3H + h))
                    dve.tensor_tensor(y_lo[:, :], tg[:, :], y_hi[:, :], ALU.subtract).then_inc(y_lo_ok.sem, 1)
                if t == 5 and h == HOPS:
                    dve.wait_ge(*y_hi_ok.at(b, Y_T))
                    dve.tensor_tensor(y_lo[:, :], flat(tr_p), y_hi[:, :], ALU.subtract).then_inc(y_lo_ok.sem, 1)

            def p_out(b, t):
                if t == 2:
                    dve.wait_ge(*l1_biased.at(b, 1))
                    dve.scalar_tensor_tensor(tg[:, :], tg[:, :], 0.2, tg[:, :], ALU.mult, ALU.max).then_inc(l1_leaky.sem, 1)
                if t == 3:
                    dve.wait_ge(*deg_ch.at(b, 6))
                    dve.wait_ge(*out_ok.at(b, 0))
                    dve.wait_ge(*out_sent.at(b, 0))
                    dve.tensor_copy(rdeg[:, :], dg[:, 5, :]).then_inc(rdeg_ok.sem, 1)
                    dve.wait_ge(*l1_leaky.at(b, 1))
                    dve.tensor_tensor(xq[:, :, :], xp[:, :, :], blocks(tg), ALU.add).then_inc(x2_ok.sem, 1)

            def q_ht(b, n, t):
                if t == 2:
                    dve.wait_ge(*ht_hi_ok.at(b, n + 1))
                    dve.tensor_tensor(ht_lo[:, :], flat(tr_q), ht_hi[:, :], ALU.subtract).then_inc(ht_lo_ok.sem, 1)

            def q_s(b, f, t):
                if t == 2:
                    dve.wait_ge(*ss_hi_ok.at(b, f + 1))
                    dve.tensor_tensor(ss_lo[:, fs(f)], tmp1[:, fs(f)], ss_hi[:, fs(f)], ALU.subtract).then_inc(ss_lo_ok.sem, 1)
                if t == 4:
                    dve.wait_ge(*rl_done.at(b, f + 1))
                    dve.wait_ge(*ss_lo_ok.at(b, f + 1))
                    dve.tensor_tensor(tmp1[:, fs(f)], t1[:, fs(f)], tr_q[:, 0, :], ALU.add).then_inc(r32_ok.sem, 1)
                    dve.scalar_tensor_tensor(tmp2[:, fs(f)], t1[:, fs(f)], 2.0, acc_q[:, f, :], ALU.mult, ALU.add).then_inc(l32_ok.sem, 1)
                if t == 6:
                    dve.wait_ge(*r_hi_ok.at(b, f + 1))
                    for a in (32, 96):
                        dve.tensor_tensor(ker_r[a:a + 32, fs(f)], tmp1[a:a + 32, fs(f)], ker_r[a:a + 32, fs(f)], ALU.subtract)
                    dve.wait_ge(*l_hi_ok.at(b, f + 1))
                    dve.tensor_tensor(ker_l[64:128, fs(f)], tmp2[64:128, fs(f)], ker_l[64:128, fs(f)], ALU.subtract).then_inc(rl_ok.sem, 1)

            def q_msg(b, t):
                if t == 1:
                    dve.wait_ge(*msg_done.at(b, 1))
                    dve.tensor_tensor(blocks(msg32), blocks(acc_q), const[:, C_MSG:C_MSG + 1, :].to_broadcast([P, NB, P]),
                                      ALU.add).then_inc(msg_b.sem, 1)
                if t == 3:
                    dve.wait_ge(*msg_hi_ok.at(b, 1))
                    dve.wait_ge(*c1_lo_ok.at(b, 2))
                    dve.scalar_tensor_tensor(g_lo[:, :], msg32[:, :], 0.0, g_hi[:, :], ALU.max, ALU.subtract).then_inc(msg_lo_ok.sem, 1)

            def q_ker(b, s):
                if s < 2 * NB:
                    m = s // 2
                    if s % 2 == 0:
                        dve.wait_ge(*row_got[m % 2].at(b, 16 * (m // 2 + 1)))
                    dve.wait_ge(*a_f_ok.at(b, s + 1))
                    dve.tensor_tensor(a_f[:, s % SLOTS, :], a_f[:, s % SLOTS, :], row_in[:, m % 2, fs(s % 2)], ALU.mult).then_inc(a_m_ok.sem, 1)

            def q_nmp(b, t):
                if t == 1:
                    dve.wait_ge(*nmp_hi_ok.at(b, 1))
                    dve.tensor_tensor(nmp_lo[:, :], flat(acc_q), nmp_hi[:, :], ALU.subtract).then_inc(nmp_lo_ok.sem, 1)

            def q_xc(b, f, t):
                if t == 0:
                    if f == 0:
                        dve.wait_ge(*l32_ok.at(b, 2))
                    dve.wait_ge(*c2_done.at(b, f + 1))
                    dve.scalar_tensor_tensor(t1[:, fs(f)], tr_q[:, 1, :], x_(X_SC2), ht_hi[:, fs(f)],
                                             ALU.mult, ALU.add).then_inc(xc_part.sem, 1)
                    dve.wait_ge(*xc_part.at(b, f + 1))
                    dve.tensor_tensor(t1[:, fs(f)], t1[:, fs(f)], ht_lo[:, fs(f)], ALU.add).then_inc(xc_sum.sem, 1)
                if t == 3:
                    dve.wait_ge(*xc_hi_ok.at(b, f + 1))
                    dve.tensor_tensor(g_lo[:, fs(f)], t1[:, fs(f)], g_hi[:, fs(f)], ALU.subtract).then_inc(xc_lo_ok.sem, 1)

            def q_gru(b, f, t):
                if t == 2:
                    dve.wait_ge(*gate_th.at(b, f + 1))
                    dve.scalar_tensor_tensor(gate[f][:, 2, :], gate[f][:, 0, :], 1.0, gate[f][:, 2, :], ALU.add, ALU.mult).then_inc(gate_r.sem, 1)
                    dve.wait_ge(*gate_r.at(b, f + 1))
                    dve.tensor_tensor(gate[f][:, 2, :], acc_q[:, 0, :], gate[f][:, 2, :], ALU.add).then_inc(gate_n_in.sem, 1)
                if t == 4:
                    dve.wait_ge(*gate_d.at(b, f + 1))
                    dve.scalar_tensor_tensor(gate[f][:, 1, :], gate[f][:, 1, :], 1.0, gate[f][:, 0, :], ALU.add, ALU.mult).then_inc(gate_zd.sem, 1)
                    dve.wait_ge(*gate_zd.at(b, f + 1))
                    dve.scalar_tensor_tensor(t1[:, fs(f)], gate[f][:, 1, :], 0.5, gate[f][:, 2, :], ALU.mult, ALU.add).then_inc(gru_ok.sem, 1)

            def q_x3(b, t):
                if t == 1:
                    dve.wait_ge(*gru_turned.at(b, 1))
                    dve.tensor_tensor(xq[:, :, :], xq[:, :, :], blocks(tr_q), ALU.add).then_inc(x3_ok.sem, 1)

            def q_att(b, i, t):
                s = i % 2
                if t == 2:
                    if i >= 4:
                        dve.wait_ge(*p_turned.at(b, 4 * (i // 2 - 1)))
                    elif i == 0:
                        dve.wait_ge(*gru_ok.at(b, 2))
                    dve.wait_ge(*row_got[s].at(b, 16 * (NB // 2 + i // 2 + 1)))
                    dve.tensor_scalar(prow[i % 4][:, :], row_in[:, s, :], 0.0, NEG_INF, ALU.is_le, ALU.mult)
                if t == 3:
                    dve.wait_ge(*s2_ok.at(b, i + 1))
                    if i == 0:
                        dve.wait_ge(*h3_lo_ok.at(b, 1))
                        dve.wait_ge(*rep_s_ok.at(b, 2))
                    if i >= 2:
                        dve.wait_ge(*prow_ok.at(b, i - 1))
                    dve.scalar_tensor_tensor(pre[:, s, :], s1rep[:, :], s2[:, i:i + 1], row_in[:, s, :],
                                             ALU.add, ALU.mult).then_inc(mask_ok.sem, 1)
                    dve.wait_ge(*mask_ok.at(b, i + 1))
                    dve.scalar_tensor_tensor(pre[:, s, :], pre[:, s, :], 0.2, pre[:, s, :], ALU.mult, ALU.max).then_inc(leaky_ok.sem, 1)
                if t == 4:
                    dve.wait_ge(*alpha_ok.at(b, i + 1))
                    dve.memset(carrier[:, 1:2], 0.0)
                    dve.tensor_tensor_reduce(out=pre[:, s, :], in0=pre[:, s, :], in1=prow[i % 4][:, :], scale=1.0,
                                             scalar=-3e38, op0=ALU.add, op1=ALU.max, accum_out=amax[:, i:i + 1]).then_inc(att_ok.sem, 1)
                    dve.wait_ge(*att_ok.at(b, i + 1))
                    dve.tensor_scalar(nmax[:, i:i + 1], amax[:, i:i + 1], -1.0, None, ALU.mult).then_inc(nmax_ok.sem, 1)

            def q_edge(b, q, v):
                f = q // 2
                if v < 4:
                    n = 4 * q + v
                    dve.wait_ge(*pt_hi_ok.at(b, n + 1))
                    dve.tensor_tensor(pt_lo[:, n % 2, :], tr_q[:, n % 2, :], pt_hi[:, n % 2, :], ALU.subtract).then_inc(pt_lo_ok.sem, 1)
                if v == 4:
                    dve.wait_ge(*prow_ok.at(b, HB * (f + 1)))
                    dve.reciprocal(rinv[:, f * HB:(f + 1) * HB], psum3[:, f * HB:(f + 1) * HB]).then_inc(rinv_ok.sem, 1)
                if v == 5:
                    dve.wait_ge(*rinv_ok.at(b, f + 1))
                    dve.wait_ge(*ot_turned.at(b, f + 1))
                    for j in range(HB):
                        n = f * HB + j
                        dst = (xq[:, n, :], last_half[:, j, :])[f]
                        last = dve.scalar_tensor_tensor(dst, tr_q[:, 0, ks(j)], rinv[:, n:n + 1], xq[:, n, :], ALU.mult, ALU.add)
                    last.then_inc(out_ok.sem, 1)

            walk(dve, dict(p_ln=ln, p_adj=p_adj, p_deg=p_deg, p_agg=p_agg, p_rms=p_rms, p_silu=p_silu, p_x1=p_x1,
                           p_hop=p_hop, p_out=p_out, q_ln=ln, q_ht=q_ht, q_s=q_s, q_msg=q_msg,
                           q_ker=q_ker, q_nmp=q_nmp, q_xc=q_xc, q_gru=q_gru, q_x3=q_x3,
                           q_att=q_att, q_edge=q_edge))

        @block.tensor
        def _(pe):
            pe.wait_ge(setup_in.sem, 64)
            pe.wait_ge(w_ok.sem, 1)
            pe.wait_ge(set_act.sem, 1)

            def three(dst, l_hi, l_lo, r_hi, r_lo, first, last):
                pe.matmul(dst, l_lo, r_hi, start=first, stop=False)
                pe.matmul(dst, l_hi, r_lo, start=False, stop=False)
                return pe.matmul(dst, l_hi, r_hi, start=False, stop=last)

            def weight(dst, n, r_hi, r_lo, first=True, last=True):
                return three(dst, w_hi[:, n, :], w_lo[:, n, :], r_hi, r_lo, first, last)

            def turn(dst, src, n=NB):
                for j in range(n):
                    last = pe.transpose(dst[:, j // HB, ks(j % HB)], src[:, ks(j)], ident)
                return last

            def p_h0t(b, t):
                if t == 0:
                    pe.wait_ge(*LN[0]["h"].at(b, 1))
                    pe.wait_ge(*y_lo_ok.at(b, 0))
                    turn(tr_p, hrow).then_inc(h0_turned.sem, 1)

            def p_prod0(b, k):
                if k == 0:
                    pe.wait_ge(*y_lo_ok.at(b, Y_H0))
                    pe.wait_ge(*l1_biased.at(b, 0))
                pe.wait_ge(*adj_lo_ok.at(b, k + 1))
                for f in range(2):
                    last = three(acc_p[:, f, :], y_hi[:, ks(k)], y_lo[:, ks(k)], adj_hi[:, k, fs(f)], adj_lo[:, k, fs(f)],
                                 k == 0, k == NB - 1)
                    if k == NB - 1:
                        last.then_inc(prod_done.sem, 1)

            def p_deg(b):
                pe.wait_ge(*deg_added.at(b, NB))
                pe.wait_ge(*eh_ok.at(b, 1))
                for j in range(NB):
                    last = pe.matmul(tr_p[:, 0, j:j + 1], dacc[:, ks(j)], const[:, C_ONE, 0:1], start=True, stop=True)
                last.then_inc(deg_summed.sem, 1)

            def p_prod(b, h, f, k0):
                if k0 == 0:
                    if f == 0:
                        pe.wait_ge(*y_lo_ok.at(b, Y_W3H + h - 1))
                    if h == 1:
                        pe.wait_ge(*(u_ok.at(b, 2 * HC) if f == 0 else y0_ok.at(b, 2)))
                    if h > 1:
                        pe.wait_ge(*hop_copied.at(b, 2 * (h - 2) + f + 1))
                for k in (k0, k0 + 1):
                    last = three(acc_p[:, f, :], y_hi[:, ks(k)], y_lo[:, ks(k)], adj_hi[:, k, fs(f)], adj_lo[:, k, fs(f)],
                                 k == 0, k == NB - 1)
                if k0 + 2 == NB:
                    last.then_inc(prod_done.sem, 1)

            def p_z(b, f, c):
                if c == 0 and f == 0:
                    pe.wait_ge(*y_lo_ok.at(b, Y_AGG))
                    pe.wait_ge(*deg_ch.at(b, 1))
                if c == 0 and f == 1:
                    pe.wait_ge(*ms_read.at(b, 1))
                if HC * f + c >= 2:
                    pe.wait_ge(*sq_ok.at(b, HC * f + c - 1))
                weight(tr_p[:, c % 2, :], W_MLP1 + c, y_hi[:, fs(f)], y_lo[:, fs(f)]).then_inc(z_done.sem, 1)

            def p_rms(b, f, t):
                if t == 0:
                    pe.wait_ge(*sq_added.at(b, (HC - 1) * (f + 1)))
                    for j in range(HB):
                        last = pe.matmul(tr_p[:, 0, j:j + 1], sqsum[:, ks(j)], const[:, C_ONE, 0:1], start=True, stop=True)
                    last.then_inc(ms_done.sem, 1)
                if t == 1:
                    pe.wait_ge(*diag_ok.at(b, f + 1))
                    pe.wait_ge(*(agg_ok.at(b, 2) if f == 0 else u_ok.at(b, HC)))
                    pe.matmul(acc_p[:, 0, :], ones, sqsum[:, :], start=True, stop=True).then_inc(rep_done.sem, 1)

            def p_silu(b, f, t):
                if t in (3, 7):
                    for c in ((t - 3) // 2, (t - 3) // 2 + 1):
                        if f == 1 and c == 0:
                            pe.wait_ge(*y0_ok.at(b, 1))
                        pe.wait_ge(*s_lo_ok.at(b, HC * f + c + 1))
                        weight(acc_p[:, 1, :], W_MLP2 + c, s_hi[:, c % 2, :], s_lo[:, c % 2, :], c == 0, c == HC - 1).then_inc(w2_done.sem, 1)

            def p_x1(b, t):
                if t == 0:
                    pe.wait_ge(*y0_ok.at(b, 2))
                    pe.wait_ge(*ms_read.at(b, 2))
                    turn(tr_p, ta).then_inc(y0_turned.sem, 1)

            def p_hop(b, h, t):
                if t in (1, 2):
                    f = t - 1
                    pe.wait_ge(*hop_copied.at(b, 2 * (h - 1) + f + 1))
                    if h == 1:
                        pe.wait_ge(*x1_ok.at(b, 1))
                    for j in range(HB):
                        last = pe.transpose(tr_p[:, f, ks(j)], ta[:, ks(f * HB + j)], ident)
                    last.then_inc(hop_turned.sem, 1)
                if t == 3 and h == HOPS:
                    pe.wait_ge(*hop_ok.at(b, 2 * HOPS))
                    turn(tr_p, tg).then_inc(yt_turned.sem, 1)

            def p_out(b, t):
                if t == 0:
                    pe.wait_ge(*y_lo_ok.at(b, Y_T))
                    pe.wait_ge(*hop_copied.at(b, 2 * HOPS))
                    for j in range(NB):
                        last = three(acc_p[:, j // HB, ks(j % HB)], y_hi[:, ks(j)], y_lo[:, ks(j)],
                                     w_hi[:, W_HOP, :], w_lo[:, W_HOP, :], True, True)
                    last.then_inc(l1_done.sem, 1)

            def q_ht(b, n, t):
                if t == 0:
                    pe.wait_ge(*LN[2 + n]["h"].at(b, 1))
                    if n == 1:
                        pe.wait_ge(*x3_ok.at(b, 1))
                    turn(tr_q, hq).then_inc(ht_turned.sem, 1)

            def q_s(b, f, t):
                if t == 0:
                    pe.wait_ge(*ht_lo_ok.at(b, 1))
                    weight(acc_q[:, f, :], W_SE, ht_hi[:, fs(f)], ht_lo[:, fs(f)]).then_inc(s_done.sem, 1)
                if t == 3:
                    pe.wait_ge(*ss_lo_ok.at(b, f + 1))
                    pe.wait_ge(*s_ok.at(b, f + 1))
                    if f == 1:
                        pe.wait_ge(*r32_ok.at(b, 1))
                    for n, dst in ((1, tr_q[:, 0, :]), (0, acc_q[:, f, :])):
                        pe.matmul(dst, pat[:, n, :], ss_lo[:, fs(f)], start=True, stop=False)
                        last = pe.matmul(dst, pat[:, n, :], ss_hi[:, fs(f)], start=False, stop=True)
                    last.then_inc(rl_done.sem, 1)

            def q_msg(b, t):
                if t == 0:
                    pe.wait_ge(*l32_ok.at(b, 2))
                    for j in range(NB):
                        last = three(acc_q[:, j // HB, ks(j % HB)], ht_hi[:, ks(j)], ht_lo[:, ks(j)],
                                     w_hi[:, W_MSG, :], w_lo[:, W_MSG, :], True, True)
                    last.then_inc(msg_done.sem, 1)

            def q_ker(b, s):
                if s < 2 * NB:
                    if s == 0:
                        pe.wait_ge(*rl_ok.at(b, 2))
                    if s >= 1:
                        pe.wait_ge(*a_f_ok.at(b, s))
                    pe.matmul(tr_q[:, 0, :], ker_l[:, ks(s // 2)], ker_r[:, fs(s % 2)], start=True, stop=True).then_inc(dist_done.sem, 1)
                u = s - 3
                if u >= 0:
                    m, f = u // 2, u % 2
                    if u == 0:
                        pe.wait_ge(*msg_lo_ok.at(b, 1))
                    pe.wait_ge(*a_lo_ok.at(b, u + 1))
                    three(acc_q[:, f, :], g_hi[:, ks(m)], g_lo[:, ks(m)], a_hi[:, u % SLOTS, :], a_lo[:, u % SLOTS, :],
                          m == 0, m == NB - 1).then_inc(ker_done.sem, 1)

            def q_conv1(b, f, t):
                if t == 0:
                    if f == 0:
                        pe.wait_ge(*ht_lo_ok.at(b, 1))
                    else:
                        pe.wait_ge(*c1_f_ok.at(b, 1))
                    weight(tr_q[:, 1, :], W_CONV1, ht_hi[:, fs(f)], ht_lo[:, fs(f)]).then_inc(c1_done.sem, 1)

            def q_conv2(b, f, part):
                if f == 0 and part == 0:
                    pe.wait_ge(*c1_lo_ok.at(b, 2))
                if f == 1 and part == 0:
                    pe.wait_ge(*xc_part.at(b, 1))
                for t in TAP_PARTS[part]:
                    at = f * HALF + t
                    last = weight(tr_q[:, 1, :], W_CONV2 + t, c1_hi[:, at:at + HALF], c1_lo[:, at:at + HALF], t == 0, t == TAPS - 1)
                if part == len(TAP_PARTS) - 1:
                    last.then_inc(c2_done.sem, 1)

            def q_gru(b, f, t):
                if t not in (0, 5):
                    return
                ht = ht_hi[:, fs(f)], ht_lo[:, fs(f)]
                nmp = nmp_hi[:, fs(f)], nmp_lo[:, fs(f)]
                xc = g_hi[:, fs(f)], g_lo[:, fs(f)]
                if t == 0:
                    pe.wait_ge(*(xc_part.at(b, 2) if f == 0 else gate_th.at(b, 1)))
                    if f == 0:
                        pe.wait_ge(*nmp_lo_ok.at(b, 1))
                    for g in range(2):
                        weight(tr_q[:, g, :], W_HH + g, *ht, True, False)
                        weight(tr_q[:, g, :], W_IH + 2 * g + 1, *nmp, False, False)
                if t == 5:
                    pe.wait_ge(*(xc_lo_ok.at(b, 2) if f == 0 else gate_n_in.at(b, 1)))
                    weight(acc_q[:, 1, :], W_HH + 2, *ht, True, True)
                    weight(acc_q[:, 0, :], W_IH + 5, *nmp, True, False)
                    weight(acc_q[:, 0, :], W_IH + 4, *xc, False, True)
                    for g in range(2):
                        last = weight(tr_q[:, g, :], W_IH + 2 * g, *xc, False, True)
                    last.then_inc(gate_done.sem, 1)

            def q_x3(b, t):
                if t == 0:
                    pe.wait_ge(*gru_ok.at(b, 2))
                    turn(tr_q, t1).then_inc(gru_turned.sem, 1)

            def q_rep(b, t):
                if t == 0:
                    pe.wait_ge(*ht_lo_ok.at(b, 2))
                    for dst, w in ((tr_q, W_S2), (acc_q, W_S1)):
                        for f in range(2):
                            last = weight(dst[:, f, :], w, ht_hi[:, fs(f)], ht_lo[:, fs(f)])
                    last.then_inc(rep_s_done.sem, 1)

            def q_edge(b, q, v):
                def turn_p(v):
                    n = 4 * q + v
                    if n >= 2:
                        pe.wait_ge(*pt_lo_ok.at(b, n - 1))
                    for m in range(2):
                        for r in range(2):
                            last = pe.transpose(tr_q[:, n % 2, ks(2 * m + r)], prow[(2 * q + r) % 4][:, ks(2 * v + m)], ident)
                    last.then_inc(p_turned.sem, 1)

                if v == 0:
                    pe.wait_ge(*prow_ok.at(b, 2 * (q + 1)))
                    if q == 0:
                        pe.wait_ge(*rep_s_ok.at(b, 2))
                        pe.wait_ge(*h3_lo_ok.at(b, 1))
                    if q == 2:
                        pe.wait_ge(*out_ok.at(b, 1))
                    turn_p(0)
                if v < 3:
                    turn_p(v + 1)
                if v < 4:
                    n = 4 * q + v
                    pe.wait_ge(*pt_lo_ok.at(b, n + 1))
                    cols_q = slice((q % 2) * 2 * P, (q % 2 + 1) * 2 * P)
                    for m in range(2):
                        half = slice(m * 2 * P, (m + 1) * 2 * P)
                        k = 2 * v + m
                        last = three(acc_q[:, q // 2, cols_q], g_hi[:, ks(k)], g_lo[:, ks(k)], pt_hi[:, n % 2, half], pt_lo[:, n % 2, half],
                                     k == 0, k == NB - 1)
                    last.then_inc(edge_done.sem, 1)
                if v == 4:
                    pe.wait_ge(*ot_ok.at(b, q // 2 + 1))
                    for j in range(HB):
                        last = pe.transpose(tr_q[:, 0, ks(j)], ot[:, ks(j)], ident)
                    last.then_inc(ot_turned.sem, 1)

            walk(pe, dict(p_h0t=p_h0t, p_prod0=p_prod0, p_deg=p_deg, p_prod=p_prod, p_z=p_z, p_rms=p_rms, p_silu=p_silu,
                          p_x1=p_x1, p_hop=p_hop, p_out=p_out, q_ht=q_ht, q_s=q_s, q_msg=q_msg, q_ker=q_ker,
                          q_conv1=q_conv1, q_conv2=q_conv2, q_gru=q_gru, q_x3=q_x3, q_rep=q_rep, q_edge=q_edge))


def kernel(**inputs):
    import numpy as np
    import concourse.bacc as bacc
    from concourse.bass_utils import run_bass_kernel_spmd

    a = {k: np.ascontiguousarray(v) for k, v in inputs.items()}
    f32 = np.float32

    mats = [a["L0_gnn_W1"][:, c * P:(c + 1) * P] for c in range(HC)]
    mats += [a["L0_gnn_W2"][c * P:(c + 1) * P, :] for c in range(HC)]
    mats += [a["L1_gnn_W"].T, a["L2_gnn_conv1_w"][:, :, 0].T]
    mats += [a["L2_gnn_conv2_w"][:, :, t].T for t in range(TAPS)]
    mats += [a["L2_gnn_w_msg"].T]
    se = np.zeros((D, P), f32)
    bse = np.zeros((P,), f32)
    for q in range(4):
        se[:, 32 * q:32 * q + 3] = a["L2_gnn_w_se"].T
        bse[32 * q:32 * q + 3] = a["L2_gnn_b_se"]
        bse[32 * q + 3] = 1.0
    mats += [se]
    mats += [a["L2_gnn_w_ih"][g * P:(g + 1) * P, h * P:(h + 1) * P].T for g in range(3) for h in range(2)]
    mats += [a["L2_gnn_w_hh"][g * P:(g + 1) * P, :].T for g in range(3)]
    wpack = np.stack(mats, axis=1).reshape(P, NW_IN * P)
    w3 = a["L3_gnn_w3"][:, 0]
    rep = [np.broadcast_to(w3[n * P:(n + 1) * P], (P, P)) for n in range(2)]
    l3pack = np.stack([a["L3_gnn_W1"], a["L3_gnn_W2"], *rep], axis=1).reshape(P, 4 * P)

    pat_l, pat_r = np.zeros((P, P), f32), np.zeros((P, P), f32)
    for q in range(4):
        pat_r[0:3, 32 * q + 3] = -1.0
        pat_r[3, 32 * q + 3] = -1.0
        pat_r[3, 32 * q + 4] = 1.0
        pat_l[0:3, 32 * q + 4] = -1.0
        pat_l[3, 32 * q + 3] = -1.0
    cpack = np.stack([np.eye(P, dtype=f32), np.ones((P, P), f32), pat_l, pat_r,
                      np.broadcast_to(a["L2_gnn_b_msg"], (P, P))], axis=1).reshape(P, 5 * P)
    columns = [a["L0_gnn_b1"].reshape(HC, P), a["L0_gnn_rms_weight"].reshape(HC, P), a["L0_gnn_b2"][None]]
    columns += [a[f"L2_gnn_bn{n}_{v}"][None] for n in (1, 2) for v in "gbmv"]
    columns += [a["L2_gnn_b_ih"].reshape(3, P), a["L2_gnn_b_hh"].reshape(3, P)]
    columns += [np.broadcast_to(a["L1_gnn_conv_w"][:, None], (HOPS + 1, P)),
                np.broadcast_to(a["L1_gnn_conv_b"][:, None], (1, P)),
                np.broadcast_to(a["L0_gnn_epsilon"].reshape(1, 1), (1, P)), bse[None]]
    cols = np.concatenate(columns, axis=0).T

    arrays = dict(x=a["x"], adj=a["adj"], adj_t=a["adj"].transpose(0, 2, 1), wpack=wpack, l3pack=l3pack,
                  cpack=cpack, cols=cols)
    arrays = {f"in_{k}": np.ascontiguousarray(v) for k, v in arrays.items()}
    nc = bacc.Bacc("TRN2", target_bir_lowering=False, num_devices=1, dynamic_dma_scratch_size=1024)
    args = [nc.dram_tensor(k, v.shape, F32, kind="ExternalInput").ap() for k, v in arrays.items()]
    out = nc.dram_tensor("out", (B, N, D), F32, kind="ExternalOutput").ap()
    build(nc, *args, out)
    r = run_bass_kernel_spmd(nc, [arrays], core_ids=[0])
    return r.results[0]["out"]
```
